# Optimizing a Trainium2 kernel written in Bass

```python
import numpy as np
import jax
import jax.numpy as jnp

def _softmax(x, axis=-1):
    return jax.nn.softmax(x, axis=axis)

def _gelu(x):
    return jax.nn.gelu(x, approximate=True)

def _silu(x):
    return jax.nn.silu(x)

def _sigmoid(x):
    return jax.nn.sigmoid(x)

def _layernorm(x, axis=-1, eps=1e-05):
    m = jnp.mean(x, axis=axis, keepdims=True)
    v = jnp.var(x, axis=axis, keepdims=True)
    return (x - m) / jnp.sqrt(v + eps)

def _scatter_add(tgt, idx, src, axis=0):
    return tgt.at[idx].add(src)

def _segment_sum(src, seg, n):
    return jax.ops.segment_sum(src, seg, n)
kernel_name = 'mk_decoder_postln_d1_seqx_r8_75a005'

def setup_inputs(seed: int=0):
    np.random.seed(seed)
    _w = jnp.asarray

    def _rec_inputs():
        import jax
        import jax.numpy as jnp
        _rk = jax.random.key(seed)
        x = 7.22e-05 + 1 * jax.random.normal(jax.random.fold_in(_rk, 1), (32, 64, 256), jnp.float32)
        _lenS = 64 - jax.random.randint(jax.random.fold_in(_rk, 7), (32,), 0, max(1, 64 // 4) + 1, jnp.int32)
        _lenS2 = 64 - jax.random.randint(jax.random.fold_in(_rk, 8), (32,), 0, max(1, 64 // 4) + 1, jnp.int32)
        _ctx_2048P = jax.random.normal(jax.random.fold_in(_rk, 11), (32, 16, 256), jnp.float32)
        _ctx_2048c = jax.random.dirichlet(jax.random.fold_in(_rk, 511), 0.3 * jnp.ones((16,), jnp.float32), (32, 64))
        _ctx_2048t = jnp.einsum('bsk,bkd->bsd', _ctx_2048c, _ctx_2048P)
        _ctx_2048t = _ctx_2048t * jax.lax.rsqrt(jnp.mean(jnp.square(_ctx_2048t)) + 1e-12) * 0.953939
        ctx_2048 = 4.13588e-05 + 0.999923 * (_ctx_2048t + 0.3 * jax.random.normal(jax.random.fold_in(_rk, 611), (32, 64, 256), jnp.float32))
        return (x, ctx_2048)
    x, ctx_2048 = _rec_inputs()

    def _L0_attn_setup():
        import jax, jax.numpy as jnp
        import numpy as np
        HID = 256
        NH = 16
        HD = 128
        R = 16
        WIN = 128
        ROPE = HD // 2
        EPS = 1e-06

        def rmsnorm(x, w):
            return x * jax.lax.rsqrt(jnp.mean(x * x, axis=-1, keepdims=True) + EPS) * w

        def apply_rope(x, pos):
            half = ROPE // 2
            inv_freq = 1.0 / 10000.0 ** (jnp.arange(half, dtype=jnp.float32) * 2.0 / ROPE)
            ang = pos.astype(jnp.float32)[:, None] * inv_freq[None, :]
            cos, sin = (jnp.cos(ang), jnp.sin(ang))
            x1, x2, rest = (x[..., :half], x[..., half:ROPE], x[..., ROPE:])
            return jnp.concatenate([x1 * cos - x2 * sin, x1 * sin + x2 * cos, rest], axis=-1)
        key = jax.random.key(seed)
        ks = jax.random.split(key, 16)
        s = 0.02
        return {'hidden_states': jax.random.normal(ks[0], (1, 256, HID), jnp.float32), 'Wq': jax.random.normal(ks[1], (HID, NH * HD), jnp.float32) * s, 'bq': jnp.zeros((NH * HD,), jnp.float32), 'Wc': jax.random.normal(ks[2], (HID, 1), jnp.float32) * s, 'bc': jnp.zeros((1,), jnp.float32), 'Wk': jax.random.normal(ks[3], (HID, HD), jnp.float32) * s, 'bk': jnp.zeros((HD,), jnp.float32), 'Wv': jax.random.normal(ks[4], (HID, HD), jnp.float32) * s, 'bv': jnp.zeros((HD,), jnp.float32), 'Wlk': jax.random.normal(ks[5], (HID, NH * HD), jnp.float32) * s, 'blk': jnp.zeros((NH * HD,), jnp.float32), 'Wlv': jax.random.normal(ks[6], (HID, NH * HD), jnp.float32) * s, 'blv': jnp.zeros((NH * HD,), jnp.float32), 'qn_w': jnp.ones((HD,), jnp.float32), 'kn_w': jnp.ones((HD,), jnp.float32), 'sink_k': jax.random.normal(ks[7], (NH, HD), jnp.float32) * s, 'sink_v': jax.random.normal(ks[8], (NH, HD), jnp.float32) * s, 'Wo': jax.random.normal(ks[9], (NH * HD, HID), jnp.float32) * s, 'bo': jnp.zeros((HID,), jnp.float32)}
    _L0_attn_all = _L0_attn_setup()
    _L0_attn_in = {k: v for k, v in _L0_attn_all.items() if k in ('Wq', 'bq', 'Wc', 'bc', 'Wk', 'bk', 'Wv', 'bv', 'Wlk', 'blk', 'Wlv', 'blv', 'qn_w', 'kn_w', 'sink_k', 'sink_v', 'Wo', 'bo')}
    del _L0_attn_all

    def _L0_xattn_setup():
        import jax, jax.numpy as jnp
        import numpy as np
        B, S, DIM, HD = (4, 128, 256, 128)
        H = DIM // HD
        GN_EPS = 0.001

        def _decay_masks(n_heads, seq_len):
            gam = 1.0 - 2.0 ** (-5.0 - jnp.arange(n_heads, dtype=jnp.float32))
            idx = jnp.arange(seq_len, dtype=jnp.float32)
            expo = idx[None, :] - idx[:, None]
            D = jnp.where(expo[None, :, :] <= 0, gam[:, None, None] ** expo[None, :, :], 0.0)
            return D / jnp.sqrt(D.sum(axis=-1))[:, None, :]
        key = jax.random.key(seed)
        ks = jax.random.split(key, 8)
        x = jax.random.normal(ks[0], (B, S, DIM), dtype=jnp.float32)
        k = jax.random.normal(ks[1], (B, S, DIM), dtype=jnp.float32)
        v = jax.random.normal(ks[2], (B, S, DIM), dtype=jnp.float32)
        Wh = jax.random.normal(ks[3], (H, HD, HD), dtype=jnp.float32) / np.sqrt(HD)
        wg_w = jax.random.normal(ks[4], (DIM, DIM), dtype=jnp.float32) / np.sqrt(DIM)
        wo_w = jax.random.normal(ks[5], (DIM, DIM), dtype=jnp.float32) / np.sqrt(DIM)
        gn_gamma = jnp.ones((DIM,), dtype=jnp.float32)
        gn_beta = jnp.zeros((DIM,), dtype=jnp.float32)
        return {'x': x, 'k': k, 'v': v, 'Wh': Wh, 'wg_w': wg_w, 'wo_w': wo_w, 'gn_gamma': gn_gamma, 'gn_beta': gn_beta}
    _L0_xattn_all = _L0_xattn_setup()
    _L0_xattn_in = {k: v for k, v in _L0_xattn_all.items() if k in ('Wh', 'wg_w', 'wo_w', 'gn_gamma', 'gn_beta')}
    del _L0_xattn_all

    def _L0_ffn_setup():
        import jax, jax.numpy as jnp
        import numpy as np
        D = 256
        F = 176
        E = 8
        K = 2
        FS = 352
        B, S = (2, 128)
        key = jax.random.key(seed)
        ks = jax.random.split(key, 9)
        sc = 0.02
        return {'x': jax.random.normal(ks[0], (B, S, D), dtype=jnp.float32), 'Wr': jax.random.normal(ks[1], (E, D), dtype=jnp.float32) * sc, 'Wg': jax.random.normal(ks[2], (E, F, D), dtype=jnp.float32) * sc, 'Wu': jax.random.normal(ks[3], (E, F, D), dtype=jnp.float32) * sc, 'Wd': jax.random.normal(ks[4], (E, D, F), dtype=jnp.float32) * sc, 'Wsg': jax.random.normal(ks[5], (FS, D), dtype=jnp.float32) * sc, 'Wsu': jax.random.normal(ks[6], (FS, D), dtype=jnp.float32) * sc, 'Wsd': jax.random.normal(ks[7], (D, FS), dtype=jnp.float32) * sc}
    _L0_ffn_all = _L0_ffn_setup()
    _L0_ffn_in = {k: v for k, v in _L0_ffn_all.items() if k in ('Wr', 'Wg', 'Wu', 'Wd', 'Wsg', 'Wsu', 'Wsd')}
    del _L0_ffn_all
    return {'x': x, 'ctx_2048': ctx_2048, 'L0_attn_Wq': _L0_attn_in['Wq'], 'L0_attn_bq': _L0_attn_in['bq'], 'L0_attn_Wc': _L0_attn_in['Wc'], 'L0_attn_bc': _L0_attn_in['bc'], 'L0_attn_Wk': _L0_attn_in['Wk'], 'L0_attn_bk': _L0_attn_in['bk'], 'L0_attn_Wv': _L0_attn_in['Wv'], 'L0_attn_bv': _L0_attn_in['bv'], 'L0_attn_Wlk': _L0_attn_in['Wlk'], 'L0_attn_blk': _L0_attn_in['blk'], 'L0_attn_Wlv': _L0_attn_in['Wlv'], 'L0_attn_blv': _L0_attn_in['blv'], 'L0_attn_qn_w': _L0_attn_in['qn_w'], 'L0_attn_kn_w': _L0_attn_in['kn_w'], 'L0_attn_sink_k': _L0_attn_in['sink_k'], 'L0_attn_sink_v': _L0_attn_in['sink_v'], 'L0_attn_Wo': _L0_attn_in['Wo'], 'L0_attn_bo': _L0_attn_in['bo'], 'L0_xattn_Wh': _L0_xattn_in['Wh'], 'L0_xattn_wg_w': _L0_xattn_in['wg_w'], 'L0_xattn_wo_w': _L0_xattn_in['wo_w'], 'L0_xattn_gn_gamma': _L0_xattn_in['gn_gamma'], 'L0_xattn_gn_beta': _L0_xattn_in['gn_beta'], 'L0_ffn_Wr': _L0_ffn_in['Wr'], 'L0_ffn_Wg': _L0_ffn_in['Wg'], 'L0_ffn_Wu': _L0_ffn_in['Wu'], 'L0_ffn_Wd': _L0_ffn_in['Wd'], 'L0_ffn_Wsg': _L0_ffn_in['Wsg'], 'L0_ffn_Wsu': _L0_ffn_in['Wsu'], 'L0_ffn_Wsd': _L0_ffn_in['Wsd']}

def reference(x, ctx_2048, L0_attn_Wq, L0_attn_bq, L0_attn_Wc, L0_attn_bc, L0_attn_Wk, L0_attn_bk, L0_attn_Wv, L0_attn_bv, L0_attn_Wlk, L0_attn_blk, L0_attn_Wlv, L0_attn_blv, L0_attn_qn_w, L0_attn_kn_w, L0_attn_sink_k, L0_attn_sink_v, L0_attn_Wo, L0_attn_bo, L0_xattn_Wh, L0_xattn_wg_w, L0_xattn_wo_w, L0_xattn_gn_gamma, L0_xattn_gn_beta, L0_ffn_Wr, L0_ffn_Wg, L0_ffn_Wu, L0_ffn_Wd, L0_ffn_Wsg, L0_ffn_Wsu, L0_ffn_Wsd):
    import jax
    import jax.numpy as jnp

    def _L0_attn_ref(hidden_states, Wq, bq, Wc, bc, Wk, bk, Wv, bv, Wlk, blk, Wlv, blv, qn_w, kn_w, sink_k, sink_v, Wo, bo):
        import jax, jax.numpy as jnp
        import numpy as np
        HID = 256
        NH = 16
        HD = 128
        R = 16
        WIN = 128
        ROPE = HD // 2
        EPS = 1e-06

        def rmsnorm(x, w):
            return x * jax.lax.rsqrt(jnp.mean(x * x, axis=-1, keepdims=True) + EPS) * w

        def apply_rope(x, pos):
            half = ROPE // 2
            inv_freq = 1.0 / 10000.0 ** (jnp.arange(half, dtype=jnp.float32) * 2.0 / ROPE)
            ang = pos.astype(jnp.float32)[:, None] * inv_freq[None, :]
            cos, sin = (jnp.cos(ang), jnp.sin(ang))
            x1, x2, rest = (x[..., :half], x[..., half:ROPE], x[..., ROPE:])
            return jnp.concatenate([x1 * cos - x2 * sin, x1 * sin + x2 * cos, rest], axis=-1)
        B, S, _ = hidden_states.shape
        pos = jnp.arange(S)
        scale = 1.0 / jnp.sqrt(jnp.float32(HD))
        q = (hidden_states @ Wq + bq).reshape(B, S, NH, HD).transpose(0, 2, 1, 3)
        q = apply_rope(rmsnorm(q, qn_w), pos)
        C = S // R
        w = jax.nn.softmax((hidden_states @ Wc + bc).reshape(B, C, R), axis=-1)
        entries = jnp.einsum('bcr,bcrh->bch', w, hidden_states.reshape(B, C, R, HID))
        block_ends = jnp.arange(C) * R + (R - 1)
        ck = apply_rope(rmsnorm(entries @ Wk + bk, kn_w), block_ends)
        cv = entries @ Wv + bv
        cs = jnp.einsum('bhsd,bcd->bhsc', q, ck) * scale
        cmask = block_ends[None, :] <= pos[:, None]
        cs = jnp.where(cmask, cs, -1000000000.0)
        sink_s = jnp.einsum('bhsd,hd->bhs', q, sink_k) * scale
        attn = jax.nn.softmax(jnp.concatenate([cs, sink_s[..., None]], axis=-1), axis=-1)
        ctx_c = jnp.einsum('bhsc,bcd->bhsd', attn[..., :C], cv) + attn[..., C:] * sink_v[None, :, None, :]
        lk = (hidden_states @ Wlk + blk).reshape(B, S, NH, HD).transpose(0, 2, 1, 3)
        lk = apply_rope(rmsnorm(lk, kn_w), pos)
        lv = (hidden_states @ Wlv + blv).reshape(B, S, NH, HD).transpose(0, 2, 1, 3)
        ls = jnp.einsum('bhsd,bhtd->bhst', q, lk) * scale
        d = pos[:, None] - pos[None, :]
        lmask = (d >= 0) & (d <= WIN)
        lattn = jax.nn.softmax(jnp.where(lmask, ls, -1000000000.0), axis=-1)
        ctx_l = jnp.einsum('bhst,bhtd->bhsd', lattn, lv)
        merged = 0.5 * (ctx_c + ctx_l)
        out = merged.transpose(0, 2, 1, 3).reshape(B, S, NH * HD) @ Wo + bo
        return out

    def _L0_xattn_ref(x, k, v, Wh, wg_w, wo_w, gn_gamma, gn_beta):
        import jax, jax.numpy as jnp
        import numpy as np
        B, S, DIM, HD = (4, 128, 256, 128)
        H = DIM // HD
        GN_EPS = 0.001

        def _decay_masks(n_heads, seq_len):
            gam = 1.0 - 2.0 ** (-5.0 - jnp.arange(n_heads, dtype=jnp.float32))
            idx = jnp.arange(seq_len, dtype=jnp.float32)
            expo = idx[None, :] - idx[:, None]
            D = jnp.where(expo[None, :, :] <= 0, gam[:, None, None] ** expo[None, :, :], 0.0)
            return D / jnp.sqrt(D.sum(axis=-1))[:, None, :]
        b, s, dim = x.shape
        h, hd, _ = Wh.shape
        xh = x.reshape(b, s, h, hd)
        kh = k.reshape(b, s, h, hd)
        vh = v.reshape(b, s, h, hd)
        Q = jnp.einsum('bshd,hde->bshe', xh, Wh)
        K = jnp.einsum('bshd,hde->bshe', kh, Wh)
        V = jnp.einsum('bshd,hde->bshe', vh, Wh)
        scores = jnp.einsum('bshe,bthe->bhst', Q, K) / jnp.sqrt(jnp.float32(hd))
        Dn = _decay_masks(h, s)
        masked = scores * Dn[None, :, :, :]
        A = jnp.maximum(jnp.abs(masked.sum(axis=0)), 1.0)
        O = jnp.einsum('hst,bthe->bshe', A, V).reshape(b, s, dim)
        mu = O.mean(axis=-1, keepdims=True)
        var = O.var(axis=-1, keepdims=True)
        Y = (O - mu) / jnp.sqrt(var + GN_EPS) * gn_gamma + gn_beta
        W = jax.nn.relu(x @ wg_w)
        return W * Y @ wo_w

    def _L0_ffn_ref(x, Wr, Wg, Wu, Wd, Wsg, Wsu, Wsd):
        import jax, jax.numpy as jnp
        import numpy as np
        D = 256
        F = 176
        E = 8
        K = 2
        FS = 352
        B, S = (2, 128)
        silu = jax.nn.silu
        sg = silu(jnp.einsum('bsd,fd->bsf', x, Wsg))
        su = jnp.einsum('bsd,fd->bsf', x, Wsu)
        shared_out = jnp.einsum('bsf,df->bsd', sg * su, Wsd)
        logits = jnp.einsum('bsd,ed->bse', x, Wr)
        scores = jax.nn.softmax(logits, axis=-1)
        topk_scores, topk_idx = jax.lax.top_k(scores, K)
        w_full = jnp.sum(jax.nn.one_hot(topk_idx, E, dtype=x.dtype) * topk_scores[..., None], axis=-2)
        g = silu(jnp.einsum('bsd,efd->bsef', x, Wg))
        u = jnp.einsum('bsd,efd->bsef', x, Wu)
        out_e = jnp.einsum('bsef,edf->bsed', g * u, Wd)
        routed_out = jnp.einsum('bsed,bse->bsd', out_e, w_full)
        return routed_out + shared_out
    x = _layernorm(x + _L0_attn_ref(x, L0_attn_Wq, L0_attn_bq, L0_attn_Wc, L0_attn_bc, L0_attn_Wk, L0_attn_bk, L0_attn_Wv, L0_attn_bv, L0_attn_Wlk, L0_attn_blk, L0_attn_Wlv, L0_attn_blv, L0_attn_qn_w, L0_attn_kn_w, L0_attn_sink_k, L0_attn_sink_v, L0_attn_Wo, L0_attn_bo), axis=-1)
    x = _layernorm(x + _L0_xattn_ref(x, ctx_2048, ctx_2048, L0_xattn_Wh, L0_xattn_wg_w, L0_xattn_wo_w, L0_xattn_gn_gamma, L0_xattn_gn_beta), axis=-1)
    x = _layernorm(x + _L0_ffn_ref(x, L0_ffn_Wr, L0_ffn_Wg, L0_ffn_Wu, L0_ffn_Wd, L0_ffn_Wsg, L0_ffn_Wsu, L0_ffn_Wsd), axis=-1)
    return x

_drawn_inputs = setup_inputs


def setup_inputs(seed=0):
    import zlib

    import numpy as np

    out = dict(_drawn_inputs(seed))
    spreads = {'L0_attn_bq': (0.0, 0.613),
     'L0_attn_bk': (0.0, 0.8),
     'L0_attn_bv': (0.0, 0.306),
     'L0_attn_blk': (0.0, 0.8),
     'L0_attn_blv': (0.0, 0.1),
     'L0_attn_qn_w': (1.0, 0.6),
     'L0_attn_kn_w': (1.0, 0.6),
     'L0_attn_bo': (0.0, 0.1),
     'L0_xattn_gn_gamma': (1.0, 0.2),
     'L0_xattn_gn_beta': (0.0, 0.1)}
    factors = {'L0_attn_Wc': 8.0,
     'L0_attn_Wk': 6.661,
     'L0_attn_Wv': 3.131,
     'L0_attn_sink_k': 8.0,
     'L0_attn_sink_v': 8.0,
     'L0_ffn_Wr': 8.0,
     'L0_ffn_Wg': 8.0,
     'L0_ffn_Wu': 8.0,
     'L0_ffn_Wd': 8.0,
     'L0_ffn_Wsg': 14.287,
     'L0_ffn_Wsu': 4.702,
     'L0_ffn_Wsd': 4.677}
    for name, (base, spread) in spreads.items():
        noise = np.random.default_rng([zlib.crc32(name.encode()), seed]).standard_normal(out[name].shape)
        drawn = base * np.exp(spread * noise) if base else spread * noise
        out[name] = jnp.asarray(drawn.astype(out[name].dtype))
    for name, factor in factors.items():
        out[name] = (out[name] * factor).astype(out[name].dtype)
    return out
```

```python
from contextlib import ExitStack

import numpy as np

import concourse.bass as bass
from concourse import mybir

F32 = mybir.dt.float32
F32R = mybir.dt.float32r
BF16 = mybir.dt.bfloat16
ALU = mybir.AluOpType
ACT = mybir.ActivationFunctionType
AX_X = mybir.AxisListType.X

P = 128
B, S, D = 32, 64, 256
TOK = B * S
TILES = TOK // P
KD = D // P
NH, HD = 16, 128
G = 4
ST = NH // G
STEPS = TILES * ST
GW = G * HD
BLK = 16
NC = S // BLK
NE_ = B * NC
NK = S + NC + 1
HALF = 32
ROT = 2 * HALF
PC = NH * NC
SINK0 = S
SINKS = NH + 1
RH = D // HD
NE, EF, SF = 8, 176, 352
FALL = NE * EF + SF
FT = -(-FALL // P)
ET = NE * EF // P
CH = 4
CHUNKS = TILES // CH
CT = CH * P
PARTS = 3
RMS_EPS = 1e-6
LN_EPS = 1e-5
GN_EPS = 1e-3
KEPT0 = 9728
ARENA = KEPT0 + 2848
SCALE = float(HD) ** -0.5


def heads(ap, n):
    return ap.rearrange("p (h d) -> p h d", h=n)


def over(ap, n):
    return ap.unsqueeze(2).to_broadcast([ap.shape[0], ap.shape[1], n])


def halves(ap):
    return ap.rearrange("p h (a b) -> p h a b", a=2)


def wait(eng, sem, value):
    if not (isinstance(value, int) and value <= 0):
        eng.wait_ge(sem, value)


def carry(nc, stats):
    nc.vector.tensor_copy(stats[:, 101:102], stats[:, 0:1])


def program(nc, a, out, scratch):
    with ExitStack() as ctx:
        def sb(name, shape, dt=F32):
            return ctx.enter_context(nc.sbuf_tensor(name, shape, dt))

        mem = {
            "w_split": sb("w_split", [P, 3, 2, KD, NH * HD], F32R),
            "wo": sb("wo", [P, NH, D]),
            "x1": sb("x1", [P, TILES, D]),
            "qk_bias": sb("qk_bias", [P, 2, NH * HD]),
            "arena": sb("arena", [P, ARENA]),
            "x_hi": sb("x_hi", [P, KD, P], F32R),
            "x_lo": sb("x_lo", [P, KD, P], F32R),
            "ident": sb("ident", [P, P]),
            "identb": sb("identb", [P, P], BF16),
            "maskb": sb("maskb", [P, G * NK], BF16),
            "rot_c": sb("rot_c", [P, 2, HD]),
            "rot_s": sb("rot_s", [P, 2, ROT]),
            "ckT": sb("ckT", [P, NE_]),
            "sink_rows": sb("sink_rows", [P, D]),
            "stats": sb("stats", [P, 128]),
            "w_parts": sb("w_parts", [P, CT], BF16),
            "select": sb("select", [P, ET * P], BF16),
        }
        psum = ctx.enter_context(nc.psum_tensor("psum", [P, 8 * 512], F32))
        banks = [psum[:, i * 512:(i + 1) * 512] for i in range(8)]
        prologue(nc, a, scratch, mem, banks)
        attention(nc, a, scratch, mem, banks)
        mixing(nc, a, mem, psum)
        feed_forward(nc, a, mem, psum, out)


def prologue(nc, a, scratch, mem, banks):
    w_split, wo, ident = mem["w_split"], mem["wo"], mem["ident"]
    arena = mem["arena"]
    raw = [arena[:, 0:4096], arena[:, 4096:8192]]
    prod = wo[:, :, :].rearrange("p h n -> p (h n)")
    cw = mem["x1"][:, :, :].rearrange("p t d -> p (t d)")
    late = arena[:, KEPT0:ARENA]
    x_blk = mem["x1"][:, :, :]
    entry = late[:, 0:256]
    entryT = late[:, 256:512].rearrange("p (k e) -> p k e", k=KD)
    wc_b = late[:, 512:768]
    wk6 = late[:, 768:1024].rearrange("p (k d) -> p k d", k=KD)
    wv6 = late[:, 1024:1280].rearrange("p (k d) -> p k d", k=KD)
    ck = late[:, 1280:1408]
    ck_rot = late[:, 1408:1536]
    ck_part = late[:, 1536:1600]
    bk_b = late[:, 1600:1728]
    cvT = late[:, 1728:1856]
    cos_e = late[:, 1856:1984]
    sin_e = late[:, 1984:2048]
    cos_t = late[:, 2048:2176]
    sin_t = late[:, 2176:2240]
    norm_w = late[:, 2240:2496].rearrange("p (k d) -> p k d", k=2)
    sink_vT = late[:, 2496:2512]
    blvT = late[:, 2512:2528]
    bv_c = late[:, 2528:2529]
    bc_b = late[:, 2529:2530]
    logit = late[:, 2560:2576]
    weight = late[:, 2576:2592]
    one = [late[:, 2592 + i:2593 + i] for i in range(8)]
    sink_l = raw[0][:, 0:NH * (SINK0 + SINKS)]
    lw = SINK0 + SINKS

    with ExitStack() as ctx:
        def sem(name):
            return ctx.enter_context(nc.semaphore(name))

        loaded_blk, loaded_small, loaded_entry_w = sem("loaded_blk"), sem("loaded_small"), sem("loaded_entry_w")
        loaded_raw = [sem(f"loaded_raw{i}") for i in range(4)]
        loaded_const = sem("loaded_const")
        split_hi, split_lo, wo_halved = sem("split_hi"), sem("split_lo"), sem("wo_halved")
        w_logits, w_exp, entries_done = sem("w_logits"), sem("w_exp"), sem("entries_done")
        entry_turned, entryT_copied = sem("entry_turned"), sem("entryT_copied")
        ck_raw, cv_raw, cvT_done = sem("ck_raw"), sem("cv_raw"), sem("cvT_done")
        ck_sumsq, ck_inv, ck_ready, ck_turned = sem("ck_sumsq"), sem("ck_inv"), sem("ck_ready"), sem("ck_turned")
        cw_ready, cw_copied, cw_stored = sem("cw_ready"), sem("cw_copied"), sem("cw_stored")
        sink_l_ready, sink_ready = sem("sink_l_ready"), sem("sink_ready")
        dve_own, pool_own = sem("dve_own"), sem("pool_own")
        ck_done, bo_loaded = sem("ck_done"), sem("bo_loaded")
        block = ctx.enter_context(nc.Block())

        @block.sync
        def _(sp):
            sp.dma_start(x_blk, a["x"].rearrange("(e r) d -> e r d", r=BLK)).then_inc(loaded_blk, 16)
            sp.dma_start(wc_b, a["Wc"].partition_broadcast(P)).then_inc(loaded_blk, 16)
            sp.dma_start(bc_b, a["bc"].partition_broadcast(P)).then_inc(loaded_blk, 16)
            for i, name in enumerate(("Wq", "Wlk")):
                sp.dma_start(raw[i].rearrange("p (k n) -> p k n", k=KD),
                             a[name].rearrange("(k p) n -> p k n", p=P)).then_inc(loaded_raw[i], 16)
            sp.wait_ge(split_lo, 1)
            sp.dma_start(raw[0].rearrange("p (k n) -> p k n", k=KD),
                         a["Wlv"].rearrange("(k p) n -> p k n", p=P)).then_inc(loaded_raw[2], 16)
            sp.wait_ge(split_lo, 2)
            sp.dma_start(raw[1].rearrange("p (h n) -> p h n", h=NH),
                         a["Wo"].rearrange("(h p) n -> p h n", p=P)).then_inc(loaded_raw[3], 16)
            for h in range(0, NH, 2):
                sp.wait_ge(cw_copied, h // 2 + 1)
                sp.dma_start(scratch[:, h * D:(h + 2) * D], cw[:, h * D:(h + 2) * D]).then_inc(cw_stored, 16)
            sp.wait_ge(cw_stored, 16 * NH // 2)

        @block.scalar
        def _(act):
            for dst, src in ((ident[:, :], a["ident"]), (cos_e, a["cos_entry"]), (sin_e, a["sin_entry"]),
                             (cos_t, a["cos_token"]), (sin_t, a["sin_token"]),
                             (norm_w[:, 0, :], a["qn_w"].partition_broadcast(P)),
                             (norm_w[:, 1, :], a["kn_w"].partition_broadcast(P)),
                             (prod[:, 0:G * NK], a["mask"])):
                act.dma_start(dst, src).then_inc(loaded_const, 16)
            for dst, src in ((wk6, a["Wk"].rearrange("(k p) n -> p k n", p=P)),
                             (wv6, a["Wv"].rearrange("(k p) n -> p k n", p=P)),
                             (bk_b, a["bk"].partition_broadcast(P)), (bv_c, a["bvT"]),
                             (sink_vT, a["sink_vT"]), (blvT, a["blvT"])):
                act.dma_start(dst, src).then_inc(loaded_entry_w, 16)
            for i, name in enumerate(("bq", "blk")):
                act.dma_start(mem["qk_bias"][:, i, :], a[name].partition_broadcast(P)).then_inc(loaded_small, 16)
            act.wait_ge(w_logits, 1)
            nc.scalar.activation(weight, logit, ACT.Exp).then_inc(w_exp, 1)
            for i in range(3):
                act.wait_ge(loaded_raw[i], 16)
                nc.scalar.activation(w_split[:, i, 0, :, :], raw[i % 2].rearrange("p (k n) -> p k n", k=KD),
                                     ACT.Copy).then_inc(split_hi, 1)
                if i == 1:
                    act.wait_ge(entry_turned, 1)
                    nc.scalar.activation(entryT, banks[0][:, 0:KD * P].rearrange("p (k e) -> p k e", k=KD),
                                         ACT.Copy).then_inc(entryT_copied, 1)
                    act.wait_ge(cv_raw, 1)
                    nc.scalar.activation(cvT, banks[2][:, 0:P], ACT.Identity, bias=bv_c).then_inc(cvT_done, 1)
            act.wait_ge(loaded_raw[3], 16)
            nc.scalar.activation(wo[:, :, :], raw[1].rearrange("p (h n) -> p h n", h=NH), ACT.Copy,
                                 scale=0.5).then_inc(wo_halved, 1)
            for h in range(0, NH, 2):
                act.wait_ge(cw_ready, h // 2 + 1)
                nc.scalar.activation(cw[:, h * D:(h + 2) * D], banks[h // 2][:, :], ACT.Copy).then_inc(cw_copied, 1)
            act.wait_ge(sink_ready, 1)
            act.wait_ge(bo_loaded, 32)
            act.wait_ge(loaded_small, 32)

        @block.gpsimd
        def _(pool):
            def link(ins, n=[0]):
                n[0] += 1
                ins.then_inc(pool_own, 1)
                pool.wait_ge(pool_own, n[0])

            nc.gpsimd.memset(mem["stats"][:, 0:8], -0.5).then_inc(pool_own, 1)
            nc.gpsimd.memset(mem["sink_rows"][:, :], 0.0).then_inc(pool_own, 1)
            nc.gpsimd.memset(mem["stats"][:, 104:112], HD * RMS_EPS)
            nc.gpsimd.memset(mem["stats"][:, 112:113], LN_EPS)
            nc.gpsimd.memset(mem["stats"][:, 113:114], GN_EPS).then_inc(pool_own, 1)
            pool.wait_ge(pool_own, 3)
            pool.dma_start(mem["sink_rows"][SINK0 + NH:SINK0 + SINKS, :], a["bo"]).then_inc(bo_loaded, 16)
            pool.dma_start(one[7], a["bc"].partition_broadcast(P)).then_inc(bo_loaded, 16)
            pool.wait_ge(ck_sumsq, 1)
            nc.gpsimd.tensor_scalar(one[1], one[0], 1.0 / HD, RMS_EPS, ALU.mult, ALU.add).then_inc(pool_own, 1)
            pool.wait_ge(pool_own, 4)
            nc.gpsimd.tensor_tensor(one[2], one[1], mem["stats"][:, 0:1], ALU.pow).then_inc(ck_inv, 1)

        @block.vector
        def _(dve):
            count = [0]

            def link(ins):
                count[0] += 1
                ins.then_inc(dve_own, 1)
                dve.wait_ge(dve_own, count[0])

            dve.wait_ge(loaded_const, 16 * 8)
            link(nc.vector.tensor_copy(mem["maskb"][:, :], prod[:, 0:G * NK]))
            nc.vector.tensor_copy(mem["identb"][:, :], ident[:, :]).then_inc(dve_own, 1)
            count[0] += 1
            for i in range(2):
                link(nc.vector.scalar_tensor_tensor(out=mem["rot_c"][:, i, :], in0=cos_t, scalar=float(HD) ** 0.5,
                                                    in1=norm_w[:, i, :], op0=ALU.mult, op1=ALU.mult))
                for half in range(2):
                    link(nc.vector.scalar_tensor_tensor(
                        out=mem["rot_s"][:, i, half * HALF:(half + 1) * HALF],
                        in0=sin_t[:, half * HALF:(half + 1) * HALF], scalar=float(HD) ** 0.5,
                        in1=norm_w[:, i, (1 - half) * HALF:(2 - half) * HALF], op0=ALU.mult, op1=ALU.mult))
            dve.wait_ge(loaded_blk, 48)
            prod3 = prod.rearrange("p (r d) -> p r d", r=BLK)
            link(nc.vector.tensor_tensor(prod3, x_blk, wc_b.unsqueeze(1).to_broadcast([P, BLK, D]), ALU.mult))
            link(nc.vector.tensor_reduce(logit, prod3, AX_X, ALU.add))
            link(nc.vector.tensor_scalar(logit, logit, bc_b, None, ALU.add))
            link(nc.vector.tensor_reduce(one[3], logit, AX_X, ALU.max))
            nc.vector.tensor_scalar(logit, logit, one[3], None, ALU.subtract).then_inc(w_logits, 1)
            dve.wait_ge(w_exp, 1)
            link(nc.vector.tensor_reduce(one[4], weight, AX_X, ALU.add))
            link(nc.vector.reciprocal(one[5], one[4]))
            link(nc.vector.tensor_scalar(weight, weight, one[5], None, ALU.mult))
            link(nc.vector.tensor_tensor(prod3, x_blk, over(weight, D), ALU.mult))
            nc.vector.tensor_reduce(entry, prod.rearrange("p (r d) -> p d r", r=BLK), AX_X,
                                    ALU.add).then_inc(entries_done, 1)
            for i in range(3):
                dve.wait_ge(split_hi, i + 1)
                nc.vector.tensor_tensor(w_split[:, i, 1, :, :], raw[i % 2].rearrange("p (k n) -> p k n", k=KD),
                                        w_split[:, i, 0, :, :].bitcast(F32), ALU.subtract).then_inc(split_lo, 1)
                if i == 0:
                    dve.wait_ge(ck_raw, 1)
                    link(nc.vector.tensor_tensor(ck, banks[1][:, 0:HD], bk_b, ALU.add))
                    nc.vector.tensor_tensor_reduce(out=ck_rot, in0=ck, in1=ck, scale=1.0, scalar=0.0, op0=ALU.mult,
                                                   op1=ALU.add, accum_out=one[0]).then_inc(ck_sumsq, 1)
                    link(nc.vector.tensor_tensor(cos_e, cos_e, norm_w[:, 1, :], ALU.mult))
                    for half in range(2):
                        link(nc.vector.tensor_tensor(
                            sin_e[:, half * HALF:(half + 1) * HALF], sin_e[:, half * HALF:(half + 1) * HALF],
                            norm_w[:, 1, (1 - half) * HALF:(2 - half) * HALF], ALU.mult))
                    dve.wait_ge(ck_inv, 1)
                    link(nc.vector.tensor_scalar(ck, ck, one[2], None, ALU.mult))
                    link(nc.vector.tensor_tensor(ck_rot, ck, cos_e, ALU.mult))
                    for half in range(2):
                        link(nc.vector.tensor_tensor(
                            ck_part[:, half * HALF:(half + 1) * HALF], ck[:, (1 - half) * HALF:(2 - half) * HALF],
                            sin_e[:, half * HALF:(half + 1) * HALF], ALU.mult))
                    nc.vector.tensor_tensor(ck_rot[:, 0:ROT], ck_rot[:, 0:ROT], ck_part, ALU.add).then_inc(ck_ready, 1)
            dve.wait_ge(split_lo, 3)
            dve.wait_ge(loaded_entry_w, 16 * 6)
            link(nc.vector.memset(sink_l, 0.0))
            link(nc.vector.tensor_copy(sink_l[:, SINK0:SINK0 + (lw + 1) * (NH - 1) + 1:lw + 1], sink_vT))
            nc.vector.tensor_copy(sink_l[:, lw - 1::lw], blvT).then_inc(sink_l_ready, 1)
            dve.wait_ge(ck_turned, 1)
            nc.vector.tensor_copy(mem["ckT"][:, :], banks[3][:, 0:P]).then_inc(ck_done, 1)
            dve.wait_ge(sink_ready, 1)
            dve.wait_ge(bo_loaded, 32)
            rows = mem["sink_rows"][SINK0:SINK0 + SINKS, :]
            link(nc.vector.tensor_tensor(rows, banks[0][SINK0:SINK0 + SINKS, 0:D], rows, ALU.add))

        @block.tensor
        def _(pe):
            pe.wait_ge(entries_done, 1)
            for k in range(KD):
                last = nc.tensor.transpose(banks[0][:, k * P:(k + 1) * P], entry[:, k * P:(k + 1) * P], ident[:, :])
            last.then_inc(entry_turned, 1)
            pe.wait_ge(entryT_copied, 1)
            pe.wait_ge(loaded_entry_w, 16 * 6)
            for k in range(KD):
                last = nc.tensor.matmul(banks[1][:, 0:HD], entryT[:, k, :], wk6[:, k, :], start=k == 0, stop=k == KD - 1)
            last.then_inc(ck_raw, 1)
            for k in range(KD):
                last = nc.tensor.matmul(banks[2][:, 0:P], wv6[:, k, :], entryT[:, k, :], start=k == 0, stop=k == KD - 1)
            last.then_inc(cv_raw, 1)
            pe.wait_ge(ck_ready, 1)
            nc.tensor.transpose(banks[3][:, 0:P], ck_rot, ident[:, :]).then_inc(ck_turned, 1)
            pe.wait_ge(cvT_done, 1)
            pe.wait_ge(wo_halved, 1)
            pe.wait_ge(ck_done, 1)
            for h in range(0, NH, 2):
                nc.tensor.matmul(banks[h // 2][:, :], cvT, wo[:, h:h + 2, :], start=True, stop=True).then_inc(cw_ready, 1)
            pe.wait_ge(sink_l_ready, 1)
            pe.wait_ge(cw_copied, 1)
            for h in range(NH):
                last = nc.tensor.matmul(banks[0][0:lw, 0:D], sink_l[:, h * lw:(h + 1) * lw], wo[:, h, :],
                                        start=h == 0, stop=h == NH - 1)
            last.then_inc(sink_ready, 1)


def attention(nc, a, scratch, mem, banks):
    cursor = [0]

    def carve(n):
        cursor[0] += n
        return mem["arena"][:, cursor[0] - n:cursor[0]]

    qk_b = carve(2 * GW)
    squares = carve(2 * GW)
    rot = [carve(2 * GW), carve(2 * GW)]
    rot_part = carve(2 * G * ROT)
    qT = carve(GW)
    v_sb = [carve(GW) for _ in range(ST)]
    ctxT = carve(GW)
    shifted = heads(carve(G * NK), G)
    e_sb = heads(carve(G * NK), G)
    p_loc = carve(G * S)
    p_comp = carve(PC + NH)
    pcT = carve(P)
    cw_t = carve(D)
    x_t = carve(D).rearrange("p (k n) -> p k n", k=KD)
    x_res = carve(D)
    h_sb = carve(D)
    assert cursor[0] <= KEPT0
    cursor[0] = KEPT0
    pT = carve(GW).rearrange("p (h q) -> p h q", h=G)
    kT = [carve(G * 2 * NK).rearrange("p (h b k) -> p h b k", h=G, b=2) for _ in range(ST)]
    sinkT = carve(P)
    w_split, wo, x1, ident = mem["w_split"], mem["wo"], mem["x1"], mem["ident"]
    x_hi, x_lo = mem["x_hi"], mem["x_lo"]
    stats = mem["stats"]
    neg_half = stats[:, 0:8]
    ss, inv = stats[:, 8:16], stats[:, 16:24]
    mx, sums, rsums = stats[:, 24:32], stats[:, 32:40], stats[:, 40:48]
    bn, mv, rstd, var_eps = stats[:, 48:54], stats[:, 54:56], stats[:, 56:57], stats[:, 57:58]
    ms = stats[:, 64:72]
    rms_eps, ln_eps = stats[:, 104:112], stats[:, 112:113]
    bank_q, bank_k, bank_v, bank_t0, bank_t1, bank_s, bank_p, bank_o = banks

    with ExitStack() as ctx:
        def sem(name):
            return ctx.enter_context(nc.semaphore(name))

        q_proj, k_proj, v_proj = sem("q_proj"), sem("k_proj"), sem("v_proj")
        q_biased, k_biased, v_copied = sem("q_biased"), sem("k_biased"), sem("v_copied")
        squared, summed_sq, ms_ready, inv_ready = sem("squared"), sem("summed_sq"), sem("ms_ready"), sem("inv_ready")
        cos_part, sin_part, rotated, normed = sem("cos_part"), sem("sin_part"), sem("rotated"), sem("normed")
        q_turned, k_turned, qT_copied, kT_copied = sem("q_turned"), sem("k_turned"), sem("qT_copied"), sem("kT_copied")
        ck_placed, scored, maxed, s_shifted = sem("ck_placed"), sem("scored"), sem("maxed"), sem("s_shifted")
        exped, e_summed, e_recip, probs = sem("exped"), sem("e_summed"), sem("e_recip"), sem("probs")
        p_turned, pT_copied, ctx_ready, ctx_copied = sem("p_turned"), sem("pT_copied"), sem("ctx_ready"), sem("ctx_copied")
        x_loaded, res_loaded, cw_loaded = sem("x_loaded"), sem("res_loaded"), sem("cw_loaded")
        x_high, x_split = sem("x_high"), sem("x_split")
        pc_turned, pcT_copied, o_ready = sem("pc_turned"), sem("pcT_copied"), sem("o_ready")
        h_summed, h_stats, h_mv, rstd_ready, x1_ready = sem("h_summed"), sem("h_stats"), sem("h_mv"), sem("rstd_ready"), sem("x1_ready")
        var_ready = sem("var_ready")
        zeroed, sinks_placed = sem("zeroed"), sem("sinks_placed")
        block = ctx.enter_context(nc.Block())

        def has(s0, g, lag):
            return not isinstance(s0, int) or 0 <= s0 + g - lag < STEPS

        def tiles(eng, tile):
            tile(0, 0)
            tile(1, ST)
            with eng.Fori(2, TILES) as t:
                tile(t, t * ST)
            tile(TILES, STEPS)

        @block.sync
        def _(sp):
            xT = a["xT"].rearrange("(k p) (t n) -> t p k n", p=P, n=P)
            xr = a["x"].rearrange("(t p) d -> t p d", p=P)
            cwr = scratch.rearrange("(t b c) (h n) -> t b h c n", b=2, c=NC, h=NH)

            def at(view, t):
                return view[t] if isinstance(t, int) else view[bass.ds(t, 1)][0]

            def tokens(t):
                wait(sp, x_split, t)
                sp.dma_start(x_t, at(xT, t)).then_inc(x_loaded, 16)

            def rest(t):
                wait(sp, h_summed, t)
                sp.dma_start(x_res, at(xr, t)).then_inc(res_loaded, 16)
                wait(sp, o_ready, t)
                src = at(cwr, t)
                for b in range(2):
                    for h in range(NH):
                        sp.dma_start(cw_t[b * PC + h * NC:b * PC + (h + 1) * NC, :], src[b, h]).then_inc(cw_loaded, 16)

            tokens(0)
            tokens(1)
            rest(0)
            with sp.Fori(1, TILES - 1) as t:
                tokens(t + 1)
                rest(t)
            rest(TILES - 1)

        @block.tensor
        def _(pe):
            def tile(t, s0):
                for g in range(ST):
                    s = s0 + g
                    if has(s0, g, 2):
                        wait(pe, normed, s - 1)
                        wait(pe, ctx_copied, s - 3)
                        wait(pe, kT_copied, s - 2)
                        src = rot[g % 2]
                        for j in range(G):
                            last = nc.tensor.transpose(bank_t0[:, j * P:(j + 1) * P], src[:, j * HD:(j + 1) * HD], ident[:, :])
                        last.then_inc(q_turned, 1)
                        for j in range(G):
                            last = nc.tensor.transpose(bank_t1[:, j * P:(j + 1) * P],
                                                       src[:, GW + j * HD:GW + (j + 1) * HD], ident[:, :])
                        last.then_inc(k_turned, 1)
                    if has(s0, g, 3):
                        wait(pe, probs, s - 2)
                        wait(pe, pT_copied, s - 3)
                        if g == 3:
                            wait(pe, pcT_copied, t)
                        for j in range(0, G, 2):
                            last = nc.tensor.transpose(bank_p[:, j * S:j * S + P], p_loc[:, j * S:j * S + P], ident[:, :])
                        last.then_inc(p_turned, 1)
                        if g == 2:
                            nc.tensor.transpose(bank_p[0:PC + NH, 256:256 + P], p_comp, ident[:, :]).then_inc(pc_turned, 1)
                    if has(s0, g, 4):
                        wait(pe, ctx_copied, s - 3)
                        if g == 0:
                            wait(pe, h_summed, t - 1)
                        for j in range(G):
                            nc.tensor.matmul(bank_o[:, 0:D], ctxT[:, j * P:(j + 1) * P], wo[:, g * G + j, :],
                                             start=g == 0 and j == 0, stop=False)
                        if g == ST - 1:
                            wait(pe, pcT_copied, t)
                            wait(pe, cw_loaded, t * (32 * 16))
                            nc.tensor.matmul(bank_o[:, 0:D], pcT, cw_t, start=False, stop=False)
                            nc.tensor.matmul(bank_o[:, 0:D], sinkT[SINK0:SINK0 + SINKS, :],
                                             mem["sink_rows"][SINK0:SINK0 + SINKS, :], start=False,
                                             stop=True).then_inc(o_ready, 1)
                    if has(s0, g, 2):
                        wait(pe, s_shifted, s - 2)
                        wait(pe, kT_copied, s - 1)
                        wait(pe, qT_copied, s - 1)
                        wait(pe, ck_placed, s - 1)
                        for b in range(2):
                            rows = slice(b * S, (b + 1) * S)
                            for j in range(G):
                                nc.tensor.matmul(bank_s[rows, j * NK:(j + 1) * NK], qT[:, j * P + b * S:j * P + (b + 1) * S],
                                                 kT[(g + 2) % ST][:, j, b, :], start=j == 0, stop=False)
                        nc.tensor.matmul(bank_s[:, 0:G * NK], mem["identb"][:, :], mem["maskb"][:, :],
                                         start=False, stop=True).then_inc(scored, 1)
                    if has(s0, g, 3):
                        wait(pe, pT_copied, s - 2)
                        wait(pe, v_copied, s - 2)
                        wait(pe, qT_copied, min(s - 1, STEPS) if isinstance(s, int) else s - 1)
                        for j in range(G):
                            last = nc.tensor.matmul(bank_t0[:, j * P:(j + 1) * P], v_sb[(g + 1) % ST][:, j * HD:(j + 1) * HD],
                                                    pT[:, j, :], start=True, stop=True)
                        last.then_inc(ctx_ready, 1)
                    if has(s0, g, 0):
                        if g == 0:
                            wait(pe, x_split, t + 1)
                        for i, (bk, free, done) in enumerate(((bank_q, q_biased, q_proj), (bank_k, k_biased, k_proj),
                                                              (bank_v, v_copied, v_proj))):
                            wait(pe, free, s)
                            n = 0
                            for k in range(KD):
                                for xs, part in ((x_hi, 0), (x_lo, 0), (x_hi, 1)):
                                    last = nc.tensor.matmul(bk[:, :], xs[:, k, :], w_split[:, i, part, k, g * GW:(g + 1) * GW],
                                                            start=n == 0, stop=n == 5)
                                    n += 1
                            last.then_inc(done, 1)
            tiles(pe, tile)

        @block.scalar
        def _(act):
            def tile(t, s0):
                for g in range(ST):
                    s = s0 + g
                    if has(s0, g, 2):
                        wait(act, q_turned, s - 1)
                        wait(act, scored, s - 2)
                        nc.scalar.activation(qT, bank_t0[:, :], ACT.Copy).then_inc(qT_copied, 1)
                        wait(act, k_turned, s - 1)
                        nc.scalar.activation(kT[(g + 2) % ST][:, :, :, 0:S],
                                             bank_t1[:, :].rearrange("p (h b k) -> p h b k", h=G, b=2),
                                             ACT.Copy).then_inc(kT_copied, 1)
                    if has(s0, g, 3):
                        wait(act, p_turned, s - 2)
                        if g == 2:
                            wait(act, pc_turned, t)
                        wait(act, ctx_ready, s - 3)
                        if isinstance(t, int) and t == 0 and g == 3:
                            act.wait_ge(zeroed, 5)
                        src = bank_p[:, 0:256].rearrange("p (a q) -> p a q", a=2)
                        for hj in range(2):
                            for b in range(2):
                                last = nc.scalar.activation(pT[b * S:(b + 1) * S, hj::2, b * S:(b + 1) * S],
                                                            src[hj * S:(hj + 1) * S, :, b * S:(b + 1) * S], ACT.Copy)
                        last.then_inc(pT_copied, 1)
                        if g == 2:
                            wait(act, o_ready, t - 1)
                            for b in range(2):
                                nc.scalar.activation(pcT[b * PC:(b + 1) * PC, b * S:(b + 1) * S],
                                                     bank_p[0:PC, 256 + b * S:256 + (b + 1) * S], ACT.Copy)
                            nc.scalar.activation(sinkT[SINK0:SINK0 + NH, :], bank_p[PC:PC + NH, 256:256 + P],
                                                 ACT.Copy).then_inc(pcT_copied, 1)
                    if has(s0, g, 2):
                        wait(act, s_shifted, s - 1)
                        nc.scalar.activation(e_sb, shifted, ACT.Exp, scale=SCALE).then_inc(exped, 1)
                    if has(s0, g, 3):
                        wait(act, ctx_ready, s - 2)
                        nc.scalar.activation(ctxT, bank_t0[:, :], ACT.Copy).then_inc(ctx_copied, 1)
                    if has(s0, g, 0):
                        wait(act, q_biased, s + 1)
                        wait(act, k_biased, s + 1)
                        wait(act, summed_sq, s)
                        nc.scalar.activation(squares, qk_b, ACT.Square).then_inc(squared, 1)
                        wait(act, v_proj, s + 1)
                        nc.scalar.activation(v_sb[g], bank_v[:, :], ACT.Copy).then_inc(v_copied, 1)
            tiles(act, tile)

        @block.vector
        def _(dve):
            nc.vector.memset(pT, 0.0).then_inc(zeroed, 1)
            nc.vector.memset(pcT, 0.0).then_inc(zeroed, 1)
            nc.vector.memset(sinkT[SINK0:P, :], 1.0).then_inc(zeroed, 1)
            for k in range(ST):
                pass

            def split(t):
                wait(dve, x_loaded, t * 16 + 16)
                wait(dve, v_proj, t * ST)
                nc.vector.tensor_copy(x_hi[:, :, :], x_t).then_inc(x_high, 1)
                wait(dve, x_high, t + 1)
                nc.vector.tensor_tensor(x_lo[:, :, :], x_t, x_hi[:, :, :].bitcast(F32), ALU.subtract).then_inc(x_split, 1)

            def tile(t, s0):
                for g in range(ST):
                    s = s0 + g
                    if g == 0 and has(s0, 0, 0):
                        split(t)
                    if has(s0, g, 1):
                        wait(dve, squared, s)
                        wait(dve, ms_ready, s - 1)
                        nc.vector.tensor_reduce(ss, heads(squares, 2 * G), AX_X, ALU.add).then_inc(summed_sq, 1)
                        r = rot[(g + 1) % 2]
                        wait(dve, k_turned, s - 2)
                        nc.vector.tensor_tensor(
                            r.rearrange("p (i h d) -> p i h d", i=2, h=G), qk_b.rearrange("p (i h d) -> p i h d", i=2, h=G),
                            mem["rot_c"][:, :, :].unsqueeze(2).to_broadcast([P, 2, G, HD]), ALU.mult).then_inc(cos_part, 1)
                        wait(dve, cos_part, s)
                        wait(dve, sin_part, s)
                        rr = heads(r, 2 * G)[:, :, 0:ROT]
                        nc.vector.tensor_tensor(rr, rr, heads(rot_part, 2 * G), ALU.add).then_inc(rotated, 1)
                    if g == ST - 1 and has(s0, 0, ST):
                        wait(dve, o_ready, t)
                        wait(dve, res_loaded, t * 16)
                        nc.vector.tensor_tensor(h_sb, bank_o[:, 0:D], x_res, ALU.add).then_inc(h_summed, 1)
                        wait(dve, h_summed, t)
                        nc.vector.bn_stats(bn, h_sb).then_inc(h_stats, 1)
                        wait(dve, h_stats, t)
                        carry(nc, stats)
                        nc.vector.bn_aggr(mv, bn).then_inc(h_mv, 1)
                    if has(s0, g, 2):
                        sc = heads(bank_s[:, 0:G * NK], G)
                        wait(dve, scored, s - 1)
                        wait(dve, exped, s - 2)
                        nc.vector.tensor_reduce(mx[:, 0:G], sc[:, :, 0:S], AX_X, ALU.max)
                        nc.vector.tensor_reduce(mx[:, G:2 * G], sc[:, :, S:NK], AX_X, ALU.max).then_inc(maxed, 1)
                        wait(dve, maxed, s - 1)
                        nc.vector.tensor_tensor(shifted[:, :, 0:S], sc[:, :, 0:S], over(mx[:, 0:G], S), ALU.subtract)
                        nc.vector.tensor_tensor(shifted[:, :, S:NK], sc[:, :, S:NK], over(mx[:, G:2 * G], NC + 1),
                                                ALU.subtract).then_inc(s_shifted, 1)
                    if has(s0, g, 0):
                        wait(dve, squared, s)
                        wait(dve, sin_part, s)
                        wait(dve, q_proj, s + 1)
                        nc.vector.tensor_tensor(qk_b[:, 0:GW], bank_q[:, :], mem["qk_bias"][:, 0, g * GW:(g + 1) * GW],
                                                ALU.add).then_inc(q_biased, 1)
                        wait(dve, k_proj, s + 1)
                        nc.vector.tensor_tensor(qk_b[:, GW:2 * GW], bank_k[:, :], mem["qk_bias"][:, 1, g * GW:(g + 1) * GW],
                                                ALU.add).then_inc(k_biased, 1)
                    if has(s0, g, 2):
                        gg = (g + 2) % ST
                        wait(dve, exped, s - 1)
                        nc.vector.tensor_reduce(sums[:, 0:G], e_sb[:, :, 0:S], AX_X, ALU.add)
                        nc.vector.tensor_reduce(sums[:, G:2 * G], e_sb[:, :, S:NK], AX_X, ALU.add).then_inc(e_summed, 1)
                        wait(dve, e_summed, s - 1)
                        nc.vector.reciprocal(rsums, sums).then_inc(e_recip, 1)
                        wait(dve, e_recip, s - 1)
                        wait(dve, p_turned, s - 2)
                        nc.vector.tensor_tensor(heads(p_loc, G), e_sb[:, :, 0:S], over(rsums[:, 0:G], S), ALU.mult)
                        if gg == 0:
                            wait(dve, pc_turned, t)
                        nc.vector.tensor_tensor(p_comp[:, gg * G * NC:(gg + 1) * G * NC].rearrange("p (h c) -> p h c", h=G),
                                                e_sb[:, :, S:S + NC], over(rsums[:, G:2 * G], NC), ALU.mult)
                        nc.vector.tensor_tensor(p_comp[:, PC + gg * G:PC + (gg + 1) * G].unsqueeze(2), e_sb[:, :, NK - 1:NK],
                                                rsums[:, G:2 * G].unsqueeze(2), ALU.mult).then_inc(probs, 1)
                    if g == ST - 1 and has(s0, 0, ST):
                        wait(dve, rstd_ready, t)
                        dst = x1[:, t - 1, :] if isinstance(t, int) else x1[:, bass.ds(t - 1, 1), :].squeeze(1)
                        nc.vector.tensor_scalar(dst, h_sb, mv[:, 0:1], rstd, ALU.subtract, ALU.mult).then_inc(x1_ready, 1)

            tiles(dve, tile)
            wait(dve, x1_ready, TILES)

        @block.gpsimd
        def _(pool):
            pool.dma_start(ctx_sink := p_comp[:, 0:NH], a["sink_kT"]).then_inc(sinks_placed, 16)
            pool.wait_ge(sinks_placed, 16)
            for k in range(ST):
                for b in range(2):
                    nc.gpsimd.tensor_copy(kT[k][:, :, b, NK - 1:NK], ctx_sink[:, k * G:(k + 1) * G].unsqueeze(2)).then_inc(zeroed, 1)

            def tile(t, s0):
                for g in range(ST):
                    s = s0 + g
                    if has(s0, g, 1):
                        wait(pool, scored, s - ST)
                        wait(pool, q_biased, s)
                        wait(pool, k_biased, s)
                        wait(pool, rotated, s - 1)
                        src = qk_b.rearrange("p (i h d) -> p i h d", i=2, h=G)
                        part = rot_part.rearrange("p (i h d) -> p i h d", i=2, h=G)
                        for i in range(2):
                            last = nc.gpsimd.tensor_tensor(
                                halves(part[:, i]), halves(src[:, i, :, 0:ROT])[:, :, ::-1, :],
                                mem["rot_s"][:, i, :].rearrange("p (a b) -> p a b", a=2).unsqueeze(1)
                                .to_broadcast([P, G, 2, HALF]), ALU.mult)
                        last.then_inc(sin_part, 1)
                        wait(pool, inv_ready, s - 1)
                        wait(pool, summed_sq, s)
                        nc.gpsimd.tensor_tensor(ms, ss, rms_eps, ALU.add).then_inc(ms_ready, 1)
                        wait(pool, ms_ready, s)
                        wait(pool, normed, s - 1)
                        nc.gpsimd.tensor_tensor(inv, ms, neg_half, ALU.pow).then_inc(inv_ready, 1)
                        wait(pool, inv_ready, s)
                        wait(pool, rotated, s)
                        r = heads(rot[(g + 1) % 2], 2 * G)
                        nc.gpsimd.tensor_tensor(r, r, over(inv, HD), ALU.mult).then_inc(normed, 1)
                    if g == ST - 1 and has(s0, 0, ST):
                        rsqrt_var(t - 1)
                    if has(s0, g, 1):
                        gg = (g + ST - 1) % ST
                        tt = t if g else t - 1
                        src = (ckT_at(tt)).rearrange("p (b c) -> p b c", b=2)
                        for j in range(G):
                            last = nc.gpsimd.tensor_copy(kT[gg][:, j, :, S:S + NC], src)
                        last.then_inc(ck_placed, 1)

            def ckT_at(t):
                return mem["ckT"][:, t * 2 * NC:(t + 1) * 2 * NC] if isinstance(t, int) else mem["ckT"][:, bass.ds(t * (2 * NC), 2 * NC)]

            def rsqrt_var(t):
                wait(pool, h_mv, t + 1)
                nc.gpsimd.tensor_tensor(var_eps, mv[:, 1:2], ln_eps, ALU.add).then_inc(var_ready, 1)
                wait(pool, var_ready, t + 1)
                nc.gpsimd.tensor_tensor(rstd, var_eps, neg_half[:, 0:1], ALU.pow).then_inc(rstd_ready, 1)

            tiles(pool, tile)


def mixing(nc, a, mem, psum):
    arena, x1, ident, stats = mem["arena"], mem["x1"], mem["ident"], mem["stats"]
    v_all = arena[:, 0:TILES * D].rearrange("p (t d) -> p t d", t=TILES)
    w_all = arena[:, TILES * D:2 * TILES * D].rearrange("p (t d) -> p t d", t=TILES)
    low = arena[:, 2 * TILES * D:ARENA]
    mixT = low[:, 0:RH * P].rearrange("p (h q) -> p h q", h=RH)
    cursor = [RH * P]

    def carve(n):
        cursor[0] += n
        assert cursor[0] <= ARENA - 2 * TILES * D
        return low[:, cursor[0] - n:cursor[0]]

    xg = [carve(2 * D) for _ in range(2)]
    cT = [carve(D).rearrange("p (h n) -> p h n", h=RH) for _ in range(2)]
    xs = [carve(D) for _ in range(2)]
    wg = carve(KD * D).rearrange("p (k n) -> p k n", k=KD)
    wh = carve(RH * HD).rearrange("p (h e) -> p h e", h=RH)
    whT = carve(RH * HD).rearrange("p (h e) -> p h e", h=RH)
    gram = carve(RH * HD).rearrange("p (h e) -> p h e", h=RH)
    decay = carve(RH * S)
    mix = carve(RH * S)
    zero = carve(P).bitcast(BF16)
    raw = mem["qk_bias"][:, :, :].rearrange("p i n -> p (i n)")[:, 0:KD * FALL].rearrange("p (k n) -> p k n", k=KD)
    wd = mem["wo"][:, :, :]
    gu = ffn_weights(mem)
    b_xg = [psum[:, i * 512:(i + 1) * 512] for i in range(2)]
    b_v = [psum[:, (2 + i) * 512:(2 + i) * 512 + D] for i in range(2)]
    b_w = [psum[:, (4 + i) * 512:(4 + i) * 512 + D] for i in range(2)]
    b_s = psum[:, 6 * 512:7 * 512]
    b_t = psum[:, 7 * 512:8 * 512]

    with ExitStack() as ctx:
        def sem(name):
            return ctx.enter_context(nc.semaphore(name))

        cT_loaded = [sem(f"cT_loaded{i}") for i in range(2)]
        staged, xg_ready, v_ready, xg_copied, v_stored = sem("staged"), sem("xg_ready"), sem("v_ready"), sem("xg_copied"), sem("v_stored")
        w_ready, w_stored, s_added = sem("w_ready"), sem("w_stored"), sem("s_added")
        small_loaded, gram_ready, gram_copied, zeroed = sem("small_loaded"), sem("gram_ready"), sem("gram_copied"), sem("mix_zeroed")
        s_closed, decayed, mix_ready, mix_turned, mix_placed = sem("s_closed"), sem("decayed"), sem("mix_ready"), sem("mix_turned"), sem("mix_placed")
        raw_loaded, ffn_hi, ffn_lo, wd_loaded = sem("raw_loaded"), sem("ffn_hi"), sem("ffn_lo"), sem("wd_loaded")
        block = ctx.enter_context(nc.Block())

        def pairs(eng, tile):
            for t in range(4):
                tile(t, t % 2)
            with eng.Fori(2, TILES // 2) as pair:
                tile(pair * 2, 0)
                tile(pair * 2 + 1, 1)
            tile(TILES, 0)

        def new(t):
            return not isinstance(t, int) or t < TILES

        def lag(t):
            return not isinstance(t, int) or t > 0

        def at(view, t):
            return view[:, t, :] if isinstance(t, int) else view[:, bass.ds(t, 1), :].squeeze(1)

        @block.sync
        def _(sp):
            for dst, src in ((whT, a["WhT"].rearrange("h e d -> e h d")), (wh, a["Wh"].rearrange("h d e -> d h e")),
                             (wg, a["wg_w"].rearrange("(k p) n -> p k n", p=P)), (decay[0:S, :], a["decay"])):
                sp.dma_start(dst, src).then_inc(small_loaded, 16)
            cTv = a["ctxT"].rearrange("(h p) (t n) -> t p h n", p=P, n=P)
            for name in range(2):
                sp.dma_start(cT[name], cTv[name]).then_inc(cT_loaded[name], 16)
            sp.dma_start(raw, a["gateT"].rearrange("(k p) n -> p k n", p=P)).then_inc(raw_loaded, 16)
            sp.dma_start(wd[:, 0:FT - 1, :], a["down"][0:(FT - 1) * P, :].rearrange("(f p) n -> p f n", p=P)).then_inc(wd_loaded, 16)
            sp.dma_start(wd[0:FALL - (FT - 1) * P, FT - 1, :], a["down"][(FT - 1) * P:FALL, :]).then_inc(wd_loaded, 16)
            with sp.Fori(1, TILES // 2) as pair:
                for i in range(2):
                    sp.wait_ge(v_ready, pair * 2 + (i - 1))
                    sp.dma_start(cT[i], cTv[bass.ds(pair * 2 + i, 1)][0]).then_inc(cT_loaded[i], 16)
            sp.wait_ge(ffn_lo, 1)
            sp.dma_start(raw, a["upT"].rearrange("(k p) n -> p k n", p=P)).then_inc(raw_loaded, 16)
            sp.wait_ge(wd_loaded, 32)

        @block.tensor
        def _(pe):
            pe.wait_ge(small_loaded, 64)
            for h in range(RH):
                last = nc.tensor.matmul(b_t[:, h * HD:(h + 1) * HD], whT[:, h, :], whT[:, h, :], start=True, stop=True)
            last.then_inc(gram_ready, 1)
            pe.wait_ge(gram_copied, 1)
            pe.wait_ge(zeroed, 2)
            nc.tensor.matmul(b_s[0:S, 0:RH * S], zero[:, 0:S], zero[:, 0:RH * S], start=True, stop=False)

            def tile(t, i):
                if new(t):
                    wait(pe, staged, t + 1)
                    wait(pe, xg_copied, t - 1)
                    wait(pe, cT_loaded[i], 8 * (t - i) + 16)
                    for k in range(KD):
                        nc.tensor.transpose(b_xg[i][:, k * P:(k + 1) * P], xs[i][:, k * P:(k + 1) * P], ident[:, :])
                    for h in range(RH):
                        last = nc.tensor.matmul(b_xg[i][:, D + h * P:D + (h + 1) * P], gram[:, h, :], cT[i][:, h, :],
                                                start=True, stop=True)
                    last.then_inc(xg_ready, 1)
                    wait(pe, v_stored, t - 1)
                    for h in range(RH):
                        last = nc.tensor.matmul(b_v[i][:, h * HD:(h + 1) * HD], cT[i][:, h, :], wh[:, h, :],
                                                start=True, stop=True)
                    last.then_inc(v_ready, 1)
                if lag(t):
                    j = 1 - i
                    wait(pe, xg_copied, t)
                    wait(pe, w_stored, t - 2)
                    for k in range(KD):
                        last = nc.tensor.matmul(b_w[j], xg[j][:, k * P:(k + 1) * P], wg[:, k, :], start=k == 0, stop=k == KD - 1)
                    last.then_inc(w_ready, 1)
                    for b in range(2):
                        for h in range(RH):
                            c = h * P + b * S
                            last = nc.tensor.matmul(b_s[0:S, h * S:(h + 1) * S], xg[j][:, c:c + S], xg[j][:, D + c:D + c + S],
                                                    start=False, stop=False)
                    last.then_inc(s_added, 1)
            pairs(pe, tile)
            nc.tensor.matmul(b_s[0:S, 0:RH * S], zero[:, 0:S], zero[:, 0:RH * S], start=False, stop=True).then_inc(s_closed, 1)
            pe.wait_ge(mix_ready, 1)
            nc.tensor.transpose(b_t[:, 0:S], mix[0:S, :], ident[0:S, 0:S]).then_inc(mix_turned, 1)

        @block.scalar
        def _(act):
            act.wait_ge(gram_ready, 1)
            nc.scalar.activation(gram, b_t[:, 0:RH * HD].rearrange("p (h e) -> p h e", h=RH), ACT.Copy).then_inc(gram_copied, 1)

            def tile(t, i):
                if new(t):
                    wait(act, xg_ready, t - 1)
                    nc.scalar.activation(xs[i], at(x1, t), ACT.Copy).then_inc(staged, 1)
                    wait(act, xg_ready, t + 1)
                    wait(act, s_added, t - 1)
                    nc.scalar.activation(xg[i], b_xg[i], ACT.Copy).then_inc(xg_copied, 1)
            pairs(act, tile)
            act.wait_ge(mix_turned, 1)
            for h in range(RH):
                for b in range(2):
                    last = nc.scalar.activation(mixT[b * S:(b + 1) * S, h, b * S:(b + 1) * S], b_t[h * S:(h + 1) * S, 0:S], ACT.Copy)
            last.then_inc(mix_placed, 1)
            act.wait_ge(mix_placed, 1)

        @block.vector
        def _(dve):
            nc.vector.memset(mixT, 0.0).then_inc(zeroed, 1)
            nc.vector.memset(zero, 0.0).then_inc(zeroed, 1)

            def tile(t, i):
                if new(t):
                    wait(dve, v_ready, t + 1)
                    nc.vector.tensor_copy(at(v_all, t), b_v[i]).then_inc(v_stored, 1)
                if lag(t):
                    wait(dve, w_ready, t)
                    nc.vector.tensor_scalar(at(w_all, t - 1), b_w[1 - i], 0.0, None, ALU.max).then_inc(w_stored, 1)
            pairs(dve, tile)
            dve.wait_ge(s_closed, 1)
            nc.vector.tensor_tensor(mix[0:S, :], b_s[0:S, 0:RH * S], decay[0:S, :], ALU.mult).then_inc(decayed, 1)
            dve.wait_ge(decayed, 1)
            nc.vector.scalar_tensor_tensor(out=mix[0:S, :], in0=mix[0:S, :], scalar=-1.0, in1=mix[0:S, :], op0=ALU.mult,
                                           op1=ALU.max).then_inc(decayed, 1)
            dve.wait_ge(decayed, 2)
            nc.vector.tensor_scalar(mix[0:S, :], mix[0:S, :], 1.0, None, ALU.max).then_inc(mix_ready, 1)
            dve.wait_ge(v_stored, TILES)
            dve.wait_ge(w_stored, TILES)

        @block.gpsimd
        def _(pool):
            for i in range(2):
                pool.wait_ge(raw_loaded, 16 * (i + 1))
                nc.gpsimd.tensor_copy(gu[:, i, 0], raw).then_inc(ffn_hi, 1)
                pool.wait_ge(ffn_hi, i + 1)
                nc.gpsimd.tensor_tensor(gu[:, i, 1], raw, gu[:, i, 0].bitcast(F32), ALU.subtract).then_inc(ffn_lo, 1)
            pool.wait_ge(ffn_lo, 2)


def ffn_weights(mem):
    flat = mem["w_split"][:, :, :, :, :].rearrange("p i j k n -> p (i j k n)")
    return flat[:, 0:4 * KD * FALL].rearrange("p (i j k n) -> p i j k n", i=2, j=2, k=KD)


def feed_forward(nc, a, mem, psum, out):
    arena, x1, ident, stats = mem["arena"], mem["x1"], mem["ident"], mem["stats"]
    v_all = arena[:, 0:TILES * D].rearrange("p (t d) -> p t d", t=TILES)
    w_all = arena[:, TILES * D:2 * TILES * D].rearrange("p (t d) -> p t d", t=TILES)
    low = arena[:, 2 * TILES * D:ARENA]
    mixT = low[:, 0:RH * P].rearrange("p (h q) -> p h q", h=RH)
    cursor = [RH * P]

    def carve(n):
        cursor[0] += n
        assert cursor[0] <= ARENA - 2 * TILES * D
        return low[:, cursor[0] - n:cursor[0]]

    wo_w = carve(KD * D).rearrange("p (k n) -> p k n", k=KD)
    gamma, beta = carve(D), carve(D)
    x2n = carve(CH * D)
    sil = carve(CT)
    hid = [carve(CT) for _ in range(2)]
    rank = [carve(CH * NE * NE) for _ in range(2)]
    flat = mem["qk_bias"][:, :, :].rearrange("p i n -> p (i n)")
    y = flat[:, 0:CH * D]
    turned = flat[:, CH * D:2 * CH * D]
    h3 = flat[:, 2 * CH * D:3 * CH * D]
    x2c = flat[:, 3 * CH * D:4 * CH * D]
    gu = ffn_weights(mem)
    rflat = mem["w_split"][:, :, :, :, :].rearrange("p i j k n -> p (i j k n)")[:, 4 * KD * FALL:]
    x2_hi = rflat[:, 0:KD * CT].rearrange("p (k n) -> p k n", k=KD)
    x2_lo = rflat[:, KD * CT:2 * KD * CT].rearrange("p (k n) -> p k n", k=KD)
    wd = mem["wo"][:, :, :]
    select = mem["select"]
    wr = mem["ckT"][:, 0:KD * NE].rearrange("p (k e) -> p k e", k=KD)
    before = mem["rot_c"][:, 0, 0:NE * NE].rearrange("p (e j) -> p e j", e=NE)
    zero = mem["rot_c"][:, 1, 0:64].bitcast(BF16)
    zeros = mem["sink_rows"][:, :].bitcast(BF16)
    score = mem["rot_s"][:, 0, 0:CH * NE].rearrange("p (t e) -> p t e", t=CH)
    ranks = mem["rot_s"][:, 0, 32:32 + CH * NE].rearrange("p (t e) -> p t e", t=CH)
    rest = mem["rot_s"][:, 1, 0:CH * NE].rearrange("p (t e) -> p t e", t=CH)
    parts = mem["maskb"][:, 0:CH * PARTS * NE].rearrange("p (t c e) -> p t c e", t=CH, c=PARTS)
    wT_b = mem["w_parts"][0:PARTS * NE, :]
    smax, ssum, srec = stats[:, 8:12], stats[:, 12:16], stats[:, 16:20]
    bn = [stats[:, 20 + 6 * j:26 + 6 * j] for j in range(CH)]
    mv = stats[:, 44:52].rearrange("p (t c) -> p t c", t=CH)
    ve, rstd = stats[:, 52:56], stats[:, 56:60]
    bn3 = [stats[:, 60 + 6 * j:66 + 6 * j] for j in range(CH)]
    mv3 = stats[:, 84:92].rearrange("p (t c) -> p t c", t=CH)
    ve3, rstd3 = stats[:, 92:96], stats[:, 96:100]
    neg_half = stats[:, 0:CH]
    ln_eps, gn_eps = stats[:, 112:113], stats[:, 113:114]
    b_g, b_u, b_w = [psum[:, i * 512:(i + 1) * 512] for i in range(3)]
    b_acc = psum[:, 3 * 512:5 * 512]
    b_f = psum[:, 5 * 512:7 * 512]
    b_r = psum[:, 7 * 512:8 * 512]

    def tok(ap):
        return ap.rearrange("p (t d) -> p t d", t=CH)

    with ExitStack() as ctx:
        def sem(name):
            return ctx.enter_context(nc.semaphore(name))

        g_ready, u_ready, w_ready = sem("g_ready"), sem("u_ready"), sem("wsel_ready")
        silued, gated, hid_ready, down_done = sem("silued"), sem("gated"), sem("hid_ready"), sem("down_done")
        o_ready, o_stats, o_mv, o_var, o_rstd, o_normed = [sem("f_" + n) for n in ("o_ready", "o_stats", "o_mv", "o_var", "o_rstd", "o_normed")]
        scaled, biased, wy_ready, wy_turned, wyT_copied, mixed = [sem("f_" + n) for n in ("scaled", "biased", "wy_ready", "wy_turned", "wyT_copied", "mixed")]
        h_ready, h_stats, h_mv, h_var, h_rstd, x2_ready = [sem("f_" + n) for n in ("h_ready", "h_stats", "h_mv", "h_var", "h_rstd", "x2_ready")]
        x2_turned, x2T_copied, logits, maxed, less, exped = [sem("f_" + n) for n in ("x2_turned", "x2T_copied", "logits", "maxed", "less", "exped")]
        summed, recip, scored, ranked, parts_ready, parts_turned, wT_ready = [sem("f_" + n) for n in ("summed", "recip", "scored", "ranked", "parts_ready", "parts_turned", "wT_ready")]
        own, split3 = sem("f_own"), sem("f_split3")
        high, split, cur_copied = sem("f_high"), sem("f_split"), sem("f_cur_copied")
        acc_ready, h3_ready, h3_stats, h3_mv, h3_var, h3_rstd, y3_ready, stored = [
            sem("t_" + n) for n in ("acc_ready", "h3_ready", "h3_stats", "h3_mv", "h3_var", "h3_rstd", "y3_ready", "stored")]
        f_loaded, sel_loaded, sel_ready, zeroed = sem("f_loaded"), sem("sel_loaded"), sem("sel_ready"), sem("f_zeroed")
        block = ctx.enter_context(nc.Block())

        def chunks(eng, front, slot, turn, tail=None):
            for i in range(FT):
                front(i, 0)
            turn(0)

            def both(c):
                for i in range(FT):
                    slot(c, i)
                    front(i, c + 1)
                end(eng, c)
                turn(c + 1)
            both(0)
            with eng.Fori(1, CHUNKS - 1) as c:
                both(c)
            for i in range(FT):
                slot(CHUNKS - 1, i)
            end(eng, CHUNKS - 1)
            if tail is not None:
                tail()

        ends = {}

        def end(eng, c):
            if eng in ends:
                ends[eng](c)

        def part(view, f):
            return view[:, f * CH:(f + 1) * CH, :] if isinstance(f, int) else view[:, bass.ds(f * CH, CH), :]

        @block.sync
        def _(sp):
            for dst, src in ((wo_w, a["wo_w"].rearrange("(k p) n -> p k n", p=P)), (gamma, a["gn_gamma"].partition_broadcast(P)),
                             (beta, a["gn_beta"].partition_broadcast(P)), (wr, a["WrT"].rearrange("(k p) e -> p k e", p=P)),
                             (before, a["before"].partition_broadcast(P))):
                sp.dma_start(dst, src).then_inc(f_loaded, 16)
            sp.dma_start(h3[0:PARTS * NE, 0:CH * D], a["select"][:, 0:CH * D]).then_inc(sel_loaded, 16)
            sp.dma_start(x2c[0:PARTS * NE, 0:ET * P - CH * D], a["select"][:, CH * D:ET * P]).then_inc(sel_loaded, 16)
            o = out.rearrange("(c t p) d -> c p t d", t=CH, p=P)

            def store(c):
                wait(sp, y3_ready, c + 1)
                dst = o[c] if isinstance(c, int) else o[bass.ds(c, 1)][0]
                sp.dma_start(dst, tok(h3)).then_inc(stored, 16)
            with sp.Fori(0, CHUNKS) as c:
                store(c)
            sp.wait_ge(stored, 16 * CHUNKS)

        @block.tensor
        def _(pe):
            pe.wait_ge(f_loaded, 16 * 5)
            pe.wait_ge(zeroed, 1)
            pe.wait_ge(sel_ready, 1)

            def front(i, f):
                if i == 0:
                    wait(pe, x2T_copied, f)
                    for h in range(RH):
                        last = nc.tensor.matmul(b_f[:, h * 512:(h + 1) * 512].rearrange("p (t e) -> p t e", t=CH), mixT[:, h, :],
                                                part(v_all, f)[:, :, h * HD:(h + 1) * HD], start=True, stop=True)
                    last.then_inc(o_ready, 1)
                if i == 4:
                    wait(pe, wy_ready, f + 1)
                    wait(pe, o_normed, f + 1)
                    for k in range(KD):
                        for t in range(CH):
                            last = nc.tensor.transpose(b_f[:, k * CT + t * P:k * CT + (t + 1) * P],
                                                       y[:, t * D + k * P:t * D + (k + 1) * P], ident[:, :])
                    last.then_inc(wy_turned, 1)
                if i == 5:
                    wait(pe, wyT_copied, f + 1)
                    for t in range(CH):
                        for k in range(KD):
                            last = nc.tensor.matmul(b_f[:, t * D:(t + 1) * D], turned[:, k * CT + t * P:k * CT + (t + 1) * P],
                                                    wo_w[:, k, :], start=k == 0, stop=k == KD - 1)
                    last.then_inc(mixed, 1)
                if i == 8:
                    wait(pe, x2_ready, f + 1)
                    wait(pe, h_ready, f + 1)
                    for k in range(KD):
                        for t in range(CH):
                            last = nc.tensor.transpose(b_f[:, k * CT + t * P:k * CT + (t + 1) * P],
                                                       x2n[:, t * D + k * P:t * D + (k + 1) * P], ident[:, :])
                    last.then_inc(x2_turned, 1)
                if i == 9:
                    wait(pe, x2T_copied, f + 1)
                    wait(pe, wT_ready, f)
                    for t in range(CH):
                        for k in range(KD):
                            last = nc.tensor.matmul(b_r[:, t * NE:(t + 1) * NE], turned[:, k * CT + t * P:k * CT + (t + 1) * P],
                                                    wr[:, k, :], start=k == 0, stop=k == KD - 1)
                    last.then_inc(logits, 1)
                if i == 12:
                    wait(pe, parts_ready, f + 1)
                    for t in range(CH):
                        last = nc.tensor.transpose(b_rb[0:PARTS * NE, t * P:(t + 1) * P],
                                                   parts[:, t].rearrange("p c e -> p (c e)"), mem["identb"][:, :])
                    last.then_inc(parts_turned, 1)

            b_rb = b_r[:, 0:CT // 2].bitcast(BF16)

            def down(c, i):
                n = rows(i)
                wait(pe, hid_ready, c * FT + (i + 1))
                for t in range(CH):
                    last = nc.tensor.matmul(b_acc[:, t * D:(t + 1) * D], hid[i % 2][0:n, t * P:(t + 1) * P], wd[0:n, i, :],
                                            start=False, stop=False)
                last.then_inc(down_done, 1)

            def slot(c, i):
                n = rows(i)
                cols = slice(i * P, i * P + n)
                if i == 0:
                    wait(pe, split, c + 1)
                for which, bk, free, done in ((0, b_g, silued, g_ready), (1, b_u, gated, u_ready)):
                    wait(pe, free, c * FT + i)
                    m = 0
                    for k in range(KD):
                        for xs, p in ((x2_hi, 0), (x2_lo, 0), (x2_hi, 1)):
                            last = nc.tensor.matmul(bk[0:n, :], gu[:, which, p, k, cols], xs[:, k, :], start=m == 0, stop=m == 5)
                            m += 1
                    last.then_inc(done, 1)
                if i < ET:
                    if i == 0:
                        wait(pe, wT_ready, c + 1)
                    wait(pe, hid_ready, c * FT + i)
                    nc.tensor.matmul(b_w[:, :], select[0:PARTS * NE, i * P:(i + 1) * P], wT_b, start=True,
                                     stop=True).then_inc(w_ready, 1)
                if i == 0:
                    wait(pe, h3_ready, c)
                    for k in range(2):
                        nc.tensor.matmul(b_acc[:, k * 512:(k + 1) * 512], zero[:, 0:P], zeros[:, :], start=True, stop=False)
                else:
                    down(c, i - 1)
                if i == FT - 1:
                    down(c, i)
                    for k in range(2):
                        last = nc.tensor.matmul(b_acc[:, k * 512:(k + 1) * 512], zero[:, 0:P], zeros[:, :], start=False, stop=True)
                    last.then_inc(acc_ready, 1)

            chunks(pe, front, slot, lambda f: None)

        @block.scalar
        def _(act):
            act.wait_ge(sel_loaded, 32)
            nc.scalar.activation(select[0:PARTS * NE, 0:CH * D], h3[0:PARTS * NE, :], ACT.Copy)
            nc.scalar.activation(select[0:PARTS * NE, CH * D:ET * P], x2c[0:PARTS * NE, 0:ET * P - CH * D], ACT.Copy).then_inc(sel_ready, 1)

            def front(i, f):
                if i == 4:
                    wait(act, wy_turned, f + 1)
                    wait(act, split, f)
                    nc.scalar.activation(turned, b_f, ACT.Copy).then_inc(wyT_copied, 1)
                if i == 8:
                    wait(act, x2_turned, f + 1)
                    wait(act, mixed, f + 1)
                    nc.scalar.activation(turned, b_f, ACT.Copy).then_inc(x2T_copied, 1)
                if i == 10:
                    wait(act, less, f + 1)
                    nc.scalar.activation(score, score, ACT.Exp).then_inc(exped, 1)

            def slot(c, i):
                n = rows(i)
                wait(act, g_ready, c * FT + (i + 1))
                wait(act, gated, c * FT + i)
                nc.scalar.activation(sil[0:n, :], b_g[0:n, :], ACT.Silu).then_inc(silued, 1)

            def turn(f):
                wait(act, u_ready, f * FT)
                wait(act, x2T_copied, f + 1)
                nc.scalar.activation(x2_hi, turned.rearrange("p (k n) -> p k n", k=KD), ACT.Copy).then_inc(high, 1)
                wait(act, h3_ready, f)
                wait(act, x2_ready, f + 1)
                nc.scalar.activation(x2c, x2n, ACT.Copy).then_inc(cur_copied, 1)

            chunks(act, front, slot, turn)

        @block.vector
        def _(dve):
            nc.vector.memset(zeros, 0.0)
            nc.vector.memset(zero, 0.0).then_inc(zeroed, 1)
            dve.wait_ge(f_loaded, 16 * 5)
            dve.wait_ge(sel_ready, 1)
            OWN = 5

            def front(i, f):
                if i == 0:
                    wait(dve, o_ready, f + 1)
                    o = b_f.rearrange("p (h t e) -> p h t e", h=RH, t=CH)
                    for t in range(CH):
                        last = nc.vector.bn_stats(bn[t], o[:, :, t, :])
                    last.then_inc(o_stats, 1)
                    wait(dve, o_stats, f + 1)
                    carry(nc, stats)
                    for t in range(CH):
                        last = nc.vector.bn_aggr(mv[:, t, :], bn[t])
                    last.then_inc(o_mv, 1)
                if i == 1:
                    wait(dve, o_rstd, f + 1)
                    o = b_f.rearrange("p (h t e) -> p h t e", h=RH, t=CH)
                    for t in range(CH):
                        last = nc.vector.tensor_scalar(y[:, t * D:(t + 1) * D].rearrange("p (h e) -> p h e", h=RH), o[:, :, t, :],
                                                       mv[:, t, 0:1], rstd[:, t:t + 1], ALU.subtract, ALU.mult)
                    last.then_inc(o_normed, 1)
                if i == 3:
                    wait(dve, biased, f + 1)
                    nc.vector.tensor_tensor(tok(y), tok(y), part(w_all, f), ALU.mult).then_inc(wy_ready, 1)
                if i == 6:
                    wait(dve, mixed, f + 1)
                    wait(dve, wy_turned, f + 1)
                    nc.vector.tensor_tensor(tok(y), tok(b_f), part(x1, f), ALU.add).then_inc(h_ready, 1)
                    wait(dve, h_ready, f + 1)
                    for t in range(CH):
                        last = nc.vector.bn_stats(bn[t], y[:, t * D:(t + 1) * D])
                    last.then_inc(h_stats, 1)
                    wait(dve, h_stats, f + 1)
                    carry(nc, stats)
                    for t in range(CH):
                        last = nc.vector.bn_aggr(mv[:, t, :], bn[t])
                    last.then_inc(h_mv, 1)
                if i == 7:
                    wait(dve, h_rstd, f + 1)
                    wait(dve, cur_copied, f)
                    for t in range(CH):
                        last = nc.vector.tensor_scalar(x2n[:, t * D:(t + 1) * D], y[:, t * D:(t + 1) * D], mv[:, t, 0:1],
                                                       rstd[:, t:t + 1], ALU.subtract, ALU.mult)
                    last.then_inc(x2_ready, 1)
                if i == 10:
                    lg = b_r[:, 0:CH * NE].rearrange("p (t e) -> p t e", t=CH)
                    wait(dve, logits, f + 1)
                    nc.vector.tensor_reduce(smax, lg, AX_X, ALU.max).then_inc(maxed, 1)
                    wait(dve, maxed, f + 1)
                    nc.vector.tensor_tensor(score, lg, over(smax, NE), ALU.subtract).then_inc(less, 1)
                if i == 11:
                    wait(dve, exped, f + 1)
                    nc.vector.tensor_reduce(ssum, score, AX_X, ALU.add).then_inc(summed, 1)
                    wait(dve, summed, f + 1)
                    nc.vector.reciprocal(srec, ssum).then_inc(recip, 1)
                    wait(dve, recip, f + 1)
                    nc.vector.tensor_tensor(score, score, over(srec, NE), ALU.mult).then_inc(scored, 1)
                    wait(dve, scored, f + 1)
                    for t in range(CH):
                        above = rank[0][:, t * 64:(t + 1) * 64].rearrange("p (e j) -> p e j", e=NE)
                        equal = rank[1][:, t * 64:(t + 1) * 64].rearrange("p (e j) -> p e j", e=NE)
                        of_j = score[:, t, :].unsqueeze(1).to_broadcast([P, NE, NE])
                        of_e = over(score[:, t, :], NE)
                        nc.vector.tensor_tensor(above, of_j, of_e, ALU.is_gt)
                        last = nc.vector.tensor_tensor(equal, of_j, of_e, ALU.is_equal)
                    last.then_inc(own, 1)
                    wait(dve, own, f * OWN + 1)
                    r1 = rank[1].rearrange("p (t e j) -> p t (e j)", t=CH, e=NE)
                    nc.vector.tensor_tensor(r1, r1, before.rearrange("p e j -> p (e j)").unsqueeze(1).to_broadcast([P, CH, NE * NE]),
                                            ALU.mult).then_inc(own, 1)
                    wait(dve, own, f * OWN + 2)
                    nc.vector.tensor_tensor(rank[0], rank[0], rank[1], ALU.add).then_inc(own, 1)
                    wait(dve, own, f * OWN + 3)
                    nc.vector.tensor_reduce(ranks, rank[0].rearrange("p (t e j) -> p t e j", t=CH, e=NE), AX_X,
                                            ALU.add).then_inc(ranked, 1)
                    wait(dve, ranked, f + 1)
                    nc.vector.tensor_scalar(ranks, ranks, 1.5, None, ALU.is_lt).then_inc(own, 1)
                    wait(dve, own, f * OWN + 4)
                    nc.vector.tensor_tensor(rest, score, ranks, ALU.mult).then_inc(own, 1)
                    wait(dve, own, f * OWN + 5)
                    for c in range(PARTS):
                        nc.vector.tensor_copy(parts[:, :, c, :], rest).then_inc(split3, 1)
                        wait(dve, split3, f * (2 * PARTS) + (2 * c + 1))
                        nc.vector.tensor_tensor(rest, rest, parts[:, :, c, :], ALU.subtract).then_inc(split3, 1)
                        wait(dve, split3, f * (2 * PARTS) + (2 * c + 2))
                    nc.vector.tensor_copy(smax, srec).then_inc(parts_ready, 1)
                if i == 12:
                    wait(dve, parts_turned, f + 1)
                    wait(dve, w_ready, f * ET)
                    nc.vector.tensor_copy(wT_b, b_r[:, 0:CT // 2].bitcast(BF16)[0:PARTS * NE, :]).then_inc(wT_ready, 1)

            def slot(c, i):
                n = rows(i)
                wait(dve, u_ready, c * FT + (i + 1))
                wait(dve, silued, c * FT + (i + 1))
                h = hid[i % 2][0:n, :]
                if not (isinstance(c, int) and c * FT + i < 2):
                    if isinstance(c, int) or i >= 2:
                        wait(dve, down_done, c * FT + (i - 1))
                if i < ET:
                    nc.vector.tensor_tensor(h, sil[0:n, :], b_u[0:n, :], ALU.mult).then_inc(gated, 1)
                    wait(dve, w_ready, c * ET + (i + 1))
                    wait(dve, gated, c * FT + (i + 1))
                    nc.vector.tensor_tensor(h, h, b_w[0:n, :], ALU.mult).then_inc(hid_ready, 1)
                else:
                    nc.vector.tensor_tensor(h, sil[0:n, :], b_u[0:n, :], ALU.mult).then_inc(gated, 1)
                    wait(dve, gated, c * FT + (i + 1))
                    nc.vector.tensor_copy(stats[:, 100:101], stats[:, 0:1]).then_inc(hid_ready, 1)
                if i == 1:
                    pass

            def stats3(c):
                for t in range(CH):
                    last = nc.vector.bn_stats(bn3[t], h3[:, t * D:(t + 1) * D])
                last.then_inc(h3_stats, 1)
                wait(dve, h3_stats, c + 1)
                carry(nc, stats)
                for t in range(CH):
                    last = nc.vector.bn_aggr(mv3[:, t, :], bn3[t])
                last.then_inc(h3_mv, 1)
                wait(dve, h3_rstd, c + 1)
                for t in range(CH):
                    last = nc.vector.tensor_scalar(h3[:, t * D:(t + 1) * D], h3[:, t * D:(t + 1) * D], mv3[:, t, 0:1],
                                                   rstd3[:, t:t + 1], ALU.subtract, ALU.mult)
                last.then_inc(y3_ready, 1)

            def finish(c):
                wait(dve, acc_ready, c + 1)
                wait(dve, cur_copied, c + 1)
                wait(dve, stored, c * 16)
                nc.vector.tensor_tensor(h3, b_acc, x2c, ALU.add).then_inc(h3_ready, 1)
                wait(dve, h3_ready, c + 1)
                stats3(c)

            def turn(f):
                wait(dve, u_ready, f * FT)
                wait(dve, high, f + 1)
                nc.vector.tensor_tensor(x2_lo, turned.rearrange("p (k n) -> p k n", k=KD), x2_hi.bitcast(F32),
                                        ALU.subtract).then_inc(split, 1)

            ends[dve] = finish
            chunks(dve, front, slot, turn)

        @block.gpsimd
        def _(pool):
            pool.wait_ge(f_loaded, 16 * 5)
            pool.wait_ge(sel_ready, 1)

            def rsqrt(var, eps, tmp, dst, ready, between, done, n):
                wait(pool, ready, n)
                nc.gpsimd.tensor_tensor(tmp.unsqueeze(2), var[:, :, 1:2], eps.to_broadcast([P, CH]).unsqueeze(2),
                                        ALU.add).then_inc(between, 1)
                wait(pool, between, n)
                nc.gpsimd.tensor_tensor(dst, tmp, neg_half, ALU.pow).then_inc(done, 1)

            def front(i, f):
                if i == 0:
                    rsqrt(mv, gn_eps, ve, rstd, o_mv, o_var, o_rstd, f + 1)
                if i == 1:
                    wait(pool, o_normed, f + 1)
                    nc.gpsimd.tensor_tensor(tok(y), tok(y), gamma.unsqueeze(1).to_broadcast([P, CH, D]), ALU.mult).then_inc(scaled, 1)
                if i == 2:
                    wait(pool, scaled, f + 1)
                    nc.gpsimd.tensor_tensor(tok(y), tok(y), beta.unsqueeze(1).to_broadcast([P, CH, D]), ALU.add).then_inc(biased, 1)
                if i == 6:
                    rsqrt(mv, ln_eps, ve, rstd, h_mv, h_var, h_rstd, f + 1)

            def finish(c):
                rsqrt(mv3, ln_eps, ve3, rstd3, h3_mv, h3_var, h3_rstd, c + 1)

            ends[pool] = finish
            chunks(pool, front, lambda c, i: None, lambda f: None)


def rows(i):
    return min(P, FALL - i * P)


def constants():
    inv_freq = (1.0 / np.float32(10000.0) ** (np.arange(HALF, dtype=np.float32) * np.float32(2.0 / ROT))).astype(np.float32)

    def rotation(pos):
        ang = (pos.astype(np.float32)[:, None] * inv_freq[None, :]).astype(np.float32)
        c, s = np.cos(ang).astype(np.float32), np.sin(ang).astype(np.float32)
        ones = np.ones((len(pos), HD - ROT), np.float32)
        return np.concatenate([c, c, ones], 1), np.concatenate([-s, s], 1)

    pos = np.arange(P) % S
    ends = (np.arange(P) % NC) * BLK + BLK - 1
    cos_t, sin_t = rotation(pos)
    cos_e, sin_e = rotation(ends)
    open_ = np.concatenate([np.arange(S)[None] <= pos[:, None], (np.arange(NC) * BLK + BLK - 1)[None] <= pos[:, None],
                            np.ones((P, 1), bool)], 1)
    gam = (1.0 - 2.0 ** (-5.0 - np.arange(RH, dtype=np.float32))).astype(np.float32)
    expo = np.arange(S, dtype=np.float32)[None, :] - np.arange(S, dtype=np.float32)[:, None]
    dm = np.where(expo[None] <= 0, gam[:, None, None] ** expo[None], 0.0).astype(np.float32)
    dm = dm / np.sqrt(dm.sum(axis=-1))[:, None, :] / np.sqrt(np.float32(HD))
    decay = dm.transpose(1, 0, 2).reshape(S, RH * S).astype(np.float32)
    expert = np.arange(ET * P) // EF
    select = np.tile((expert[None] == np.arange(NE)[:, None]).astype(np.float32), (PARTS, 1))
    before = (np.arange(NE)[None] < np.arange(NE)[:, None]).astype(np.float32).reshape(1, -1)
    mask = np.where(open_, 0.0, -1e30).astype(np.float32)
    return {"ident": np.eye(P, dtype=np.float32), "cos_token": cos_t, "sin_token": sin_t, "cos_entry": cos_e,
            "sin_entry": sin_e, "mask": np.tile(mask, (1, G)), "decay": decay, "select": select, "before": before}


def kernel(**inputs):
    import concourse.bacc as _bacc
    from concourse import mybir as _mybir
    from concourse.bass_utils import run_bass_kernel_spmd as _run

    i = {k: np.asarray(v) for k, v in inputs.items()}
    at = {k[len("L0_attn_"):]: v for k, v in i.items() if k.startswith("L0_attn_")}
    x = i["x"].reshape(TOK, D)
    arrays = {
        "x": x, "xT": x.T, "Wq": at["Wq"], "Wlk": at["Wlk"], "Wlv": at["Wlv"], "Wo": at["Wo"],
        "Wk": at["Wk"], "Wv": at["Wv"], "Wc": at["Wc"].reshape(1, D), "bc": at["bc"].reshape(1, 1),
        "bq": at["bq"].reshape(1, -1), "blk": at["blk"].reshape(1, -1), "bk": at["bk"].reshape(1, -1),
        "bvT": at["bv"].reshape(HD, 1), "blvT": at["blv"].reshape(NH, HD).T, "qn_w": at["qn_w"].reshape(1, -1),
        "kn_w": at["kn_w"].reshape(1, -1), "sink_kT": at["sink_k"].T, "sink_vT": at["sink_v"].T,
        "bo": at["bo"].reshape(1, D),
    }
    xa = {k[len("L0_xattn_"):]: v for k, v in i.items() if k.startswith("L0_xattn_")}
    ff = {k[len("L0_ffn_"):]: v for k, v in i.items() if k.startswith("L0_ffn_")}
    arrays |= {
        "ctxT": i["ctx_2048"].reshape(TOK, D).T, "Wh": xa["Wh"], "WhT": xa["Wh"].transpose(0, 2, 1), "wg_w": xa["wg_w"],
        "wo_w": xa["wo_w"], "gn_gamma": xa["gn_gamma"].reshape(1, D), "gn_beta": xa["gn_beta"].reshape(1, D),
        "WrT": ff["Wr"].T,
        "gateT": np.concatenate([ff["Wg"].reshape(NE * EF, D), ff["Wsg"]]).T,
        "upT": np.concatenate([ff["Wu"].reshape(NE * EF, D), ff["Wsu"]]).T,
        "down": np.concatenate([ff["Wd"].transpose(0, 2, 1).reshape(NE * EF, D), ff["Wsd"].T]),
    }
    arrays |= constants()
    arrays = {k: np.ascontiguousarray(v) for k, v in arrays.items()}
    nc = _bacc.Bacc("TRN2", target_bir_lowering=False, num_devices=1)
    a = {k: nc.dram_tensor(f"in_{k}", v.shape, _mybir.dt.from_np(v.dtype), kind="ExternalInput").ap()
         for k, v in arrays.items()}
    out = nc.dram_tensor("out", (TOK, D), F32, kind="ExternalOutput").ap()
    scratch = nc.dram_tensor("cw_scratch", (NE_, NH * D), F32, kind="Internal").ap()
    program(nc, a, out, scratch)
    r = _run(nc, [{f"in_{k}": v for k, v in arrays.items()}], core_ids=[0])
    return r.results[0]["out"].reshape(B, S, D)
```

```python
from contextlib import ExitStack

import numpy as np

import concourse.bass as bass
from concourse import mybir

F32 = mybir.dt.float32
F32R = mybir.dt.float32r
BF16 = mybir.dt.bfloat16
ALU = mybir.AluOpType
ACT = mybir.ActivationFunctionType
AX_X = mybir.AxisListType.X

P = 128
B, S, D = 32, 64, 256
TOK = B * S
TILES = TOK // P
KD = D // P
NH, HD = 16, 128
G = 4
ST = NH // G
STEPS = TILES * ST
GW = G * HD
BLK = 16
NC = S // BLK
NE_ = B * NC
NK = S + NC + 1
HALF = 32
ROT = 2 * HALF
PC = NH * NC
SINK0 = S
SINKS = NH + 1
RH = D // HD
NE, EF, SF = 8, 176, 352
FALL = NE * EF + SF
FT = -(-FALL // P)
ET = NE * EF // P
CH = 4
CHUNKS = TILES // CH
CT = CH * P
PARTS = 3
RMS_EPS = 1e-6
LN_EPS = 1e-5
GN_EPS = 1e-3
KEPT0 = 9728
ARENA = KEPT0 + 2848
SCALE = float(HD) ** -0.5
CW_BANKS = (4, 5, 6, 7, 0, 2, 1, 4)


def heads(ap, n):
    return ap.rearrange("p (h d) -> p h d", h=n)


def over(ap, n):
    return ap.unsqueeze(2).to_broadcast([ap.shape[0], ap.shape[1], n])


def halves(ap):
    return ap.rearrange("p h (a b) -> p h a b", a=2)


def rows(i):
    return min(P, FALL - i * P)


def wait(eng, sem, value):
    if not (isinstance(value, int) and value <= 0):
        eng.wait_ge(sem, value)


def carry(nc, stats):
    nc.vector.tensor_copy(stats[:, 101:102], stats[:, 0:1])


def program(nc, a, out, scratch):
    with ExitStack() as ctx:
        def sb(name, shape, dt=F32):
            return ctx.enter_context(nc.sbuf_tensor(name, shape, dt))

        mem = {
            "w_split": sb("w_split", [P, 3, 2, KD, NH * HD], F32R),
            "wo": sb("wo", [P, NH, D]),
            "x1": sb("x1", [P, TILES, D]),
            "qk_bias": sb("qk_bias", [P, 2, NH * HD]),
            "arena": sb("arena", [P, ARENA]),
            "x_parts": sb("x_parts", [P, 2, KD, P], F32R),
            "gram": sb("gram", [P, RH, HD]),
            "wh": sb("wh", [P, RH, HD]),
            "wg": sb("wg", [P, KD, D]),
            "ident": sb("ident", [P, P]),
            "identb": sb("identb", [P, P], BF16),
            "maskb": sb("maskb", [P, G * NK], BF16),
            "rot_c": sb("rot_c", [P, 2, HD]),
            "rot_s": sb("rot_s", [P, 2, ROT]),
            "ckT": sb("ckT", [P, NE_]),
            "sink_rows": sb("sink_rows", [P, D]),
            "stats": sb("stats", [P, 128]),
            "w_parts": sb("w_parts", [P, CT], BF16),
            "select": sb("select", [P, ET * P], BF16),
        }
        psum = ctx.enter_context(nc.psum_tensor("psum", [P, 8 * 512], F32))
        banks = [psum[:, i * 512:(i + 1) * 512] for i in range(8)]
        mem["cw_stored"] = ctx.enter_context(nc.semaphore("cw_stored"))
        mem["wg_loaded"] = ctx.enter_context(nc.semaphore("wg_loaded"))
        prologue(nc, a, scratch, mem, banks)
        attention(nc, a, scratch, mem, banks)
        mixing(nc, a, mem, psum)
        feed_forward(nc, a, mem, psum, out)


def prologue(nc, a, scratch, mem, banks):
    w_split, wo, ident = mem["w_split"], mem["wo"], mem["ident"]
    arena = mem["arena"]
    prod = mem["qk_bias"][:, :, :].rearrange("p i n -> p (i n)")
    raw = [arena[:, 0:4096], arena[:, 4096:8192], prod]
    spare = arena[:, 8192:KEPT0]
    cw = mem["x1"][:, :, :].rearrange("p t d -> p (t d)")
    late = arena[:, KEPT0:ARENA]
    x_blk = mem["x1"][:, :, :]
    entry = late[:, 0:256]
    entryT = late[:, 256:512].rearrange("p (k e) -> p k e", k=KD)
    wc_b = late[:, 512:768]
    wk6 = late[:, 768:1024].rearrange("p (k d) -> p k d", k=KD)
    wv6 = late[:, 1024:1280].rearrange("p (k d) -> p k d", k=KD)
    ck = late[:, 1280:1408]
    ck_rot = late[:, 1408:1536]
    ck_part = late[:, 1536:1600]
    bk_b = late[:, 1600:1728]
    cvT = late[:, 1728:1856]
    cos_e = late[:, 1856:1984]
    sin_e = late[:, 1984:2048]
    cos_t = late[:, 2048:2176]
    sin_t = late[:, 2176:2240]
    norm_w = late[:, 2240:2496].rearrange("p (k d) -> p k d", k=2)
    sink_vT = late[:, 2496:2512]
    blvT = late[:, 2512:2528]
    bv_c = late[:, 2528:2529]
    bc_b = late[:, 2529:2530]
    logit = late[:, 2530:2546]
    weight = late[:, 2546:2562]
    one = [late[:, 2562 + i:2563 + i] for i in range(6)]
    mask = late[:, 2568:2568 + G * NK]
    lw = SINK0 + SINKS
    sink_l = spare[:, 0:NH * lw]
    x_t = spare[:, 0:D].rearrange("p (k n) -> p k n", k=KD)
    whT = mem["wg"][:, 0, :].rearrange("p (h d) -> p h d", h=RH)

    with ExitStack() as ctx:
        def sem(name):
            return ctx.enter_context(nc.semaphore(name))

        loaded_blk, loaded_entry_w, loaded_sink = sem("loaded_blk"), sem("loaded_entry_w"), sem("loaded_sink")
        loaded_raw = [sem(f"loaded_raw{i}") for i in range(3)]
        loaded_wo, loaded_const = sem("loaded_wo"), sem("loaded_const")
        split_hi = sem("split_hi")
        w_logits, w_exp, entries_done = sem("w_logits"), sem("w_exp"), sem("entries_done")
        entry_turned, entryT_copied = sem("entry_turned"), sem("entryT_copied")
        ck_raw, cv_raw, cvT_done = sem("ck_raw"), sem("cv_raw"), sem("cvT_done")
        ck_sumsq, ck_inv, ck_ready, ck_turned = sem("ck_sumsq"), sem("ck_inv"), sem("ck_ready"), sem("ck_turned")
        cw_ready, cw_copied, cw_stored = sem("cw_ready"), sem("cw_copied"), mem["cw_stored"]
        whT_loaded, gram_ready, x_loaded = sem("whT_loaded"), sem("gram_ready"), sem("first_x_loaded")
        gram_copied = sem("gram_copied")
        sink_l_ready, sink_ready = sem("sink_l_ready"), sem("sink_ready")
        dve_own, pool_own = sem("dve_own"), sem("pool_own")
        sink_rows_done, bo_loaded = sem("sink_rows_done"), sem("bo_loaded")
        block = ctx.enter_context(nc.Block())

        def halves_of(i, k):
            return raw[i].rearrange("p (k n) -> p k n", k=KD)[:, k, :], w_split[:, i, 0, k, :], w_split[:, i, 1, k, :]

        @block.sync
        def _(sp):
            sp.dma_start(x_blk, a["x"].rearrange("(e r) d -> e r d", r=BLK)).then_inc(loaded_blk, 16)
            sp.dma_start(wc_b, a["Wc"].partition_broadcast(P)).then_inc(loaded_blk, 16)
            sp.dma_start(bc_b, a["bc"].partition_broadcast(P)).then_inc(loaded_blk, 16)
            sp.dma_start(raw[0].rearrange("p (k n) -> p k n", k=KD),
                         a["Wq"].rearrange("(k p) n -> p k n", p=P)).then_inc(loaded_raw[0], 16)
            sp.dma_start(wo[:, :, :], a["Wo"].rearrange("(h p) n -> p h n", p=P)).then_inc(loaded_wo, 16)
            sp.dma_start(raw[1].rearrange("p (k n) -> p k n", k=KD),
                         a["Wlk"].rearrange("(k p) n -> p k n", p=P)).then_inc(loaded_raw[1], 16)
            sp.wait_ge(w_logits, 1)
            sp.dma_start(raw[2].rearrange("p (k n) -> p k n", k=KD),
                         a["Wlv"].rearrange("(k p) n -> p k n", p=P)).then_inc(loaded_raw[2], 16)
            sp.wait_ge(sink_ready, 1)
            sp.dma_start(x_t, a["xT"].rearrange("(k p) n -> p k n", p=P)[:, :, 0:P]).then_inc(x_loaded, 16)
            rows = scratch.rearrange("(b h c) n -> c b h n", h=NH, c=NC)
            for half in range(2):
                sp.wait_ge(cw_copied, (half + 1) * NH // 4)
                cols = slice(half * NH // 2, (half + 1) * NH // 2)
                for c in range(NC):
                    sp.dma_start(rows[c, :, cols, :], cw[c::NC, :].rearrange("p (h n) -> p h n", h=NH)[:, cols, :]).then_inc(cw_stored, 16)

        @block.scalar
        def _(act):
            for dst, src in ((sink_vT, a["sink_vT"]), (blvT, a["blvT"])):
                act.dma_start(dst, src).then_inc(loaded_sink, 16)
            act.dma_start(whT, a["WhT"].rearrange("h e d -> e h d")).then_inc(whT_loaded, 16)
            for dst, src in ((ident[:, :], a["ident"]), (cos_e, a["cos_entry"]), (sin_e, a["sin_entry"]),
                             (cos_t, a["cos_token"]), (sin_t, a["sin_token"]),
                             (norm_w[:, 0, :], a["qn_w"].partition_broadcast(P)),
                             (norm_w[:, 1, :], a["kn_w"].partition_broadcast(P)), (mask, a["mask"])):
                act.dma_start(dst, src).then_inc(loaded_const, 16)
            for dst, src in ((wk6, a["Wk"].rearrange("(k p) n -> p k n", p=P)),
                             (wv6, a["Wv"].rearrange("(k p) n -> p k n", p=P)),
                             (bk_b, a["bk"].partition_broadcast(P)), (bv_c, a["bvT"])):
                act.dma_start(dst, src).then_inc(loaded_entry_w, 16)

            def high(i, k):
                src, hi, _ = halves_of(i, k)
                nc.scalar.activation(hi, src, ACT.Copy).then_inc(split_hi, 1)

            act.wait_ge(gram_ready, 1)
            nc.scalar.activation(mem["gram"][:, :, :], banks[2][:, 0:RH * HD].rearrange("p (h e) -> p h e", h=RH),
                                 ACT.Copy).then_inc(gram_copied, 1)
            act.dma_start(mem["wh"][:, :, :], a["Wh"].rearrange("h d e -> d h e")).then_inc(mem["wg_loaded"], 16)
            act.dma_start(mem["wg"][:, :, :], a["wg_w"].rearrange("(k p) n -> p k n", p=P)).then_inc(mem["wg_loaded"], 16)
            act.wait_ge(loaded_raw[0], 16)
            high(0, 0)
            high(0, 1)
            act.wait_ge(w_logits, 1)
            nc.scalar.activation(weight, logit, ACT.Exp).then_inc(w_exp, 1)
            act.wait_ge(loaded_raw[1], 16)
            high(1, 0)
            high(1, 1)
            act.wait_ge(entry_turned, 1)
            nc.scalar.activation(entryT, banks[0][:, 0:KD * P].rearrange("p (k e) -> p k e", k=KD),
                                 ACT.Copy).then_inc(entryT_copied, 1)
            act.wait_ge(cv_raw, 1)
            nc.scalar.activation(cvT, banks[2][:, 0:P], ACT.Identity, bias=bv_c).then_inc(cvT_done, 1)
            act.wait_ge(loaded_raw[2], 16)
            high(2, 0)
            high(2, 1)
            for i in range(NH // 2):
                act.wait_ge(cw_ready, i + 1)
                nc.scalar.activation(cw[:, 2 * i * D:2 * (i + 1) * D], banks[CW_BANKS[i]][:, :], ACT.Copy,
                                     scale=0.5).then_inc(cw_copied, 1)

        @block.gpsimd
        def _(pool):
            nc.gpsimd.memset(mem["stats"][:, 0:8], -0.5).then_inc(pool_own, 1)
            nc.gpsimd.memset(mem["sink_rows"][:, :], 0.0).then_inc(pool_own, 1)
            nc.gpsimd.memset(mem["stats"][:, 104:112], HD * RMS_EPS)
            nc.gpsimd.memset(mem["stats"][:, 112:113], LN_EPS)
            nc.gpsimd.memset(mem["stats"][:, 113:114], GN_EPS).then_inc(pool_own, 1)
            pool.wait_ge(pool_own, 3)
            pool.dma_start(mem["sink_rows"][SINK0 + NH:SINK0 + SINKS, :], a["bo"]).then_inc(bo_loaded, 16)
            nc.gpsimd.memset(sink_l, 0.0).then_inc(pool_own, 1)
            pool.wait_ge(pool_own, 4)
            pool.wait_ge(loaded_sink, 32)
            nc.gpsimd.tensor_scalar(sink_l[:, SINK0:SINK0 + (lw + 1) * (NH - 1) + 1:lw + 1], sink_vT, 0.5, None,
                                    ALU.mult).then_inc(pool_own, 1)
            pool.wait_ge(pool_own, 5)
            nc.gpsimd.tensor_scalar(sink_l[:, lw - 1::lw], blvT, 0.5, None, ALU.mult).then_inc(sink_l_ready, 1)

            def low(i, k):
                src, hi, lo = halves_of(i, k)
                nc.gpsimd.tensor_tensor(lo, src, hi.bitcast(F32), ALU.subtract)

            pool.wait_ge(split_hi, 2)
            low(0, 0)
            low(0, 1)
            pool.wait_ge(split_hi, 3)
            low(1, 0)
            pool.wait_ge(ck_sumsq, 1)
            nc.gpsimd.tensor_scalar(one[1], one[0], 1.0 / HD, RMS_EPS, ALU.mult, ALU.add).then_inc(pool_own, 1)
            pool.wait_ge(pool_own, 6)
            nc.gpsimd.tensor_tensor(one[2], one[1], mem["stats"][:, 0:1], ALU.pow).then_inc(ck_inv, 1)
            pool.wait_ge(split_hi, 5)
            low(2, 0)

        @block.vector
        def _(dve):
            count = [0]

            def link(ins):
                count[0] += 1
                ins.then_inc(dve_own, 1)
                dve.wait_ge(dve_own, count[0])

            dve.wait_ge(loaded_blk, 48)
            prod3 = prod.rearrange("p (r d) -> p r d", r=BLK)
            link(nc.vector.tensor_tensor(prod3, x_blk, wc_b.unsqueeze(1).to_broadcast([P, BLK, D]), ALU.mult))
            link(nc.vector.tensor_reduce(logit, prod3, AX_X, ALU.add))
            link(nc.vector.tensor_scalar(logit, logit, bc_b, None, ALU.add))
            link(nc.vector.tensor_reduce(one[3], logit, AX_X, ALU.max))
            nc.vector.tensor_scalar(logit, logit, one[3], None, ALU.subtract).then_inc(w_logits, 1)
            dve.wait_ge(w_exp, 1)
            link(nc.vector.tensor_reduce(one[4], weight, AX_X, ALU.add))
            link(nc.vector.reciprocal(one[5], one[4]))
            link(nc.vector.tensor_scalar(weight, weight, one[5], None, ALU.mult))
            link(nc.vector.tensor_tensor(x_blk, x_blk, over(weight, D), ALU.mult))
            nc.vector.tensor_reduce(entry, cw.rearrange("p (r d) -> p d r", r=BLK), AX_X,
                                    ALU.add).then_inc(entries_done, 1)
            dve.wait_ge(loaded_const, 16 * 8)
            nc.vector.tensor_copy(mem["maskb"][:, :], mask)
            nc.vector.tensor_copy(mem["identb"][:, :], ident[:, :])
            for i in range(2):
                nc.vector.scalar_tensor_tensor(out=mem["rot_c"][:, i, :], in0=cos_t, scalar=float(HD) ** 0.5,
                                               in1=norm_w[:, i, :], op0=ALU.mult, op1=ALU.mult)
                for half in range(2):
                    nc.vector.scalar_tensor_tensor(
                        out=mem["rot_s"][:, i, half * HALF:(half + 1) * HALF],
                        in0=sin_t[:, half * HALF:(half + 1) * HALF], scalar=float(HD) ** 0.5,
                        in1=norm_w[:, i, (1 - half) * HALF:(2 - half) * HALF], op0=ALU.mult, op1=ALU.mult)
            nc.vector.tensor_tensor(cos_e, cos_e, norm_w[:, 1, :], ALU.mult)
            for half in range(2):
                last = nc.vector.tensor_tensor(
                    sin_e[:, half * HALF:(half + 1) * HALF], sin_e[:, half * HALF:(half + 1) * HALF],
                    norm_w[:, 1, (1 - half) * HALF:(2 - half) * HALF], ALU.mult)
            link(last)
            dve.wait_ge(ck_raw, 1)
            link(nc.vector.tensor_tensor(ck, banks[1][:, 0:HD], bk_b, ALU.add))
            nc.vector.tensor_tensor_reduce(out=ck_rot, in0=ck, in1=ck, scale=1.0, scalar=0.0, op0=ALU.mult,
                                           op1=ALU.add, accum_out=one[0]).then_inc(ck_sumsq, 1)

            def low(i, k):
                src, hi, lo = halves_of(i, k)
                nc.vector.tensor_tensor(lo, src, hi.bitcast(F32), ALU.subtract)

            dve.wait_ge(split_hi, 4)
            low(1, 1)
            dve.wait_ge(ck_inv, 1)
            link(nc.vector.tensor_scalar(ck, ck, one[2], None, ALU.mult))
            nc.vector.tensor_tensor(ck_rot, ck, cos_e, ALU.mult)
            for half in range(2):
                last = nc.vector.tensor_tensor(
                    ck_part[:, half * HALF:(half + 1) * HALF], ck[:, (1 - half) * HALF:(2 - half) * HALF],
                    sin_e[:, half * HALF:(half + 1) * HALF], ALU.mult)
            link(last)
            nc.vector.tensor_tensor(ck_rot[:, 0:ROT], ck_rot[:, 0:ROT], ck_part, ALU.add).then_inc(ck_ready, 1)
            dve.wait_ge(sink_ready, 1)
            dve.wait_ge(bo_loaded, 16)
            rows = mem["sink_rows"][SINK0:SINK0 + SINKS, :]
            nc.vector.tensor_tensor(rows, banks[3][SINK0:SINK0 + SINKS, 0:D], rows, ALU.add).then_inc(sink_rows_done, 1)
            dve.wait_ge(x_loaded, 16)
            link(nc.vector.tensor_copy(mem["x_parts"][:, 0], x_t))
            nc.vector.tensor_tensor(mem["x_parts"][:, 1], x_t, mem["x_parts"][:, 0].bitcast(F32), ALU.subtract)
            dve.wait_ge(split_hi, 6)
            low(2, 1)
            dve.wait_ge(ck_turned, 1)
            nc.vector.tensor_copy(mem["ckT"][:, :], banks[3][:, D:D + P])

        @block.tensor
        def _(pe):
            pe.wait_ge(whT_loaded, 16)
            for h in range(RH):
                last = nc.tensor.matmul(banks[2][:, h * HD:(h + 1) * HD], whT[:, h, :], whT[:, h, :], start=True, stop=True)
            last.then_inc(gram_ready, 1)
            pe.wait_ge(sink_l_ready, 1)
            pe.wait_ge(loaded_wo, 16)
            for h in range(NH):
                last = nc.tensor.matmul(banks[3][0:lw, 0:D], sink_l[:, h * lw:(h + 1) * lw], wo[:, h, :],
                                        start=h == 0, stop=h == NH - 1)
            last.then_inc(sink_ready, 1)
            pe.wait_ge(entries_done, 1)
            pe.wait_ge(loaded_const, 16 * 8)
            for k in range(KD):
                last = nc.tensor.transpose(banks[0][:, k * P:(k + 1) * P], entry[:, k * P:(k + 1) * P], ident[:, :])
            last.then_inc(entry_turned, 1)
            pe.wait_ge(entryT_copied, 1)
            pe.wait_ge(loaded_entry_w, 16 * 4)
            pe.wait_ge(gram_copied, 1)
            for k in range(KD):
                last = nc.tensor.matmul(banks[2][:, 0:P], wv6[:, k, :], entryT[:, k, :], start=k == 0, stop=k == KD - 1)
            last.then_inc(cv_raw, 1)
            for k in range(KD):
                last = nc.tensor.matmul(banks[1][:, 0:HD], entryT[:, k, :], wk6[:, k, :], start=k == 0, stop=k == KD - 1)
            last.then_inc(ck_raw, 1)
            pe.wait_ge(cvT_done, 1)
            for i in range(NH // 2):
                if CW_BANKS[i] == 1:
                    pe.wait_ge(ck_sumsq, 1)
                if CW_BANKS[i] in CW_BANKS[:i]:
                    pe.wait_ge(cw_copied, CW_BANKS.index(CW_BANKS[i]) + 1)
                nc.tensor.matmul(banks[CW_BANKS[i]][:, :], cvT, wo[:, 2 * i:2 * i + 2, :], start=True, stop=True).then_inc(cw_ready, 1)
            pe.wait_ge(sink_rows_done, 1)
            pe.wait_ge(ck_ready, 1)
            nc.tensor.transpose(banks[3][:, D:D + P], ck_rot, ident[:, :]).then_inc(ck_turned, 1)


def attention(nc, a, scratch, mem, banks):
    cursor = [0]

    def carve(n):
        cursor[0] += n
        return mem["arena"][:, cursor[0] - n:cursor[0]]

    qk_b = carve(2 * GW)
    squares = carve(2 * GW)
    rot = [carve(2 * GW), carve(2 * GW)]
    rot_part = carve(2 * G * ROT)
    qT = carve(GW)
    v_sb = [carve(GW) for _ in range(ST)]
    ctxT = carve(GW)
    shifted = heads(carve(G * NK), G)
    e_sb = heads(carve(G * NK), G)
    p_loc = carve(G * S)
    p_comp = carve(PC + NH)
    pcT = carve(P)
    cw_t = carve(D)
    x_t = carve(D).rearrange("p (k n) -> p k n", k=KD)
    x_res = carve(D)
    h_sb = carve(D)
    assert cursor[0] <= KEPT0
    cursor[0] = KEPT0
    pT = carve(GW).rearrange("p (h q) -> p h q", h=G)
    kT = [carve(G * 2 * NK).rearrange("p (h b k) -> p h b k", h=G, b=2) for _ in range(ST)]
    sinkT = carve(P)
    w_split, wo, x1, ident = mem["w_split"], mem["wo"], mem["x1"], mem["ident"]
    x_hi, x_lo = mem["x_parts"][:, 0], mem["x_parts"][:, 1]
    stats = mem["stats"]
    neg_half = stats[:, 0:8]
    ss, inv = stats[:, 8:16], stats[:, 16:24]
    mx, sums, rsums = stats[:, 24:32], stats[:, 32:40], stats[:, 40:48]
    bn, mv, rstd, var_eps = stats[:, 48:54], stats[:, 54:56], stats[:, 56:57], stats[:, 57:58]
    ms = stats[:, 64:72]
    rms_eps, ln_eps = stats[:, 104:112], stats[:, 112:113]
    bank_q, bank_k, bank_v, bank_t0, bank_t1, bank_s, bank_p, bank_o = banks

    with ExitStack() as ctx:
        def sem(name):
            return ctx.enter_context(nc.semaphore(name))

        q_proj, k_proj, v_proj = sem("q_proj"), sem("k_proj"), sem("v_proj")
        q_biased, k_biased, v_copied = sem("q_biased"), sem("k_biased"), sem("v_copied")
        squared, summed_sq, ms_ready, inv_ready = sem("squared"), sem("summed_sq"), sem("ms_ready"), sem("inv_ready")
        cos_part, sin_part, rotated, normed = sem("cos_part"), sem("sin_part"), sem("rotated"), sem("normed")
        q_turned, k_turned, qT_copied, kT_copied = sem("q_turned"), sem("k_turned"), sem("qT_copied"), sem("kT_copied")
        ck_placed, scored, maxed, s_shifted = sem("ck_placed"), sem("scored"), sem("maxed"), sem("s_shifted")
        exped, e_summed, e_recip, probs = sem("exped"), sem("e_summed"), sem("e_recip"), sem("probs")
        p_turned, pT_copied, ctx_ready, ctx_copied = sem("p_turned"), sem("pT_copied"), sem("ctx_ready"), sem("ctx_copied")
        x_loaded, res_loaded, cw_loaded = sem("x_loaded"), sem("res_loaded"), sem("cw_loaded")
        x_high, x_split = sem("x_high"), sem("x_split")
        pc_turned, pcT_copied, o_ready = sem("pc_turned"), sem("pcT_copied"), sem("o_ready")
        h_summed, h_stats, h_mv, rstd_ready, x1_ready = sem("h_summed"), sem("h_stats"), sem("h_mv"), sem("rstd_ready"), sem("x1_ready")
        var_ready = sem("var_ready")
        zeroed, sinks_placed = sem("zeroed"), sem("sinks_placed")
        bias_loaded = [sem("bias_loaded_first"), sem("bias_loaded_rest")]
        block = ctx.enter_context(nc.Block())

        def has(s0, g, lag):
            return not isinstance(s0, int) or 0 <= s0 + g - lag < STEPS

        def tiles(eng, tile):
            tile(0, 0)
            tile(1, ST)
            with eng.Fori(2, TILES) as t:
                tile(t, t * ST)
            tile(TILES, STEPS)

        @block.sync
        def _(sp):
            xT = a["xT"].rearrange("(k p) (t n) -> t p k n", p=P, n=P)
            xr = a["x"].rearrange("(t p) d -> t p d", p=P)
            cwr = scratch.rearrange("(t r) n -> t r n", r=P)

            def at(view, t):
                return view[t] if isinstance(t, int) else view[bass.ds(t, 1)][0]

            def tokens(t):
                wait(sp, x_split, t - 1)
                sp.dma_start(x_t, at(xT, t)).then_inc(x_loaded, 16)

            def rest(t):
                wait(sp, h_summed, t)
                sp.dma_start(x_res, at(xr, t)).then_inc(res_loaded, 16)
                wait(sp, o_ready, t)
                sp.dma_start(cw_t, at(cwr, t)).then_inc(cw_loaded, 16)

            for g in range(ST):
                for i, name in enumerate(("bq", "blk")):
                    sp.dma_start(mem["qk_bias"][:, i, g * GW:(g + 1) * GW],
                                 a[name][:, g * GW:(g + 1) * GW].partition_broadcast(P)).then_inc(bias_loaded[min(g, 1)], 16)
            tokens(1)
            sp.wait_ge(mem["cw_stored"], 16 * 2 * NC)
            rest(0)
            with sp.Fori(1, TILES - 1) as t:
                tokens(t + 1)
                rest(t)
            rest(TILES - 1)

        @block.tensor
        def _(pe):
            def tile(t, s0):
                for g in range(ST):
                    s = s0 + g
                    if has(s0, g, 2):
                        wait(pe, normed, s - 1)
                        wait(pe, ctx_copied, s - 3)
                        wait(pe, kT_copied, s - 2)
                        src = rot[g % 2]
                        for j in range(G):
                            last = nc.tensor.transpose(bank_t0[:, j * P:(j + 1) * P], src[:, j * HD:(j + 1) * HD], ident[:, :])
                        last.then_inc(q_turned, 1)
                        for j in range(G):
                            last = nc.tensor.transpose(bank_t1[:, j * P:(j + 1) * P],
                                                       src[:, GW + j * HD:GW + (j + 1) * HD], ident[:, :])
                        last.then_inc(k_turned, 1)
                    if has(s0, g, 3):
                        wait(pe, probs, s - 2)
                        wait(pe, pT_copied, s - 3)
                        if g == 3:
                            wait(pe, pcT_copied, t)
                        for j in range(0, G, 2):
                            last = nc.tensor.transpose(bank_p[:, j * S:j * S + P], p_loc[:, j * S:j * S + P], ident[:, :])
                        last.then_inc(p_turned, 1)
                        if g == 2:
                            nc.tensor.transpose(bank_p[0:PC + NH, 256:256 + P], p_comp, ident[:, :]).then_inc(pc_turned, 1)
                    if has(s0, g, 4):
                        wait(pe, ctx_copied, s - 3)
                        if g == 0:
                            wait(pe, h_summed, t - 1)
                        for j in range(G):
                            nc.tensor.matmul(bank_o[:, 0:D], ctxT[:, j * P:(j + 1) * P], wo[:, g * G + j, :],
                                             start=g == 0 and j == 0, stop=False)
                        if g == ST - 1:
                            wait(pe, pcT_copied, t)
                            wait(pe, cw_loaded, t * 16)
                            nc.tensor.matmul(bank_o[:, 0:D], pcT, cw_t, start=False, stop=False)
                            nc.tensor.matmul(bank_o[:, 0:D], sinkT[SINK0:SINK0 + SINKS, :],
                                             mem["sink_rows"][SINK0:SINK0 + SINKS, :], start=False,
                                             stop=True).then_inc(o_ready, 1)
                    if has(s0, g, 2):
                        wait(pe, s_shifted, s - 2)
                        wait(pe, kT_copied, s - 1)
                        wait(pe, qT_copied, s - 1)
                        wait(pe, ck_placed, s - 1)
                        for b in range(2):
                            rows = slice(b * S, (b + 1) * S)
                            for j in range(G):
                                nc.tensor.matmul(bank_s[rows, j * NK:(j + 1) * NK], qT[:, j * P + b * S:j * P + (b + 1) * S],
                                                 kT[(g + 2) % ST][:, j, b, :], start=j == 0, stop=False)
                        nc.tensor.matmul(bank_s[:, 0:G * NK], mem["identb"][:, :], mem["maskb"][:, :],
                                         start=False, stop=True).then_inc(scored, 1)
                    if has(s0, g, 3):
                        wait(pe, pT_copied, s - 2)
                        wait(pe, v_copied, s - 2)
                        wait(pe, qT_copied, min(s - 1, STEPS) if isinstance(s, int) else s - 1)
                        for j in range(G):
                            last = nc.tensor.matmul(bank_t0[:, j * P:(j + 1) * P], v_sb[(g + 1) % ST][:, j * HD:(j + 1) * HD],
                                                    pT[:, j, :], start=True, stop=True)
                        last.then_inc(ctx_ready, 1)
                    if has(s0, g, 0):
                        if g == 0:
                            wait(pe, x_split, t)
                        for i, (bk, free, done) in enumerate(((bank_q, q_biased, q_proj), (bank_k, k_biased, k_proj),
                                                              (bank_v, v_copied, v_proj))):
                            wait(pe, free, s)
                            n = 0
                            for k in range(KD):
                                for xs, part in ((x_hi, 0), (x_lo, 0), (x_hi, 1)):
                                    last = nc.tensor.matmul(bk[:, :], xs[:, k, :], w_split[:, i, part, k, g * GW:(g + 1) * GW],
                                                            start=n == 0, stop=n == 5)
                                    n += 1
                            last.then_inc(done, 1)
            tiles(pe, tile)

        @block.scalar
        def _(act):
            def tile(t, s0):
                for g in range(ST):
                    s = s0 + g
                    if has(s0, g, 2):
                        wait(act, q_turned, s - 1)
                        wait(act, scored, s - 2)
                        nc.scalar.activation(qT, bank_t0[:, :], ACT.Copy).then_inc(qT_copied, 1)
                        wait(act, k_turned, s - 1)
                        nc.scalar.activation(kT[(g + 2) % ST][:, :, :, 0:S],
                                             bank_t1[:, :].rearrange("p (h b k) -> p h b k", h=G, b=2),
                                             ACT.Copy).then_inc(kT_copied, 1)
                    if has(s0, g, 3):
                        wait(act, p_turned, s - 2)
                        if g == 2:
                            wait(act, pc_turned, t)
                        wait(act, ctx_ready, s - 3)
                        if isinstance(t, int) and t == 0 and g == 3:
                            act.wait_ge(zeroed, 5)
                        src = bank_p[:, 0:256].rearrange("p (a q) -> p a q", a=2)
                        for hj in range(2):
                            for b in range(2):
                                last = nc.scalar.activation(pT[b * S:(b + 1) * S, hj::2, b * S:(b + 1) * S],
                                                            src[hj * S:(hj + 1) * S, :, b * S:(b + 1) * S], ACT.Copy)
                        last.then_inc(pT_copied, 1)
                        if g == 2:
                            wait(act, o_ready, t - 1)
                            for b in range(2):
                                nc.scalar.activation(pcT[b * PC:(b + 1) * PC, b * S:(b + 1) * S],
                                                     bank_p[0:PC, 256 + b * S:256 + (b + 1) * S], ACT.Copy)
                            nc.scalar.activation(sinkT[SINK0:SINK0 + NH, :], bank_p[PC:PC + NH, 256:256 + P],
                                                 ACT.Copy).then_inc(pcT_copied, 1)
                    if has(s0, g, 2):
                        wait(act, s_shifted, s - 1)
                        nc.scalar.activation(e_sb, shifted, ACT.Exp, scale=SCALE).then_inc(exped, 1)
                    if has(s0, g, 3):
                        wait(act, ctx_ready, s - 2)
                        nc.scalar.activation(ctxT, bank_t0[:, :], ACT.Copy, scale=0.5).then_inc(ctx_copied, 1)
                    if has(s0, g, 0):
                        wait(act, q_biased, s + 1)
                        wait(act, k_biased, s + 1)
                        wait(act, summed_sq, s)
                        nc.scalar.activation(squares, qk_b, ACT.Square).then_inc(squared, 1)
                        wait(act, v_proj, s + 1)
                        nc.scalar.activation(v_sb[g], bank_v[:, :], ACT.Copy).then_inc(v_copied, 1)
            tiles(act, tile)

        @block.vector
        def _(dve):
            nc.vector.memset(pT, 0.0).then_inc(zeroed, 1)
            nc.vector.memset(pcT, 0.0).then_inc(zeroed, 1)
            nc.vector.memset(sinkT[SINK0:P, :], 1.0).then_inc(zeroed, 1)
            def split(t):
                wait(dve, x_loaded, t * 16)
                wait(dve, v_proj, t * ST)
                nc.vector.tensor_copy(x_hi, x_t).then_inc(x_high, 1)
                wait(dve, x_high, t)
                nc.vector.tensor_tensor(x_lo, x_t, x_hi.bitcast(F32), ALU.subtract).then_inc(x_split, 1)

            def tile(t, s0):
                for g in range(ST):
                    s = s0 + g
                    if g == 0 and has(s0, 0, 0) and not (isinstance(t, int) and t == 0):
                        split(t)
                    if has(s0, g, 1):
                        wait(dve, squared, s)
                        wait(dve, ms_ready, s - 1)
                        nc.vector.tensor_reduce(ss, heads(squares, 2 * G), AX_X, ALU.add).then_inc(summed_sq, 1)
                        r = rot[(g + 1) % 2]
                        wait(dve, k_turned, s - 2)
                        nc.vector.tensor_tensor(
                            r.rearrange("p (i h d) -> p i h d", i=2, h=G), qk_b.rearrange("p (i h d) -> p i h d", i=2, h=G),
                            mem["rot_c"][:, :, :].unsqueeze(2).to_broadcast([P, 2, G, HD]), ALU.mult).then_inc(cos_part, 1)
                        wait(dve, cos_part, s)
                        wait(dve, sin_part, s)
                        rr = heads(r, 2 * G)[:, :, 0:ROT]
                        nc.vector.tensor_tensor(rr, rr, heads(rot_part, 2 * G), ALU.add).then_inc(rotated, 1)
                    if g == ST - 1 and has(s0, 0, ST):
                        wait(dve, o_ready, t)
                        wait(dve, res_loaded, t * 16)
                        nc.vector.tensor_tensor(h_sb, bank_o[:, 0:D], x_res, ALU.add).then_inc(h_summed, 1)
                        wait(dve, h_summed, t)
                        nc.vector.bn_stats(bn, h_sb).then_inc(h_stats, 1)
                        wait(dve, h_stats, t)
                        carry(nc, stats)
                        nc.vector.bn_aggr(mv, bn).then_inc(h_mv, 1)
                    if has(s0, g, 2):
                        sc = heads(bank_s[:, 0:G * NK], G)
                        wait(dve, scored, s - 1)
                        wait(dve, exped, s - 2)
                        nc.vector.tensor_reduce(mx[:, 0:G], sc[:, :, 0:S], AX_X, ALU.max)
                        nc.vector.tensor_reduce(mx[:, G:2 * G], sc[:, :, S:NK], AX_X, ALU.max).then_inc(maxed, 1)
                        wait(dve, maxed, s - 1)
                        nc.vector.tensor_tensor(shifted[:, :, 0:S], sc[:, :, 0:S], over(mx[:, 0:G], S), ALU.subtract)
                        nc.vector.tensor_tensor(shifted[:, :, S:NK], sc[:, :, S:NK], over(mx[:, G:2 * G], NC + 1),
                                                ALU.subtract).then_inc(s_shifted, 1)
                    if has(s0, g, 0):
                        if isinstance(t, int) and t == 0 and g < 2:
                            dve.wait_ge(bias_loaded[g], 32 if g == 0 else 32 * (ST - 1))
                        wait(dve, squared, s)
                        wait(dve, sin_part, s)
                        wait(dve, q_proj, s + 1)
                        nc.vector.tensor_tensor(qk_b[:, 0:GW], bank_q[:, :], mem["qk_bias"][:, 0, g * GW:(g + 1) * GW],
                                                ALU.add).then_inc(q_biased, 1)
                        wait(dve, k_proj, s + 1)
                        nc.vector.tensor_tensor(qk_b[:, GW:2 * GW], bank_k[:, :], mem["qk_bias"][:, 1, g * GW:(g + 1) * GW],
                                                ALU.add).then_inc(k_biased, 1)
                    if has(s0, g, 2):
                        gg = (g + 2) % ST
                        wait(dve, exped, s - 1)
                        nc.vector.tensor_reduce(sums[:, 0:G], e_sb[:, :, 0:S], AX_X, ALU.add)
                        nc.vector.tensor_reduce(sums[:, G:2 * G], e_sb[:, :, S:NK], AX_X, ALU.add).then_inc(e_summed, 1)
                        wait(dve, e_summed, s - 1)
                        nc.vector.reciprocal(rsums, sums).then_inc(e_recip, 1)
                        wait(dve, e_recip, s - 1)
                        wait(dve, p_turned, s - 2)
                        nc.vector.tensor_tensor(heads(p_loc, G), e_sb[:, :, 0:S], over(rsums[:, 0:G], S), ALU.mult)
                        if gg == 0:
                            wait(dve, pc_turned, t)
                        nc.vector.tensor_tensor(p_comp[:, gg * G * NC:(gg + 1) * G * NC].rearrange("p (h c) -> p h c", h=G),
                                                e_sb[:, :, S:S + NC], over(rsums[:, G:2 * G], NC), ALU.mult)
                        nc.vector.tensor_tensor(p_comp[:, PC + gg * G:PC + (gg + 1) * G].unsqueeze(2), e_sb[:, :, NK - 1:NK],
                                                rsums[:, G:2 * G].unsqueeze(2), ALU.mult).then_inc(probs, 1)
                    if g == ST - 1 and has(s0, 0, ST):
                        wait(dve, rstd_ready, t)
                        dst = x1[:, t - 1, :] if isinstance(t, int) else x1[:, bass.ds(t - 1, 1), :].squeeze(1)
                        nc.vector.tensor_scalar(dst, h_sb, mv[:, 0:1], rstd, ALU.subtract, ALU.mult).then_inc(x1_ready, 1)

            tiles(dve, tile)
            wait(dve, x1_ready, TILES)

        @block.gpsimd
        def _(pool):
            pool.dma_start(ctx_sink := p_comp[:, 0:NH], a["sink_kT"]).then_inc(sinks_placed, 16)
            pool.wait_ge(sinks_placed, 16)
            for k in range(ST):
                for b in range(2):
                    nc.gpsimd.tensor_copy(kT[k][:, :, b, NK - 1:NK], ctx_sink[:, k * G:(k + 1) * G].unsqueeze(2)).then_inc(zeroed, 1)

            def tile(t, s0):
                for g in range(ST):
                    s = s0 + g
                    if has(s0, g, 1):
                        wait(pool, scored, s - ST)
                        wait(pool, q_biased, s)
                        wait(pool, k_biased, s)
                        wait(pool, rotated, s - 1)
                        src = qk_b.rearrange("p (i h d) -> p i h d", i=2, h=G)
                        part = rot_part.rearrange("p (i h d) -> p i h d", i=2, h=G)
                        for i in range(2):
                            last = nc.gpsimd.tensor_tensor(
                                halves(part[:, i]), halves(src[:, i, :, 0:ROT])[:, :, ::-1, :],
                                mem["rot_s"][:, i, :].rearrange("p (a b) -> p a b", a=2).unsqueeze(1)
                                .to_broadcast([P, G, 2, HALF]), ALU.mult)
                        last.then_inc(sin_part, 1)
                        wait(pool, inv_ready, s - 1)
                        wait(pool, summed_sq, s)
                        nc.gpsimd.tensor_tensor(ms, ss, rms_eps, ALU.add).then_inc(ms_ready, 1)
                        wait(pool, ms_ready, s)
                        wait(pool, normed, s - 1)
                        nc.gpsimd.tensor_tensor(inv, ms, neg_half, ALU.pow).then_inc(inv_ready, 1)
                        wait(pool, inv_ready, s)
                        wait(pool, rotated, s)
                        r = heads(rot[(g + 1) % 2], 2 * G)
                        nc.gpsimd.tensor_tensor(r, r, over(inv, HD), ALU.mult).then_inc(normed, 1)
                    if g == ST - 1 and has(s0, 0, ST):
                        rsqrt_var(t - 1)
                    if has(s0, g, 1):
                        gg = (g + ST - 1) % ST
                        tt = t if g else t - 1
                        src = (ckT_at(tt)).rearrange("p (b c) -> p b c", b=2)
                        for j in range(G):
                            last = nc.gpsimd.tensor_copy(kT[gg][:, j, :, S:S + NC], src)
                        last.then_inc(ck_placed, 1)

            def ckT_at(t):
                return mem["ckT"][:, t * 2 * NC:(t + 1) * 2 * NC] if isinstance(t, int) else mem["ckT"][:, bass.ds(t * (2 * NC), 2 * NC)]

            def rsqrt_var(t):
                wait(pool, h_mv, t + 1)
                nc.gpsimd.tensor_tensor(var_eps, mv[:, 1:2], ln_eps, ALU.add).then_inc(var_ready, 1)
                wait(pool, var_ready, t + 1)
                nc.gpsimd.tensor_tensor(rstd, var_eps, neg_half[:, 0:1], ALU.pow).then_inc(rstd_ready, 1)

            tiles(pool, tile)


def mixing(nc, a, mem, psum):
    arena, x1, ident, stats = mem["arena"], mem["x1"], mem["ident"], mem["stats"]
    v_all = arena[:, 0:TILES * D].rearrange("p (t d) -> p t d", t=TILES)
    w_all = arena[:, TILES * D:2 * TILES * D].rearrange("p (t d) -> p t d", t=TILES)
    low = arena[:, 2 * TILES * D:ARENA]
    mixT = low[:, 0:RH * P].rearrange("p (h q) -> p h q", h=RH)
    cursor = [RH * P]

    def carve(n):
        cursor[0] += n
        assert cursor[0] <= ARENA - 2 * TILES * D
        return low[:, cursor[0] - n:cursor[0]]

    xg = [carve(2 * D) for _ in range(2)]
    cT = [carve(D).rearrange("p (h n) -> p h n", h=RH) for _ in range(2)]
    xs = [carve(D) for _ in range(2)]
    gram, wh, wg = mem["gram"], mem["wh"], mem["wg"]
    decay = carve(RH * S)
    mix = carve(RH * S)
    zero = carve(P).bitcast(BF16)
    assert cursor[0] <= FFN_KEPT0
    raw = mem["qk_bias"][:, :, :].rearrange("p i n -> p (i n)")[:, 0:KD * FALL].rearrange("p (k n) -> p k n", k=KD)
    wd_raw = mem["wo"][:, :, :]
    gu, wd = ffn_weights(mem)
    select = mem["select"]
    sel_raw = w_all[0:PARTS * NE, 10:TILES, :].rearrange("p t d -> p (t d)")[:, 0:ET * P]
    wo_w, gamma, beta, wr, before = ffn_small(mem)
    b_xg = [psum[:, i * 512:(i + 1) * 512] for i in range(2)]
    b_v = [psum[:, (2 + i) * 512:(2 + i) * 512 + D] for i in range(2)]
    b_w = [psum[:, (4 + i) * 512:(4 + i) * 512 + D] for i in range(2)]
    b_s = psum[:, 6 * 512:7 * 512]
    b_t = psum[:, 7 * 512:8 * 512]

    with ExitStack() as ctx:
        def sem(name):
            return ctx.enter_context(nc.semaphore(name))

        cT_loaded = [sem(f"cT_loaded{i}") for i in range(2)]
        staged, xg_ready, v_ready, xg_copied, v_stored = sem("staged"), sem("xg_ready"), sem("v_ready"), sem("xg_copied"), sem("v_stored")
        w_ready, w_stored, s_added = sem("w_ready"), sem("w_stored"), sem("s_added")
        decay_loaded, zeroed, sel_loaded, sel_ready = sem("decay_loaded"), sem("mix_zeroed"), sem("sel_loaded"), sem("sel_ready")
        s_closed, decayed, mix_ready, mix_turned, mix_placed = sem("s_closed"), sem("decayed"), sem("mix_ready"), sem("mix_turned"), sem("mix_placed")
        raw_loaded, ffn_hi, ffn_lo, wd_loaded = sem("raw_loaded"), sem("ffn_hi"), sem("ffn_lo"), sem("wd_loaded")
        wd_hi_ready, small_loaded = sem("wd_hi_ready"), sem("small_loaded")
        block = ctx.enter_context(nc.Block())

        def pairs(eng, tile, piece=lambda which, k, n: None):
            for t in range(4):
                tile(t, t % 2)
            for first, which in ((2, 0), (4, None), (6, 1)):
                with eng.Fori(first, first + KD) as pair:
                    tile(pair * 2, 0)
                    tile(pair * 2 + 1, 1)
                    if which is not None:
                        piece(which, pair - first, pair - first + (which * KD + 1))
            tile(TILES, 0)

        def new(t):
            return not isinstance(t, int) or t < TILES

        def lag(t):
            return not isinstance(t, int) or t > 0

        def at(view, t):
            return view[:, t, :] if isinstance(t, int) else view[:, bass.ds(t, 1), :].squeeze(1)

        def one_of(view, k):
            return view[:, bass.ds(k, 1), :].squeeze(1)

        @block.sync
        def _(sp):
            cTv = a["ctxT"].rearrange("(h p) (t n) -> t p h n", p=P, n=P)
            for i in range(2):
                sp.dma_start(cT[i], cTv[i]).then_inc(cT_loaded[i], 16)

            def load(pair):
                for i in range(2):
                    sp.wait_ge(v_ready, pair * 2 + (i - 1))
                    sp.dma_start(cT[i], (cTv[pair * 2 + i] if isinstance(pair, int) else cTv[bass.ds(pair * 2 + i, 1)][0])
                                 ).then_inc(cT_loaded[i], 16)
            sp.dma_start(sel_raw, a["select"]).then_inc(sel_loaded, 16)
            load(1)
            for k in range(KD):
                sp.dma_start(raw[:, k, :], a["gateT"][k * P:(k + 1) * P, :]).then_inc(raw_loaded, 16)
            load(2)
            sp.dma_start(wd_raw[:, 0:FT - 1, :], a["down"][0:(FT - 1) * P, :].rearrange("(f p) n -> p f n", p=P)).then_inc(wd_loaded, 16)
            sp.dma_start(wd_raw[0:rows(FT - 1), FT - 1, :], a["down"][(FT - 1) * P:FALL, :]).then_inc(wd_loaded, 16)
            load(3)
            sp.dma_start(decay[0:S, :], a["decay"]).then_inc(decay_loaded, 16)
            for dst, src in ((wo_w, a["wo_w"].rearrange("(k p) n -> p k n", p=P)), (gamma, a["gn_gamma"].partition_broadcast(P)),
                             (beta, a["gn_beta"].partition_broadcast(P)), (wr, a["WrT"].rearrange("(k p) e -> p k e", p=P)),
                             (before, a["before"].partition_broadcast(P))):
                sp.dma_start(dst, src).then_inc(small_loaded, 16)
            load(4)
            sp.wait_ge(ffn_lo, KD)
            for k in range(KD):
                sp.dma_start(raw[:, k, :], a["upT"][k * P:(k + 1) * P, :]).then_inc(raw_loaded, 16)
            with sp.Fori(5, TILES // 2) as pair:
                load(pair)
            sp.wait_ge(small_loaded, 16 * 5)

        @block.tensor
        def _(pe):
            pe.wait_ge(mem["wg_loaded"], 32)
            pe.wait_ge(zeroed, 2)
            nc.tensor.matmul(b_s[0:S, 0:RH * S], zero[:, 0:S], zero[:, 0:RH * S], start=True, stop=False)

            def tile(t, i):
                if new(t):
                    wait(pe, staged, t + 1)
                    wait(pe, xg_copied, t - 1)
                    wait(pe, cT_loaded[i], 8 * (t - i) + 16)
                    for k in range(KD):
                        nc.tensor.transpose(b_xg[i][:, k * P:(k + 1) * P], xs[i][:, k * P:(k + 1) * P], ident[:, :])
                    for h in range(RH):
                        last = nc.tensor.matmul(b_xg[i][:, D + h * P:D + (h + 1) * P], gram[:, h, :], cT[i][:, h, :],
                                                start=True, stop=True)
                    last.then_inc(xg_ready, 1)
                    wait(pe, v_stored, t - 1)
                    for h in range(RH):
                        last = nc.tensor.matmul(b_v[i][:, h * HD:(h + 1) * HD], cT[i][:, h, :], wh[:, h, :],
                                                start=True, stop=True)
                    last.then_inc(v_ready, 1)
                if lag(t):
                    j = 1 - i
                    wait(pe, xg_copied, t)
                    wait(pe, w_stored, t - 2)
                    for k in range(KD):
                        last = nc.tensor.matmul(b_w[j], xg[j][:, k * P:(k + 1) * P], wg[:, k, :], start=k == 0, stop=k == KD - 1)
                    last.then_inc(w_ready, 1)
                    for b in range(2):
                        for h in range(RH):
                            c = h * P + b * S
                            last = nc.tensor.matmul(b_s[0:S, h * S:(h + 1) * S], xg[j][:, c:c + S], xg[j][:, D + c:D + c + S],
                                                    start=False, stop=False)
                    last.then_inc(s_added, 1)
            pairs(pe, tile)
            nc.tensor.matmul(b_s[0:S, 0:RH * S], zero[:, 0:S], zero[:, 0:RH * S], start=False, stop=True).then_inc(s_closed, 1)
            pe.wait_ge(mix_ready, 1)
            nc.tensor.transpose(b_t[:, 0:S], mix[0:S, :], ident[0:S, 0:S]).then_inc(mix_turned, 1)

        @block.scalar
        def _(act):
            def tile(t, i):
                if new(t):
                    wait(act, xg_ready, t - 1)
                    nc.scalar.activation(xs[i], at(x1, t), ACT.Copy).then_inc(staged, 1)
                    wait(act, xg_ready, t + 1)
                    wait(act, s_added, t - 1)
                    nc.scalar.activation(xg[i], b_xg[i], ACT.Copy).then_inc(xg_copied, 1)

            def piece(which, k, n):
                act.wait_ge(raw_loaded, 16 * KD * (which + 1))
                nc.scalar.activation(one_of(gu[:, which, 0], k), one_of(raw, k), ACT.Copy).then_inc(ffn_hi, 1)
            pairs(act, tile, piece)
            act.wait_ge(mix_turned, 1)
            for h in range(RH):
                for b in range(2):
                    last = nc.scalar.activation(mixT[b * S:(b + 1) * S, h, b * S:(b + 1) * S], b_t[h * S:(h + 1) * S, 0:S], ACT.Copy)
            last.then_inc(mix_placed, 1)
            act.wait_ge(mix_placed, 1)

        @block.vector
        def _(dve):
            nc.vector.memset(mixT, 0.0).then_inc(zeroed, 1)
            nc.vector.memset(zero, 0.0).then_inc(zeroed, 1)

            def tile(t, i):
                if new(t):
                    wait(dve, v_ready, t + 1)
                    nc.vector.tensor_copy(at(v_all, t), b_v[i]).then_inc(v_stored, 1)
                if lag(t):
                    wait(dve, w_ready, t)
                    if isinstance(t, int) and t == 3:
                        dve.wait_ge(sel_ready, 1)
                    nc.vector.tensor_scalar(at(w_all, t - 1), b_w[1 - i], 0.0, None, ALU.max).then_inc(w_stored, 1)

            def piece(which, k, n):
                dve.wait_ge(ffn_hi, n)
                nc.vector.tensor_tensor(one_of(gu[:, which, 1], k), one_of(raw, k), one_of(gu[:, which, 0], k).bitcast(F32),
                                        ALU.subtract).then_inc(ffn_lo, 1)
            pairs(dve, tile, piece)
            dve.wait_ge(s_closed, 1)
            dve.wait_ge(decay_loaded, 16)
            nc.vector.tensor_tensor(mix[0:S, :], b_s[0:S, 0:RH * S], decay[0:S, :], ALU.mult).then_inc(decayed, 1)
            dve.wait_ge(decayed, 1)
            nc.vector.scalar_tensor_tensor(out=mix[0:S, :], in0=mix[0:S, :], scalar=-1.0, in1=mix[0:S, :], op0=ALU.mult,
                                           op1=ALU.max).then_inc(decayed, 1)
            dve.wait_ge(decayed, 2)
            nc.vector.tensor_scalar(mix[0:S, :], mix[0:S, :], 1.0, None, ALU.max).then_inc(mix_ready, 1)
            dve.wait_ge(v_stored, TILES)
            dve.wait_ge(w_stored, TILES)

        @block.gpsimd
        def _(pool):
            pool.wait_ge(sel_loaded, 16)
            nc.gpsimd.tensor_copy(select[0:PARTS * NE, :], sel_raw).then_inc(sel_ready, 1)
            pool.wait_ge(wd_loaded, 32)
            full, last = (slice(0, P), slice(0, FT - 1)), (slice(0, rows(FT - 1)), slice(FT - 1, FT))
            for n, (p, f) in enumerate((full, last)):
                nc.gpsimd.tensor_copy(wd[p, 0, f], wd_raw[p, f]).then_inc(wd_hi_ready, 1)
                pool.wait_ge(wd_hi_ready, n + 1)
                nc.gpsimd.tensor_tensor(wd[p, 1, f], wd_raw[p, f], wd[p, 0, f].bitcast(F32), ALU.subtract)


FFN_KEPT0 = 3328


def ffn_weights(mem):
    flat = mem["w_split"][:, :, :, :, :].rearrange("p i j k n -> p (i j k n)")
    return (flat[:, 0:4 * KD * FALL].rearrange("p (i j k n) -> p i j k n", i=2, j=2, k=KD),
            flat[:, 4 * KD * FALL:4 * KD * FALL + 2 * FT * D].rearrange("p (j f n) -> p j f n", j=2, f=FT))


def ffn_small(mem):
    flat = mem["arena"][:, 2 * TILES * D + FFN_KEPT0:ARENA]
    return (flat[:, 0:KD * D].rearrange("p (k n) -> p k n", k=KD), flat[:, 2 * D:3 * D], flat[:, 3 * D:4 * D],
            mem["ckT"][:, 0:KD * NE].rearrange("p (k e) -> p k e", k=KD),
            mem["rot_c"][:, 0, 0:NE * NE].rearrange("p (e j) -> p e j", e=NE))


def feed_forward(nc, a, mem, psum, out):
    arena, x1, ident, stats = mem["arena"], mem["x1"], mem["ident"], mem["stats"]
    v_all = arena[:, 0:TILES * D].rearrange("p (t d) -> p t d", t=TILES)
    w_all = arena[:, TILES * D:2 * TILES * D].rearrange("p (t d) -> p t d", t=TILES)
    low = arena[:, 2 * TILES * D:ARENA]
    mixT = low[:, 0:RH * P].rearrange("p (h q) -> p h q", h=RH)
    cursor = [RH * P]

    def carve(n):
        cursor[0] += n
        assert cursor[0] <= ARENA - 2 * TILES * D
        return low[:, cursor[0] - n:cursor[0]]

    x2n = carve(CH * D)
    sil = carve(CT)
    hid = [carve(CT) for _ in range(2)]
    rank = [carve(CH * NE * NE) for _ in range(2)]
    assert cursor[0] <= FFN_KEPT0
    wo_w, gamma, beta, wr, before = ffn_small(mem)
    flat = mem["qk_bias"][:, :, :].rearrange("p i n -> p (i n)")
    y = flat[:, 0:CH * D]
    turned = flat[:, CH * D:2 * CH * D]
    h3 = flat[:, 2 * CH * D:3 * CH * D]
    x2c = flat[:, 3 * CH * D:4 * CH * D]
    gu, wd = ffn_weights(mem)
    rflat = mem["w_split"][:, :, :, :, :].rearrange("p i j k n -> p (i j k n)")[:, 4 * KD * FALL + 2 * FT * D:]
    x2_hi = rflat[:, 0:KD * CT].rearrange("p (k n) -> p k n", k=KD)
    x2_lo = rflat[:, KD * CT:2 * KD * CT].rearrange("p (k n) -> p k n", k=KD)
    hid_hi = [rflat[:, (2 * KD + i) * CT:(2 * KD + i + 1) * CT] for i in range(2)]
    hid_lo = mem["x_parts"][:, :, :, :].rearrange("p j k n -> p (j k n)")
    select = mem["select"]
    zero = mem["rot_c"][:, 1, 0:64].bitcast(BF16)
    zeros = mem["sink_rows"][:, :].bitcast(BF16)
    score = mem["rot_s"][:, 0, 0:CH * NE].rearrange("p (t e) -> p t e", t=CH)
    ranks = mem["rot_s"][:, 0, 32:32 + CH * NE].rearrange("p (t e) -> p t e", t=CH)
    rest = mem["rot_s"][:, 1, 0:CH * NE].rearrange("p (t e) -> p t e", t=CH)
    parts = mem["maskb"][:, 0:CH * PARTS * NE].rearrange("p (t c e) -> p t c e", t=CH, c=PARTS)
    wT_b = mem["w_parts"][0:PARTS * NE, :]
    smax, ssum, srec = stats[:, 8:12], stats[:, 12:16], stats[:, 16:20]
    bn = [stats[:, 20 + 6 * j:26 + 6 * j] for j in range(CH)]
    mv = stats[:, 44:52].rearrange("p (t c) -> p t c", t=CH)
    ve, rstd = stats[:, 52:56], stats[:, 56:60]
    bn3 = [stats[:, 60 + 6 * j:66 + 6 * j] for j in range(CH)]
    mv3 = stats[:, 84:92].rearrange("p (t c) -> p t c", t=CH)
    ve3, rstd3 = stats[:, 92:96], stats[:, 96:100]
    neg_half = stats[:, 0:CH]
    ln_eps, gn_eps = stats[:, 112:113], stats[:, 113:114]
    b_g, b_u, b_w = [psum[:, i * 512:(i + 1) * 512] for i in range(3)]
    b_acc = psum[:, 3 * 512:5 * 512]
    b_f = psum[:, 5 * 512:7 * 512]
    b_r = psum[:, 7 * 512:8 * 512]

    def tok(ap):
        return ap.rearrange("p (t d) -> p t d", t=CH)

    with ExitStack() as ctx:
        def sem(name):
            return ctx.enter_context(nc.semaphore(name))

        g_ready, u_ready, w_ready = sem("g_ready"), sem("u_ready"), sem("wsel_ready")
        silued, gated, hid_ready, down_done = sem("silued"), sem("gated"), sem("hid_ready"), sem("down_done")
        o_ready, o_stats, o_mv, o_var, o_rstd, o_normed = [sem("f_" + n) for n in ("o_ready", "o_stats", "o_mv", "o_var", "o_rstd", "o_normed")]
        scaled, biased, wy_ready, wy_turned, wyT_copied, mixed = [sem("f_" + n) for n in ("scaled", "biased", "wy_ready", "wy_turned", "wyT_copied", "mixed")]
        h_ready, h_stats, h_mv, h_var, h_rstd, x2_ready = [sem("f_" + n) for n in ("h_ready", "h_stats", "h_mv", "h_var", "h_rstd", "x2_ready")]
        x2_turned, x2T_copied, logits, maxed, less, exped = [sem("f_" + n) for n in ("x2_turned", "x2T_copied", "logits", "maxed", "less", "exped")]
        parts_ready, parts_turned, wT_ready, own = [sem("f_" + n) for n in ("parts_ready", "parts_turned", "wT_ready", "own")]
        high, split, cur_copied = sem("f_high"), sem("f_split"), sem("f_cur_copied")
        acc_ready, h3_ready, h3_stats, h3_mv, h3_var, h3_rstd, y3_ready, stored = [
            sem("t_" + n) for n in ("acc_ready", "h3_ready", "h3_stats", "h3_mv", "h3_var", "h3_rstd", "y3_ready", "stored")]
        zeroed, hid_high, hid_made = sem("f_zeroed"), sem("hid_high"), sem("hid_made")
        block = ctx.enter_context(nc.Block())

        def nothing(i, c):
            pass

        def chunks(eng, front=nothing, slot=lambda c, i: None, turn=lambda f: None, back=nothing):
            for i in range(FT):
                front(i, 0)
            turn(0)

            def both(c):
                for i in range(FT):
                    slot(c, i)
                    front(i, c + 1)
                    if not isinstance(c, int):
                        back(i, c - 1)
                turn(c + 1)
            both(0)
            with eng.Fori(1, CHUNKS - 1) as c:
                both(c)
            for i in range(FT):
                slot(CHUNKS - 1, i)
                back(i, CHUNKS - 2)
            slot(CHUNKS, 0)
            for i in range(FT):
                back(i, CHUNKS - 1)

        def c_past(c, i, lag):
            return not isinstance(c, int) or c > 0 or i >= lag

        def part(view, f):
            return view[:, f * CH:(f + 1) * CH, :] if isinstance(f, int) else view[:, bass.ds(f * CH, CH), :]

        @block.sync
        def _(sp):
            o = out.rearrange("(c t p) d -> c p t d", t=CH, p=P)

            def store(c):
                wait(sp, y3_ready, c + 1)
                dst = o[c] if isinstance(c, int) else o[bass.ds(c, 1)][0]
                sp.dma_start(dst, tok(h3)).then_inc(stored, 16)
            with sp.Fori(0, CHUNKS) as c:
                store(c)
            sp.wait_ge(stored, 16 * CHUNKS)

        @block.tensor
        def _(pe):
            pe.wait_ge(zeroed, 1)

            def front(i, f):
                if i == 0:
                    wait(pe, x2T_copied, f)
                    for h in range(RH):
                        last = nc.tensor.matmul(b_f[:, h * 512:(h + 1) * 512].rearrange("p (t e) -> p t e", t=CH), mixT[:, h, :],
                                                part(v_all, f)[:, :, h * HD:(h + 1) * HD], start=True, stop=True)
                    last.then_inc(o_ready, 1)
                if i == 4:
                    wait(pe, wy_ready, f + 1)
                    wait(pe, o_normed, f + 1)
                    for k in range(KD):
                        for t in range(CH):
                            last = nc.tensor.transpose(b_f[:, k * CT + t * P:k * CT + (t + 1) * P],
                                                       y[:, t * D + k * P:t * D + (k + 1) * P], ident[:, :])
                    last.then_inc(wy_turned, 1)
                if i == 5:
                    wait(pe, wyT_copied, f + 1)
                    for t in range(CH):
                        for k in range(KD):
                            last = nc.tensor.matmul(b_f[:, t * D:(t + 1) * D], turned[:, k * CT + t * P:k * CT + (t + 1) * P],
                                                    wo_w[:, k, :], start=k == 0, stop=k == KD - 1)
                    last.then_inc(mixed, 1)
                if i == 8:
                    wait(pe, x2_ready, f + 1)
                    wait(pe, h_ready, f + 1)
                    for k in range(KD):
                        for t in range(CH):
                            last = nc.tensor.transpose(b_f[:, k * CT + t * P:k * CT + (t + 1) * P],
                                                       x2n[:, t * D + k * P:t * D + (k + 1) * P], ident[:, :])
                    last.then_inc(x2_turned, 1)
                if i == 9:
                    wait(pe, x2T_copied, f + 1)
                    wait(pe, wT_ready, f)
                    for t in range(CH):
                        for k in range(KD):
                            last = nc.tensor.matmul(b_r[:, t * NE:(t + 1) * NE], turned[:, k * CT + t * P:k * CT + (t + 1) * P],
                                                    wr[:, k, :], start=k == 0, stop=k == KD - 1)
                    last.then_inc(logits, 1)
                if i == 12:
                    wait(pe, parts_ready, f + 1)
                    for t in range(CH):
                        last = nc.tensor.transpose(b_rb[0:PARTS * NE, t * P:(t + 1) * P],
                                                   parts[:, t].rearrange("p c e -> p (c e)"), mem["identb"][:, :])
                    last.then_inc(parts_turned, 1)

            b_rb = b_r[:, 0:CT // 2].bitcast(BF16)

            def down(c, i):
                n = rows(i)
                wait(pe, hid_ready, c * FT + (i + 1))
                for t in range(CH):
                    for hs, p in ((hid_hi[i % 2], 0), (hid_lo, 0), (hid_hi[i % 2], 1)):
                        last = nc.tensor.matmul(b_acc[:, t * D:(t + 1) * D], hs[0:n, t * P:(t + 1) * P], wd[0:n, p, i, :],
                                                start=False, stop=False)
                last.then_inc(down_done, 1)

            def close(c):
                down(c, FT - 1)
                for k in range(2):
                    last = nc.tensor.matmul(b_acc[:, k * 512:(k + 1) * 512], zero[:, 0:P], zeros[:, :], start=False, stop=True)
                last.then_inc(acc_ready, 1)

            def slot(c, i):
                if isinstance(c, int) and c == CHUNKS:
                    close(c - 1)
                    return
                n = rows(i)
                cols = slice(i * P, i * P + n)
                if i == 0:
                    wait(pe, split, c + 1)
                for which, bk, free, done in ((0, b_g, silued, g_ready), (1, b_u, gated, u_ready)):
                    wait(pe, free, c * FT + i)
                    m = 0
                    for k in range(KD):
                        for xs, p in ((x2_hi, 0), (x2_lo, 0), (x2_hi, 1)):
                            last = nc.tensor.matmul(bk[0:n, :], gu[:, which, p, k, cols], xs[:, k, :], start=m == 0, stop=m == 5)
                            m += 1
                    last.then_inc(done, 1)
                if i < ET:
                    if i == 0:
                        wait(pe, wT_ready, c + 1)
                    wait(pe, hid_made, c * FT + i)
                    nc.tensor.matmul(b_w[:, :], select[0:PARTS * NE, i * P:(i + 1) * P], wT_b, start=True,
                                     stop=True).then_inc(w_ready, 1)
                if i == 0:
                    if not isinstance(c, int) or c > 0:
                        close(c - 1)
                else:
                    if i == 1:
                        wait(pe, h3_ready, c)
                        for k in range(2):
                            nc.tensor.matmul(b_acc[:, k * 512:(k + 1) * 512], zero[:, 0:P], zeros[:, :], start=True, stop=False)
                    down(c, i - 1)

            chunks(pe, front, slot)

        @block.scalar
        def _(act):
            def front(i, f):
                if i == 4:
                    wait(act, wy_turned, f + 1)
                    wait(act, split, f)
                    nc.scalar.activation(turned, b_f, ACT.Copy).then_inc(wyT_copied, 1)
                if i == 8:
                    wait(act, x2_turned, f + 1)
                    wait(act, mixed, f + 1)
                    nc.scalar.activation(turned, b_f, ACT.Copy).then_inc(x2T_copied, 1)
                if i == 10:
                    wait(act, less, f + 1)
                    nc.scalar.activation(score, score, ACT.Exp).then_inc(exped, 1)

            def slot(c, i):
                if isinstance(c, int) and c == CHUNKS:
                    return
                n = rows(i)
                wait(act, g_ready, c * FT + (i + 1))
                wait(act, gated, c * FT + i)
                nc.scalar.activation(sil[0:n, :], b_g[0:n, :], ACT.Silu).then_inc(silued, 1)
                wait(act, hid_made, c * FT + (i + 1))
                if c_past(c, i, 2):
                    wait(act, down_done, c * FT + (i - 1))
                nc.scalar.activation(hid_hi[i % 2][0:n, :], hid[i % 2][0:n, :], ACT.Copy).then_inc(hid_high, 1)
                if i == 0:
                    wait(act, h3_ready, c)
                    wait(act, x2_ready, c + 1)
                    nc.scalar.activation(x2c, x2n, ACT.Copy).then_inc(cur_copied, 1)

            def turn(f):
                wait(act, u_ready, f * FT)
                wait(act, x2T_copied, f + 1)
                nc.scalar.activation(x2_hi, turned.rearrange("p (k n) -> p k n", k=KD), ACT.Copy).then_inc(high, 1)

            chunks(act, front, slot, turn)

        @block.vector
        def _(dve):
            nc.vector.memset(zeros, 0.0)
            nc.vector.memset(zero, 0.0).then_inc(zeroed, 1)
            OWN = 13

            def front(i, f):
                if i == 0:
                    wait(dve, o_ready, f + 1)
                    o = b_f.rearrange("p (h t e) -> p h t e", h=RH, t=CH)
                    for t in range(CH):
                        last = nc.vector.bn_stats(bn[t], o[:, :, t, :])
                    last.then_inc(o_stats, 1)
                    wait(dve, o_stats, f + 1)
                    carry(nc, stats)
                    for t in range(CH):
                        last = nc.vector.bn_aggr(mv[:, t, :], bn[t])
                    last.then_inc(o_mv, 1)
                if i == 1:
                    wait(dve, o_rstd, f + 1)
                    o = b_f.rearrange("p (h t e) -> p h t e", h=RH, t=CH)
                    for t in range(CH):
                        last = nc.vector.tensor_scalar(y[:, t * D:(t + 1) * D].rearrange("p (h e) -> p h e", h=RH), o[:, :, t, :],
                                                       mv[:, t, 0:1], rstd[:, t:t + 1], ALU.subtract, ALU.mult)
                    last.then_inc(o_normed, 1)
                if i == 3:
                    wait(dve, biased, f + 1)
                    nc.vector.tensor_tensor(tok(y), tok(y), part(w_all, f), ALU.mult).then_inc(wy_ready, 1)
                if i == 6:
                    wait(dve, mixed, f + 1)
                    wait(dve, wy_turned, f + 1)
                    nc.vector.tensor_tensor(tok(y), tok(b_f), part(x1, f), ALU.add).then_inc(h_ready, 1)
                    wait(dve, h_ready, f + 1)
                    for t in range(CH):
                        last = nc.vector.bn_stats(bn[t], y[:, t * D:(t + 1) * D])
                    last.then_inc(h_stats, 1)
                    wait(dve, h_stats, f + 1)
                    carry(nc, stats)
                    for t in range(CH):
                        last = nc.vector.bn_aggr(mv[:, t, :], bn[t])
                    last.then_inc(h_mv, 1)
                if i == 7:
                    wait(dve, h_rstd, f + 1)
                    wait(dve, cur_copied, f)
                    for t in range(CH):
                        last = nc.vector.tensor_scalar(x2n[:, t * D:(t + 1) * D], y[:, t * D:(t + 1) * D], mv[:, t, 0:1],
                                                       rstd[:, t:t + 1], ALU.subtract, ALU.mult)
                    last.then_inc(x2_ready, 1)
                if i == 10:
                    lg = b_r[:, 0:CH * NE].rearrange("p (t e) -> p t e", t=CH)
                    wait(dve, logits, f + 1)
                    nc.vector.tensor_reduce(smax, lg, AX_X, ALU.max).then_inc(maxed, 1)
                    wait(dve, maxed, f + 1)
                    nc.vector.tensor_tensor(score, lg, over(smax, NE), ALU.subtract).then_inc(less, 1)
                if i == 11:
                    count = [0]

                    def link(ins):
                        count[0] += 1
                        ins.then_inc(own, 1)
                        wait(dve, own, f * OWN + count[0])

                    wait(dve, exped, f + 1)
                    link(nc.vector.tensor_reduce(ssum, score, AX_X, ALU.add))
                    link(nc.vector.reciprocal(srec, ssum))
                    link(nc.vector.tensor_tensor(score, score, over(srec, NE), ALU.mult))
                    for t in range(CH):
                        above = rank[0][:, t * 64:(t + 1) * 64].rearrange("p (e j) -> p e j", e=NE)
                        equal = rank[1][:, t * 64:(t + 1) * 64].rearrange("p (e j) -> p e j", e=NE)
                        of_j = score[:, t, :].unsqueeze(1).to_broadcast([P, NE, NE])
                        of_e = over(score[:, t, :], NE)
                        nc.vector.tensor_tensor(above, of_j, of_e, ALU.is_gt)
                        last = nc.vector.tensor_tensor(equal, of_j, of_e, ALU.is_equal)
                    link(last)
                    r1 = rank[1].rearrange("p (t e j) -> p t (e j)", t=CH, e=NE)
                    link(nc.vector.tensor_tensor(r1, r1, before.rearrange("p e j -> p (e j)").unsqueeze(1)
                                                 .to_broadcast([P, CH, NE * NE]), ALU.mult))
                    link(nc.vector.tensor_tensor(rank[0], rank[0], rank[1], ALU.add))
                    link(nc.vector.tensor_reduce(ranks, rank[0].rearrange("p (t e j) -> p t e j", t=CH, e=NE), AX_X,
                                                 ALU.add))
                    link(nc.vector.tensor_scalar(ranks, ranks, 1.5, None, ALU.is_lt))
                    link(nc.vector.tensor_tensor(rest, score, ranks, ALU.mult))
                    for c in range(PARTS):
                        ins = nc.vector.tensor_copy(parts[:, :, c, :], rest)
                        if c < PARTS - 1:
                            link(ins)
                            link(nc.vector.tensor_tensor(rest, rest, parts[:, :, c, :], ALU.subtract))
                    ins.then_inc(parts_ready, 1)
                    assert count[0] == OWN
                if i == 12:
                    wait(dve, parts_turned, f + 1)
                    wait(dve, w_ready, f * ET)
                    nc.vector.tensor_copy(wT_b, b_r[:, 0:CT // 2].bitcast(BF16)[0:PARTS * NE, :]).then_inc(wT_ready, 1)

            def slot(c, i):
                if isinstance(c, int) and c == CHUNKS:
                    return
                n = rows(i)
                wait(dve, u_ready, c * FT + (i + 1))
                wait(dve, silued, c * FT + (i + 1))
                if c_past(c, i, 2):
                    wait(dve, hid_ready, c * FT + (i - 1))
                h = hid[i % 2][0:n, :]
                if i < ET:
                    nc.vector.tensor_tensor(h, sil[0:n, :], b_u[0:n, :], ALU.mult).then_inc(gated, 1)
                    wait(dve, w_ready, c * ET + (i + 1))
                    wait(dve, gated, c * FT + (i + 1))
                    nc.vector.tensor_tensor(h, h, b_w[0:n, :], ALU.mult).then_inc(hid_made, 1)
                else:
                    nc.vector.tensor_tensor(h, sil[0:n, :], b_u[0:n, :], ALU.mult).then_inc(gated, 1)
                    wait(dve, gated, c * FT + (i + 1))
                    nc.vector.tensor_copy(stats[:, 100:101], stats[:, 0:1]).then_inc(hid_made, 1)
                wait(dve, hid_high, c * FT + (i + 1))
                if c_past(c, i, 1):
                    wait(dve, down_done, c * FT + i)
                nc.vector.tensor_tensor(hid_lo[0:n, :], h, hid_hi[i % 2][0:n, :].bitcast(F32), ALU.subtract).then_inc(hid_ready, 1)

            def back(i, c):
                if i == 0:
                    wait(dve, acc_ready, c + 1)
                    wait(dve, cur_copied, c + 1)
                    wait(dve, stored, c * 16)
                    nc.vector.tensor_tensor(h3, b_acc, x2c, ALU.add).then_inc(h3_ready, 1)
                if i == 1:
                    wait(dve, h3_ready, c + 1)
                    for t in range(CH):
                        last = nc.vector.bn_stats(bn3[t], h3[:, t * D:(t + 1) * D])
                    last.then_inc(h3_stats, 1)
                    wait(dve, h3_stats, c + 1)
                    carry(nc, stats)
                    for t in range(CH):
                        last = nc.vector.bn_aggr(mv3[:, t, :], bn3[t])
                    last.then_inc(h3_mv, 1)
                if i == 2:
                    wait(dve, h3_rstd, c + 1)
                    for t in range(CH):
                        last = nc.vector.tensor_scalar(h3[:, t * D:(t + 1) * D], h3[:, t * D:(t + 1) * D], mv3[:, t, 0:1],
                                                       rstd3[:, t:t + 1], ALU.subtract, ALU.mult)
                    last.then_inc(y3_ready, 1)

            def turn(f):
                wait(dve, u_ready, f * FT)
                wait(dve, high, f + 1)
                nc.vector.tensor_tensor(x2_lo, turned.rearrange("p (k n) -> p k n", k=KD), x2_hi.bitcast(F32),
                                        ALU.subtract).then_inc(split, 1)

            chunks(dve, front, slot, turn, back)

        @block.gpsimd
        def _(pool):
            def rsqrt(var, eps, tmp, dst, ready, between, done, n):
                wait(pool, ready, n)
                nc.gpsimd.tensor_tensor(tmp.unsqueeze(2), var[:, :, 1:2], eps.to_broadcast([P, CH]).unsqueeze(2),
                                        ALU.add).then_inc(between, 1)
                wait(pool, between, n)
                nc.gpsimd.tensor_tensor(dst, tmp, neg_half, ALU.pow).then_inc(done, 1)

            def front(i, f):
                if i == 0:
                    rsqrt(mv, gn_eps, ve, rstd, o_mv, o_var, o_rstd, f + 1)
                if i == 1:
                    wait(pool, o_normed, f + 1)
                    nc.gpsimd.tensor_tensor(tok(y), tok(y), gamma.unsqueeze(1).to_broadcast([P, CH, D]), ALU.mult).then_inc(scaled, 1)
                if i == 2:
                    wait(pool, scaled, f + 1)
                    nc.gpsimd.tensor_tensor(tok(y), tok(y), beta.unsqueeze(1).to_broadcast([P, CH, D]), ALU.add).then_inc(biased, 1)
                if i == 6:
                    rsqrt(mv, ln_eps, ve, rstd, h_mv, h_var, h_rstd, f + 1)

            def back(i, c):
                if i == 1:
                    rsqrt(mv3, ln_eps, ve3, rstd3, h3_mv, h3_var, h3_rstd, c + 1)

            chunks(pool, front=front, back=back)


def constants():
    inv_freq = (1.0 / np.float32(10000.0) ** (np.arange(HALF, dtype=np.float32) * np.float32(2.0 / ROT))).astype(np.float32)

    def rotation(pos):
        ang = (pos.astype(np.float32)[:, None] * inv_freq[None, :]).astype(np.float32)
        c, s = np.cos(ang).astype(np.float32), np.sin(ang).astype(np.float32)
        ones = np.ones((len(pos), HD - ROT), np.float32)
        return np.concatenate([c, c, ones], 1), np.concatenate([-s, s], 1)

    pos = np.arange(P) % S
    ends = (np.arange(P) % NC) * BLK + BLK - 1
    cos_t, sin_t = rotation(pos)
    cos_e, sin_e = rotation(ends)
    open_ = np.concatenate([np.arange(S)[None] <= pos[:, None], (np.arange(NC) * BLK + BLK - 1)[None] <= pos[:, None],
                            np.ones((P, 1), bool)], 1)
    gam = (1.0 - 2.0 ** (-5.0 - np.arange(RH, dtype=np.float32))).astype(np.float32)
    expo = np.arange(S, dtype=np.float32)[None, :] - np.arange(S, dtype=np.float32)[:, None]
    dm = np.where(expo[None] <= 0, gam[:, None, None] ** expo[None], 0.0).astype(np.float32)
    dm = dm / np.sqrt(dm.sum(axis=-1))[:, None, :] / np.sqrt(np.float32(HD))
    decay = dm.transpose(1, 0, 2).reshape(S, RH * S).astype(np.float32)
    expert = np.arange(ET * P) // EF
    select = np.tile((expert[None] == np.arange(NE)[:, None]).astype(np.float32), (PARTS, 1))
    before = (np.arange(NE)[None] < np.arange(NE)[:, None]).astype(np.float32).reshape(1, -1)
    mask = np.where(open_, 0.0, -1e30).astype(np.float32)
    return {"ident": np.eye(P, dtype=np.float32), "cos_token": cos_t, "sin_token": sin_t, "cos_entry": cos_e,
            "sin_entry": sin_e, "mask": np.tile(mask, (1, G)), "decay": decay, "select": select, "before": before}


def kernel(**inputs):
    import concourse.bacc as _bacc
    from concourse import mybir as _mybir
    from concourse.bass_utils import run_bass_kernel_spmd as _run

    i = {k: np.asarray(v) for k, v in inputs.items()}
    at = {k[len("L0_attn_"):]: v for k, v in i.items() if k.startswith("L0_attn_")}
    x = i["x"].reshape(TOK, D)
    arrays = {
        "x": x, "xT": x.T, "Wq": at["Wq"], "Wlk": at["Wlk"], "Wlv": at["Wlv"], "Wo": at["Wo"],
        "Wk": at["Wk"], "Wv": at["Wv"], "Wc": at["Wc"].reshape(1, D), "bc": at["bc"].reshape(1, 1),
        "bq": at["bq"].reshape(1, -1), "blk": at["blk"].reshape(1, -1), "bk": at["bk"].reshape(1, -1),
        "bvT": at["bv"].reshape(HD, 1), "blvT": at["blv"].reshape(NH, HD).T, "qn_w": at["qn_w"].reshape(1, -1),
        "kn_w": at["kn_w"].reshape(1, -1), "sink_kT": at["sink_k"].T, "sink_vT": at["sink_v"].T,
        "bo": at["bo"].reshape(1, D),
    }
    xa = {k[len("L0_xattn_"):]: v for k, v in i.items() if k.startswith("L0_xattn_")}
    ff = {k[len("L0_ffn_"):]: v for k, v in i.items() if k.startswith("L0_ffn_")}
    arrays |= {
        "ctxT": i["ctx_2048"].reshape(TOK, D).T, "Wh": xa["Wh"], "WhT": xa["Wh"].transpose(0, 2, 1), "wg_w": xa["wg_w"],
        "wo_w": xa["wo_w"], "gn_gamma": xa["gn_gamma"].reshape(1, D), "gn_beta": xa["gn_beta"].reshape(1, D),
        "WrT": ff["Wr"].T,
        "gateT": np.concatenate([ff["Wg"].reshape(NE * EF, D), ff["Wsg"]]).T,
        "upT": np.concatenate([ff["Wu"].reshape(NE * EF, D), ff["Wsu"]]).T,
        "down": np.concatenate([ff["Wd"].transpose(0, 2, 1).reshape(NE * EF, D), ff["Wsd"].T]),
    }
    arrays |= constants()
    arrays = {k: np.ascontiguousarray(v) for k, v in arrays.items()}
    nc = _bacc.Bacc("TRN2", target_bir_lowering=False, num_devices=1)
    a = {k: nc.dram_tensor(f"in_{k}", v.shape, _mybir.dt.from_np(v.dtype), kind="ExternalInput").ap()
         for k, v in arrays.items()}
    out = nc.dram_tensor("out", (TOK, D), F32, kind="ExternalOutput").ap()
    scratch = nc.dram_tensor("cw_scratch", (NE_ * NH, D), F32, kind="Internal").ap()
    program(nc, a, out, scratch)
    r = _run(nc, [{f"in_{k}": v for k, v in arrays.items()}], core_ids=[0])
    return r.results[0]["out"].reshape(B, S, D)
```

```python
from contextlib import ExitStack

import numpy as np

import concourse.bass as bass
from concourse import mybir

F32 = mybir.dt.float32
F32R = mybir.dt.float32r
BF16 = mybir.dt.bfloat16
ALU = mybir.AluOpType
ACT = mybir.ActivationFunctionType
AX_X = mybir.AxisListType.X

P = 128
B, S, D = 32, 64, 256
TOK = B * S
TILES = TOK // P
KD = D // P
NH, HD = 16, 128
G = 4
ST = NH // G
STEPS = TILES * ST
GW = G * HD
BLK = 16
NC = S // BLK
NE_ = B * NC
NK = S + NC + 1
HALF = 32
ROT = 2 * HALF
PC = NH * NC
SINK0 = S
SINKS = NH + 1
RH = D // HD
NE, EF, SF = 8, 176, 352
FALL = NE * EF + SF
FT = -(-FALL // P)
ET = NE * EF // P
CH = 4
CHUNKS = TILES // CH
CT = CH * P
PARTS = 3
RMS_EPS = 1e-6
LN_EPS = 1e-5
GN_EPS = 1e-3
KEPT0 = 9728
ARENA = KEPT0 + 2848
SCALE = float(HD) ** -0.5
CW_AGAIN = NH // 2 - 1
CW_BANKS = (4, 5, 6, 7, 0, 2, 1, 4)


def heads(ap, n):
    return ap.rearrange("p (h d) -> p h d", h=n)


def over(ap, n):
    return ap.unsqueeze(2).to_broadcast([ap.shape[0], ap.shape[1], n])


def halves(ap):
    return ap.rearrange("p h (a b) -> p h a b", a=2)


def rows(i):
    return min(P, FALL - i * P)


def wait(eng, sem, value):
    if not (isinstance(value, int) and value <= 0):
        eng.wait_ge(sem, value)


def carry(nc, stats):
    nc.vector.tensor_copy(stats[:, 101:102], stats[:, 0:1])


def program(nc, a, out, scratch):
    with ExitStack() as ctx:
        def sb(name, shape, dt=F32):
            return ctx.enter_context(nc.sbuf_tensor(name, shape, dt))

        mem = {
            "w_split": sb("w_split", [P, 3, 2, KD, NH * HD], F32R),
            "wo": sb("wo", [P, NH, D]),
            "x1": sb("x1", [P, TILES, D]),
            "qk_bias": sb("qk_bias", [P, 2, NH * HD]),
            "arena": sb("arena", [P, ARENA]),
            "x_parts": sb("x_parts", [P, 2, KD, P], F32R),
            "gram": sb("gram", [P, RH, HD]),
            "wh": sb("wh", [P, RH, HD]),
            "wg": sb("wg", [P, KD, D]),
            "ident": sb("ident", [P, P]),
            "identb": sb("identb", [P, P], BF16),
            "maskb": sb("maskb", [P, G * NK], BF16),
            "rot_c": sb("rot_c", [P, 2, HD]),
            "rot_s": sb("rot_s", [P, 2, ROT]),
            "ckT": sb("ckT", [P, NE_]),
            "sink_rows": sb("sink_rows", [P, D]),
            "stats": sb("stats", [P, 128]),
            "w_parts": sb("w_parts", [P, CT], BF16),
            "select": sb("select", [P, ET * P], BF16),
        }
        psum = ctx.enter_context(nc.psum_tensor("psum", [P, 8 * 512], F32))
        banks = [psum[:, i * 512:(i + 1) * 512] for i in range(8)]
        mem["cw_stored"] = ctx.enter_context(nc.semaphore("cw_stored"))
        mem["wg_loaded"] = ctx.enter_context(nc.semaphore("wg_loaded"))
        mem["ctx_loaded"] = ctx.enter_context(nc.semaphore("ctx_loaded"))
        mem["raw_loaded"] = ctx.enter_context(nc.semaphore("raw_loaded"))
        prologue(nc, a, scratch, mem, banks)
        attention(nc, a, scratch, mem, banks)
        mixing(nc, a, mem, psum)
        feed_forward(nc, a, mem, psum, out)


def prologue(nc, a, scratch, mem, banks):
    w_split, wo, ident = mem["w_split"], mem["wo"], mem["ident"]
    arena = mem["arena"]
    prod = mem["qk_bias"][:, :, :].rearrange("p i n -> p (i n)")
    raw = [arena[:, 0:4096], arena[:, 4096:8192], prod]
    spare = arena[:, 8192:KEPT0]
    cw = mem["x1"][:, :, :].rearrange("p t d -> p (t d)")
    late = arena[:, KEPT0:ARENA]
    x_blk = mem["x1"][:, :, :]
    entry = late[:, 0:256]
    entryT = late[:, 256:512].rearrange("p (k e) -> p k e", k=KD)
    wc_b = late[:, 512:768]
    wk6 = late[:, 768:1024].rearrange("p (k d) -> p k d", k=KD)
    wv6 = late[:, 1024:1280].rearrange("p (k d) -> p k d", k=KD)
    ck = late[:, 1280:1408]
    ck_rot = late[:, 1408:1536]
    ck_part = late[:, 1536:1600]
    bk_b = late[:, 1600:1728]
    cvT = late[:, 1728:1856]
    cos_e = late[:, 1856:1984]
    sin_e = late[:, 1984:2048]
    cos_t = late[:, 2048:2176]
    sin_t = late[:, 2176:2240]
    norm_w = late[:, 2240:2496].rearrange("p (k d) -> p k d", k=2)
    sink_vT = late[:, 2496:2512]
    blvT = late[:, 2512:2528]
    bv_c = late[:, 2528:2529]
    bc_b = late[:, 2529:2530]
    logit = late[:, 2530:2546]
    weight = late[:, 2546:2562]
    one = [late[:, 2562 + i:2563 + i] for i in range(6)]
    mask = late[:, 2568:2568 + G * NK]
    lw = SINK0 + SINKS
    sink_l = spare[:, 0:NH * lw]
    x_t = spare[:, 0:D].rearrange("p (k n) -> p k n", k=KD)
    whT = mem["wg"][:, 0, :].rearrange("p (h d) -> p h d", h=RH)

    with ExitStack() as ctx:
        def sem(name):
            return ctx.enter_context(nc.semaphore(name))

        loaded_blk, loaded_entry_w, loaded_sink = sem("loaded_blk"), sem("loaded_entry_w"), sem("loaded_sink")
        loaded_raw = [sem(f"loaded_raw{i}") for i in range(3)]
        loaded_wo, loaded_const = sem("loaded_wo"), sem("loaded_const")
        split_hi = sem("split_hi")
        w_logits, w_exp, entries_done = sem("w_logits"), sem("w_exp"), sem("entries_done")
        entry_turned, entryT_copied = sem("entry_turned"), sem("entryT_copied")
        ck_raw, cv_raw, cvT_done = sem("ck_raw"), sem("cv_raw"), sem("cvT_done")
        ck_sumsq, ck_inv, ck_ready, ck_turned = sem("ck_sumsq"), sem("ck_inv"), sem("ck_ready"), sem("ck_turned")
        cw_ready, cw_by_act, cw_by_dve = sem("cw_ready"), sem("cw_by_act"), sem("cw_by_dve")
        whT_loaded, gram_ready, x_loaded = sem("whT_loaded"), sem("gram_ready"), sem("first_x_loaded")
        gram_copied = sem("gram_copied")
        sink_l_ready, sink_ready = sem("sink_l_ready"), sem("sink_ready")
        dve_own, pool_own = sem("dve_own"), sem("pool_own")
        sink_rows_done, bo_loaded = sem("sink_rows_done"), sem("bo_loaded")
        block = ctx.enter_context(nc.Block())

        def halves_of(i, k):
            return raw[i].rearrange("p (k n) -> p k n", k=KD)[:, k, :], w_split[:, i, 0, k, :], w_split[:, i, 1, k, :]

        @block.sync
        def _(sp):
            sp.dma_start(x_blk, a["x"].rearrange("(e r) d -> e r d", r=BLK)).then_inc(loaded_blk, 16)
            sp.dma_start(wc_b, a["Wc"].partition_broadcast(P)).then_inc(loaded_blk, 16)
            sp.dma_start(bc_b, a["bc"].partition_broadcast(P)).then_inc(loaded_blk, 16)
            sp.dma_start(raw[0].rearrange("p (k n) -> p k n", k=KD),
                         a["Wq"].rearrange("(k p) n -> p k n", p=P)).then_inc(loaded_raw[0], 16)
            sp.dma_start(wo[:, :, :], a["Wo"].rearrange("(h p) n -> p h n", p=P)).then_inc(loaded_wo, 16)
            sp.dma_start(raw[1].rearrange("p (k n) -> p k n", k=KD),
                         a["Wlk"].rearrange("(k p) n -> p k n", p=P)).then_inc(loaded_raw[1], 16)
            sp.wait_ge(w_logits, 1)
            sp.dma_start(raw[2].rearrange("p (k n) -> p k n", k=KD),
                         a["Wlv"].rearrange("(k p) n -> p k n", p=P)).then_inc(loaded_raw[2], 16)
            sp.wait_ge(sink_ready, 1)
            sp.dma_start(x_t, a["xT"].rearrange("(k p) n -> p k n", p=P)[:, :, 0:P]).then_inc(x_loaded, 16)
            sp.wait_ge(cw_by_act, NH // 8)
            sp.wait_ge(cw_by_dve, NH // 8)
            store_cw(sp, scratch, mem, 0)

        @block.scalar
        def _(act):
            for dst, src in ((sink_vT, a["sink_vT"]), (blvT, a["blvT"])):
                act.dma_start(dst, src).then_inc(loaded_sink, 16)
            act.dma_start(whT, a["WhT"].rearrange("h e d -> e h d")).then_inc(whT_loaded, 16)
            for dst, src in ((ident[:, :], a["ident"]), (cos_e, a["cos_entry"]), (sin_e, a["sin_entry"]),
                             (cos_t, a["cos_token"]), (sin_t, a["sin_token"]),
                             (norm_w[:, 0, :], a["qn_w"].partition_broadcast(P)),
                             (norm_w[:, 1, :], a["kn_w"].partition_broadcast(P)), (mask, a["mask"])):
                act.dma_start(dst, src).then_inc(loaded_const, 16)
            for dst, src in ((wk6, a["Wk"].rearrange("(k p) n -> p k n", p=P)),
                             (wv6, a["Wv"].rearrange("(k p) n -> p k n", p=P)),
                             (bk_b, a["bk"].partition_broadcast(P)), (bv_c, a["bvT"])):
                act.dma_start(dst, src).then_inc(loaded_entry_w, 16)

            def high(i, k):
                src, hi, _ = halves_of(i, k)
                nc.scalar.activation(hi, src, ACT.Copy).then_inc(split_hi, 1)

            act.wait_ge(gram_ready, 1)
            nc.scalar.activation(mem["gram"][:, :, :], banks[2][:, 0:RH * HD].rearrange("p (h e) -> p h e", h=RH),
                                 ACT.Copy).then_inc(gram_copied, 1)
            act.dma_start(mem["wh"][:, :, :], a["Wh"].rearrange("h d e -> d h e")).then_inc(mem["wg_loaded"], 16)
            act.dma_start(mem["wg"][:, :, :], a["wg_w"].rearrange("(k p) n -> p k n", p=P)).then_inc(mem["wg_loaded"], 16)
            act.wait_ge(loaded_raw[0], 16)
            high(0, 0)
            high(0, 1)
            act.wait_ge(w_logits, 1)
            nc.scalar.activation(weight, logit, ACT.Exp).then_inc(w_exp, 1)
            act.wait_ge(loaded_raw[1], 16)
            high(1, 0)
            high(1, 1)
            act.wait_ge(entry_turned, 1)
            nc.scalar.activation(entryT, banks[0][:, 0:KD * P].rearrange("p (k e) -> p k e", k=KD),
                                 ACT.Copy).then_inc(entryT_copied, 1)
            act.wait_ge(cv_raw, 1)
            nc.scalar.activation(cvT, banks[2][:, 0:P], ACT.Identity, bias=bv_c).then_inc(cvT_done, 1)
            act.wait_ge(loaded_raw[2], 16)
            high(2, 0)
            high(2, 1)
            for i in (0, 2, 4, 6, 7):
                act.wait_ge(cw_ready, i + 1)
                nc.scalar.activation(cw[:, 2 * i * D:2 * (i + 1) * D], banks[CW_BANKS[i]][:, :], ACT.Copy,
                                     scale=0.5).then_inc(cw_by_act, 1)

        @block.gpsimd
        def _(pool):
            nc.gpsimd.memset(mem["stats"][:, 0:8], -0.5).then_inc(pool_own, 1)
            nc.gpsimd.memset(mem["sink_rows"][:, :], 0.0).then_inc(pool_own, 1)
            nc.gpsimd.memset(mem["stats"][:, 104:112], HD * RMS_EPS)
            nc.gpsimd.memset(mem["stats"][:, 112:113], LN_EPS)
            nc.gpsimd.memset(mem["stats"][:, 113:114], GN_EPS).then_inc(pool_own, 1)
            pool.wait_ge(pool_own, 3)
            pool.dma_start(mem["sink_rows"][SINK0 + NH:SINK0 + SINKS, :], a["bo"]).then_inc(bo_loaded, 16)
            nc.gpsimd.memset(sink_l, 0.0).then_inc(pool_own, 1)
            pool.wait_ge(pool_own, 4)
            pool.wait_ge(loaded_sink, 32)
            nc.gpsimd.tensor_scalar(sink_l[:, SINK0:SINK0 + (lw + 1) * (NH - 1) + 1:lw + 1], sink_vT, 0.5, None,
                                    ALU.mult).then_inc(pool_own, 1)
            pool.wait_ge(pool_own, 5)
            nc.gpsimd.tensor_scalar(sink_l[:, lw - 1::lw], blvT, 0.5, None, ALU.mult).then_inc(sink_l_ready, 1)

            def low(i, k):
                src, hi, lo = halves_of(i, k)
                nc.gpsimd.tensor_tensor(lo, src, hi.bitcast(F32), ALU.subtract)

            pool.wait_ge(split_hi, 2)
            low(0, 0)
            low(0, 1)
            pool.wait_ge(split_hi, 3)
            low(1, 0)
            pool.wait_ge(ck_sumsq, 1)
            nc.gpsimd.tensor_scalar(one[1], one[0], 1.0 / HD, RMS_EPS, ALU.mult, ALU.add).then_inc(pool_own, 1)
            pool.wait_ge(pool_own, 6)
            nc.gpsimd.tensor_tensor(one[2], one[1], mem["stats"][:, 0:1], ALU.pow).then_inc(ck_inv, 1)
            pool.wait_ge(x_loaded, 16)
            nc.gpsimd.tensor_copy(mem["x_parts"][:, 0], x_t).then_inc(pool_own, 1)
            pool.wait_ge(pool_own, 7)
            nc.gpsimd.tensor_tensor(mem["x_parts"][:, 1], x_t, mem["x_parts"][:, 0].bitcast(F32), ALU.subtract)
            pool.wait_ge(split_hi, 5)
            low(2, 0)

        @block.vector
        def _(dve):
            count = [0]

            def link(ins):
                count[0] += 1
                ins.then_inc(dve_own, 1)
                dve.wait_ge(dve_own, count[0])

            dve.wait_ge(loaded_blk, 48)
            prod3 = prod.rearrange("p (r d) -> p r d", r=BLK)
            link(nc.vector.tensor_tensor(prod3, x_blk, wc_b.unsqueeze(1).to_broadcast([P, BLK, D]), ALU.mult))
            link(nc.vector.tensor_reduce(logit, prod3, AX_X, ALU.add))
            link(nc.vector.tensor_scalar(logit, logit, bc_b, None, ALU.add))
            link(nc.vector.tensor_reduce(one[3], logit, AX_X, ALU.max))
            nc.vector.tensor_scalar(logit, logit, one[3], None, ALU.subtract).then_inc(w_logits, 1)
            dve.wait_ge(w_exp, 1)
            link(nc.vector.tensor_reduce(one[4], weight, AX_X, ALU.add))
            link(nc.vector.reciprocal(one[5], one[4]))
            link(nc.vector.tensor_scalar(weight, weight, one[5], None, ALU.mult))
            link(nc.vector.tensor_tensor(x_blk, x_blk, over(weight, D), ALU.mult))
            nc.vector.tensor_reduce(entry, cw.rearrange("p (r d) -> p d r", r=BLK), AX_X,
                                    ALU.add).then_inc(entries_done, 1)
            dve.wait_ge(loaded_const, 16 * 8)
            nc.vector.tensor_copy(mem["maskb"][:, :], mask)
            nc.vector.tensor_copy(mem["identb"][:, :], ident[:, :])
            for i in range(2):
                nc.vector.scalar_tensor_tensor(out=mem["rot_c"][:, i, :], in0=cos_t, scalar=float(HD) ** 0.5,
                                               in1=norm_w[:, i, :], op0=ALU.mult, op1=ALU.mult)
                for half in range(2):
                    nc.vector.scalar_tensor_tensor(
                        out=mem["rot_s"][:, i, half * HALF:(half + 1) * HALF],
                        in0=sin_t[:, half * HALF:(half + 1) * HALF], scalar=float(HD) ** 0.5,
                        in1=norm_w[:, i, (1 - half) * HALF:(2 - half) * HALF], op0=ALU.mult, op1=ALU.mult)
            nc.vector.tensor_tensor(cos_e, cos_e, norm_w[:, 1, :], ALU.mult)
            for half in range(2):
                last = nc.vector.tensor_tensor(
                    sin_e[:, half * HALF:(half + 1) * HALF], sin_e[:, half * HALF:(half + 1) * HALF],
                    norm_w[:, 1, (1 - half) * HALF:(2 - half) * HALF], ALU.mult)
            link(last)
            dve.wait_ge(ck_raw, 1)
            link(nc.vector.tensor_tensor(ck, banks[1][:, 0:HD], bk_b, ALU.add))
            nc.vector.tensor_tensor_reduce(out=ck_rot, in0=ck, in1=ck, scale=1.0, scalar=0.0, op0=ALU.mult,
                                           op1=ALU.add, accum_out=one[0]).then_inc(ck_sumsq, 1)

            def low(i, k):
                src, hi, lo = halves_of(i, k)
                nc.vector.tensor_tensor(lo, src, hi.bitcast(F32), ALU.subtract)

            dve.wait_ge(split_hi, 4)
            low(1, 1)
            dve.wait_ge(ck_inv, 1)
            link(nc.vector.tensor_scalar(ck, ck, one[2], None, ALU.mult))
            nc.vector.tensor_tensor(ck_rot, ck, cos_e, ALU.mult)
            for half in range(2):
                last = nc.vector.tensor_tensor(
                    ck_part[:, half * HALF:(half + 1) * HALF], ck[:, (1 - half) * HALF:(2 - half) * HALF],
                    sin_e[:, half * HALF:(half + 1) * HALF], ALU.mult)
            link(last)
            nc.vector.tensor_tensor(ck_rot[:, 0:ROT], ck_rot[:, 0:ROT], ck_part, ALU.add).then_inc(ck_ready, 1)
            dve.wait_ge(sink_ready, 1)
            dve.wait_ge(bo_loaded, 16)
            rows = mem["sink_rows"][SINK0:SINK0 + SINKS, :]
            nc.vector.tensor_tensor(rows, banks[3][SINK0:SINK0 + SINKS, 0:D], rows, ALU.add).then_inc(sink_rows_done, 1)
            for i in (1, 3, 5):
                dve.wait_ge(cw_ready, i + 1)
                nc.vector.tensor_scalar(cw[:, 2 * i * D:2 * (i + 1) * D], banks[CW_BANKS[i]][:, :], 0.5, None,
                                        ALU.mult).then_inc(cw_by_dve, 1)
            dve.wait_ge(split_hi, 6)
            low(2, 1)
            dve.wait_ge(ck_turned, 1)
            nc.vector.tensor_copy(mem["ckT"][:, :], banks[3][:, D:D + P])

        @block.tensor
        def _(pe):
            pe.wait_ge(whT_loaded, 16)
            for h in range(RH):
                last = nc.tensor.matmul(banks[2][:, h * HD:(h + 1) * HD], whT[:, h, :], whT[:, h, :], start=True, stop=True)
            last.then_inc(gram_ready, 1)
            pe.wait_ge(sink_l_ready, 1)
            pe.wait_ge(loaded_wo, 16)
            for h in range(NH):
                last = nc.tensor.matmul(banks[3][0:lw, 0:D], sink_l[:, h * lw:(h + 1) * lw], wo[:, h, :],
                                        start=h == 0, stop=h == NH - 1)
            last.then_inc(sink_ready, 1)
            pe.wait_ge(entries_done, 1)
            pe.wait_ge(loaded_const, 16 * 8)
            for k in range(KD):
                last = nc.tensor.transpose(banks[0][:, k * P:(k + 1) * P], entry[:, k * P:(k + 1) * P], ident[:, :])
            last.then_inc(entry_turned, 1)
            pe.wait_ge(entryT_copied, 1)
            pe.wait_ge(loaded_entry_w, 16 * 4)
            pe.wait_ge(gram_copied, 1)
            for k in range(KD):
                last = nc.tensor.matmul(banks[2][:, 0:P], wv6[:, k, :], entryT[:, k, :], start=k == 0, stop=k == KD - 1)
            last.then_inc(cv_raw, 1)
            for k in range(KD):
                last = nc.tensor.matmul(banks[1][:, 0:HD], entryT[:, k, :], wk6[:, k, :], start=k == 0, stop=k == KD - 1)
            last.then_inc(ck_raw, 1)
            pe.wait_ge(cvT_done, 1)
            for i in range(NH // 2):
                if CW_BANKS[i] == 1:
                    pe.wait_ge(ck_sumsq, 1)
                if i == CW_AGAIN:
                    pe.wait_ge(cw_by_act, 1)
                nc.tensor.matmul(banks[CW_BANKS[i]][:, :], cvT, wo[:, 2 * i:2 * i + 2, :], start=True, stop=True).then_inc(cw_ready, 1)
            pe.wait_ge(sink_rows_done, 1)
            pe.wait_ge(ck_ready, 1)
            nc.tensor.transpose(banks[3][:, D:D + P], ck_rot, ident[:, :]).then_inc(ck_turned, 1)


def first_ctx(mem):
    return mem["w_parts"][:, :].bitcast(F32).rearrange("p (h n) -> p h n", h=RH)


def store_cw(eng, scratch, mem, half):
    to = scratch.rearrange("(b h c) n -> c b h n", h=NH, c=NC)
    cw = mem["x1"][:, :, :].rearrange("p t d -> p (t d)").rearrange("p (h n) -> p h n", h=NH)
    cols = slice(half * NH // 2, (half + 1) * NH // 2)
    for c in range(NC):
        eng.dma_start(to[c, :, cols, :], cw[c::NC, cols, :]).then_inc(mem["cw_stored"], 16)


def attention(nc, a, scratch, mem, banks):
    cursor = [0]

    def carve(n):
        cursor[0] += n
        return mem["arena"][:, cursor[0] - n:cursor[0]]

    qk_b = carve(2 * GW)
    squares = carve(2 * GW)
    rot = [carve(2 * GW), carve(2 * GW)]
    rot_part = carve(2 * G * ROT)
    qT = carve(GW)
    v_sb = [carve(GW) for _ in range(ST)]
    ctxT = carve(GW)
    shifted = heads(carve(G * NK), G)
    e_sb = heads(carve(G * NK), G)
    p_loc = carve(G * S)
    p_comp = carve(PC + NH)
    pcT = carve(P)
    cw_t = carve(D)
    x_t = carve(D).rearrange("p (k n) -> p k n", k=KD)
    x_res = carve(D)
    h_sb = carve(D)
    assert cursor[0] <= KEPT0
    cursor[0] = KEPT0
    pT = carve(GW).rearrange("p (h q) -> p h q", h=G)
    kT = [carve(G * 2 * NK).rearrange("p (h b k) -> p h b k", h=G, b=2) for _ in range(ST)]
    sinkT = carve(P)
    w_split, wo, x1, ident = mem["w_split"], mem["wo"], mem["x1"], mem["ident"]
    x_hi, x_lo = mem["x_parts"][:, 0], mem["x_parts"][:, 1]
    stats = mem["stats"]
    neg_half = stats[:, 0:8]
    ss, inv = stats[:, 8:16], stats[:, 16:24]
    mx, sums, rsums = stats[:, 24:32], stats[:, 32:40], stats[:, 40:48]
    bn, mv, rstd, var_eps = stats[:, 48:54], stats[:, 54:56], stats[:, 56:57], stats[:, 57:58]
    ms = stats[:, 64:72]
    rms_eps, ln_eps = stats[:, 104:112], stats[:, 112:113]
    bank_q, bank_k, bank_v, bank_t0, bank_t1, bank_s, bank_p, bank_o = banks

    with ExitStack() as ctx:
        def sem(name):
            return ctx.enter_context(nc.semaphore(name))

        q_proj, k_proj, v_proj = sem("q_proj"), sem("k_proj"), sem("v_proj")
        q_biased, k_biased, v_copied = sem("q_biased"), sem("k_biased"), sem("v_copied")
        squared, summed_sq, ms_ready, inv_ready = sem("squared"), sem("summed_sq"), sem("ms_ready"), sem("inv_ready")
        cos_part, sin_part, rotated, normed = sem("cos_part"), sem("sin_part"), sem("rotated"), sem("normed")
        q_turned, k_turned, qT_copied, kT_copied = sem("q_turned"), sem("k_turned"), sem("qT_copied"), sem("kT_copied")
        ck_placed, scored, maxed, s_shifted = sem("ck_placed"), sem("scored"), sem("maxed"), sem("s_shifted")
        exped, e_summed, e_recip, probs = sem("exped"), sem("e_summed"), sem("e_recip"), sem("probs")
        p_turned, pT_copied, ctx_ready, ctx_copied = sem("p_turned"), sem("pT_copied"), sem("ctx_ready"), sem("ctx_copied")
        x_loaded, res_loaded, cw_loaded = sem("x_loaded"), sem("res_loaded"), sem("cw_loaded")
        x_high, x_split = sem("x_high"), sem("x_split")
        pc_turned, pcT_copied, o_ready = sem("pc_turned"), sem("pcT_copied"), sem("o_ready")
        h_summed, h_stats, h_mv, rstd_ready, x1_ready = sem("h_summed"), sem("h_stats"), sem("h_mv"), sem("rstd_ready"), sem("x1_ready")
        var_ready = sem("var_ready")
        zeroed, sinks_placed = sem("zeroed"), sem("sinks_placed")
        bias_loaded = [sem("bias_loaded_first"), sem("bias_loaded_rest")]
        block = ctx.enter_context(nc.Block())

        def has(s0, g, lag):
            return not isinstance(s0, int) or 0 <= s0 + g - lag < STEPS

        def tiles(eng, tile):
            tile(0, 0)
            tile(1, ST)
            with eng.Fori(2, TILES) as t:
                tile(t, t * ST)
            tile(TILES, STEPS)

        @block.sync
        def _(sp):
            xT = a["xT"].rearrange("(k p) (t n) -> t p k n", p=P, n=P)
            xr = a["x"].rearrange("(t p) d -> t p d", p=P)
            cwr = scratch.rearrange("(t r) n -> t r n", r=P)

            def at(view, t):
                return view[t] if isinstance(t, int) else view[bass.ds(t, 1)][0]

            def tokens(t):
                wait(sp, x_split, t - 1)
                sp.dma_start(x_t, at(xT, t)).then_inc(x_loaded, 16)

            def rest(t):
                wait(sp, h_summed, t)
                sp.dma_start(x_res, at(xr, t)).then_inc(res_loaded, 16)
                wait(sp, o_ready, t)
                sp.dma_start(cw_t, at(cwr, t)).then_inc(cw_loaded, 16)

            for g in range(ST):
                for i, name in enumerate(("bq", "blk")):
                    sp.dma_start(mem["qk_bias"][:, i, g * GW:(g + 1) * GW],
                                 a[name][:, g * GW:(g + 1) * GW].partition_broadcast(P)).then_inc(bias_loaded[min(g, 1)], 16)
            store_cw(sp, scratch, mem, 1)
            tokens(1)
            sp.wait_ge(mem["cw_stored"], 16 * 2 * NC)
            rest(0)
            with sp.Fori(1, TILES - 1) as t:
                tokens(t + 1)
                rest(t)
            rest(TILES - 1)
            sp.dma_start(first_ctx(mem), a["ctxT"].rearrange("(h p) n -> p h n", p=P)[:, :, 0:P]).then_inc(mem["ctx_loaded"], 16)
            sp.wait_ge(q_biased, STEPS)
            sp.wait_ge(k_biased, STEPS)
            for k in range(KD):
                load_raw(sp, a, mem, "gateT", k)

        @block.tensor
        def _(pe):
            def tile(t, s0):
                for g in range(ST):
                    s = s0 + g
                    if has(s0, g, 2):
                        wait(pe, normed, s - 1)
                        wait(pe, ctx_copied, s - 3)
                        wait(pe, kT_copied, s - 2)
                        src = rot[g % 2]
                        for j in range(G):
                            last = nc.tensor.transpose(bank_t0[:, j * P:(j + 1) * P], src[:, j * HD:(j + 1) * HD], ident[:, :])
                        last.then_inc(q_turned, 1)
                        for j in range(G):
                            last = nc.tensor.transpose(bank_t1[:, j * P:(j + 1) * P],
                                                       src[:, GW + j * HD:GW + (j + 1) * HD], ident[:, :])
                        last.then_inc(k_turned, 1)
                    if has(s0, g, 3):
                        wait(pe, probs, s - 2)
                        wait(pe, pT_copied, s - 3)
                        if g == 3:
                            wait(pe, pcT_copied, t)
                        for j in range(0, G, 2):
                            last = nc.tensor.transpose(bank_p[:, j * S:j * S + P], p_loc[:, j * S:j * S + P], ident[:, :])
                        last.then_inc(p_turned, 1)
                        if g == 2:
                            nc.tensor.transpose(bank_p[0:PC + NH, 256:256 + P], p_comp, ident[:, :]).then_inc(pc_turned, 1)
                    if has(s0, g, 4):
                        wait(pe, ctx_copied, s - 3)
                        if g == 0:
                            wait(pe, h_summed, t - 1)
                        for j in range(G):
                            nc.tensor.matmul(bank_o[:, 0:D], ctxT[:, j * P:(j + 1) * P], wo[:, g * G + j, :],
                                             start=g == 0 and j == 0, stop=False)
                        if g == ST - 1:
                            wait(pe, pcT_copied, t)
                            wait(pe, cw_loaded, t * 16)
                            nc.tensor.matmul(bank_o[:, 0:D], pcT, cw_t, start=False, stop=False)
                            nc.tensor.matmul(bank_o[:, 0:D], sinkT[SINK0:SINK0 + SINKS, :],
                                             mem["sink_rows"][SINK0:SINK0 + SINKS, :], start=False,
                                             stop=True).then_inc(o_ready, 1)
                    if has(s0, g, 2):
                        wait(pe, s_shifted, s - 2)
                        wait(pe, kT_copied, s - 1)
                        wait(pe, qT_copied, s - 1)
                        wait(pe, ck_placed, s - 1)
                        for b in range(2):
                            rows = slice(b * S, (b + 1) * S)
                            for j in range(G):
                                nc.tensor.matmul(bank_s[rows, j * NK:(j + 1) * NK], qT[:, j * P + b * S:j * P + (b + 1) * S],
                                                 kT[(g + 2) % ST][:, j, b, :], start=j == 0, stop=False)
                        nc.tensor.matmul(bank_s[:, 0:G * NK], mem["identb"][:, :], mem["maskb"][:, :],
                                         start=False, stop=True).then_inc(scored, 1)
                    if has(s0, g, 3):
                        wait(pe, pT_copied, s - 2)
                        wait(pe, v_copied, s - 2)
                        wait(pe, qT_copied, min(s - 1, STEPS) if isinstance(s, int) else s - 1)
                        for j in range(G):
                            last = nc.tensor.matmul(bank_t0[:, j * P:(j + 1) * P], v_sb[(g + 1) % ST][:, j * HD:(j + 1) * HD],
                                                    pT[:, j, :], start=True, stop=True)
                        last.then_inc(ctx_ready, 1)
                    if has(s0, g, 0):
                        if g == 0:
                            wait(pe, x_split, t)
                        for i, (bk, free, done) in enumerate(((bank_q, q_biased, q_proj), (bank_k, k_biased, k_proj),
                                                              (bank_v, v_copied, v_proj))):
                            wait(pe, free, s)
                            n = 0
                            for k in range(KD):
                                for xs, part in ((x_hi, 0), (x_lo, 0), (x_hi, 1)):
                                    last = nc.tensor.matmul(bk[:, :], xs[:, k, :], w_split[:, i, part, k, g * GW:(g + 1) * GW],
                                                            start=n == 0, stop=n == 5)
                                    n += 1
                            last.then_inc(done, 1)
            tiles(pe, tile)

        @block.scalar
        def _(act):
            def tile(t, s0):
                for g in range(ST):
                    s = s0 + g
                    if has(s0, g, 2):
                        wait(act, q_turned, s - 1)
                        wait(act, scored, s - 2)
                        nc.scalar.activation(qT, bank_t0[:, :], ACT.Copy).then_inc(qT_copied, 1)
                        wait(act, k_turned, s - 1)
                        nc.scalar.activation(kT[(g + 2) % ST][:, :, :, 0:S],
                                             bank_t1[:, :].rearrange("p (h b k) -> p h b k", h=G, b=2),
                                             ACT.Copy).then_inc(kT_copied, 1)
                    if has(s0, g, 3):
                        wait(act, p_turned, s - 2)
                        if g == 2:
                            wait(act, pc_turned, t)
                        wait(act, ctx_ready, s - 3)
                        if isinstance(t, int) and t == 0 and g == 3:
                            act.wait_ge(zeroed, 5)
                        src = bank_p[:, 0:256].rearrange("p (a q) -> p a q", a=2)
                        for hj in range(2):
                            for b in range(2):
                                last = nc.scalar.activation(pT[b * S:(b + 1) * S, hj::2, b * S:(b + 1) * S],
                                                            src[hj * S:(hj + 1) * S, :, b * S:(b + 1) * S], ACT.Copy)
                        last.then_inc(pT_copied, 1)
                        if g == 2:
                            wait(act, o_ready, t - 1)
                            for b in range(2):
                                nc.scalar.activation(pcT[b * PC:(b + 1) * PC, b * S:(b + 1) * S],
                                                     bank_p[0:PC, 256 + b * S:256 + (b + 1) * S], ACT.Copy)
                            nc.scalar.activation(sinkT[SINK0:SINK0 + NH, :], bank_p[PC:PC + NH, 256:256 + P],
                                                 ACT.Copy).then_inc(pcT_copied, 1)
                    if has(s0, g, 2):
                        wait(act, s_shifted, s - 1)
                        nc.scalar.activation(e_sb, shifted, ACT.Exp, scale=SCALE).then_inc(exped, 1)
                    if has(s0, g, 3):
                        wait(act, ctx_ready, s - 2)
                        nc.scalar.activation(ctxT, bank_t0[:, :], ACT.Copy, scale=0.5).then_inc(ctx_copied, 1)
                    if has(s0, g, 0):
                        wait(act, q_biased, s + 1)
                        wait(act, k_biased, s + 1)
                        wait(act, summed_sq, s)
                        nc.scalar.activation(squares, qk_b, ACT.Square).then_inc(squared, 1)
                        wait(act, v_proj, s + 1)
                        nc.scalar.activation(v_sb[g], bank_v[:, :], ACT.Copy).then_inc(v_copied, 1)
            tiles(act, tile)

        @block.vector
        def _(dve):
            nc.vector.memset(pT, 0.0).then_inc(zeroed, 1)
            nc.vector.memset(pcT, 0.0).then_inc(zeroed, 1)
            nc.vector.memset(sinkT[SINK0:P, :], 1.0).then_inc(zeroed, 1)
            def split(t):
                wait(dve, x_loaded, t * 16)
                wait(dve, v_proj, t * ST)
                nc.vector.tensor_copy(x_hi, x_t).then_inc(x_high, 1)
                wait(dve, x_high, t)
                nc.vector.tensor_tensor(x_lo, x_t, x_hi.bitcast(F32), ALU.subtract).then_inc(x_split, 1)

            def tile(t, s0):
                for g in range(ST):
                    s = s0 + g
                    if g == 0 and has(s0, 0, 0) and not (isinstance(t, int) and t == 0):
                        split(t)
                    if has(s0, g, 1):
                        wait(dve, squared, s)
                        wait(dve, ms_ready, s - 1)
                        nc.vector.tensor_reduce(ss, heads(squares, 2 * G), AX_X, ALU.add).then_inc(summed_sq, 1)
                        r = rot[(g + 1) % 2]
                        wait(dve, k_turned, s - 2)
                        nc.vector.tensor_tensor(
                            r.rearrange("p (i h d) -> p i h d", i=2, h=G), qk_b.rearrange("p (i h d) -> p i h d", i=2, h=G),
                            mem["rot_c"][:, :, :].unsqueeze(2).to_broadcast([P, 2, G, HD]), ALU.mult).then_inc(cos_part, 1)
                        wait(dve, cos_part, s)
                        wait(dve, sin_part, s)
                        rr = heads(r, 2 * G)[:, :, 0:ROT]
                        nc.vector.tensor_tensor(rr, rr, heads(rot_part, 2 * G), ALU.add).then_inc(rotated, 1)
                    if g == ST - 1 and has(s0, 0, ST):
                        wait(dve, o_ready, t)
                        wait(dve, res_loaded, t * 16)
                        nc.vector.tensor_tensor(h_sb, bank_o[:, 0:D], x_res, ALU.add).then_inc(h_summed, 1)
                        wait(dve, h_summed, t)
                        nc.vector.bn_stats(bn, h_sb).then_inc(h_stats, 1)
                        wait(dve, h_stats, t)
                        carry(nc, stats)
                        nc.vector.bn_aggr(mv, bn).then_inc(h_mv, 1)
                    if has(s0, g, 2):
                        sc = heads(bank_s[:, 0:G * NK], G)
                        wait(dve, scored, s - 1)
                        wait(dve, exped, s - 2)
                        nc.vector.tensor_reduce(mx[:, 0:G], sc[:, :, 0:S], AX_X, ALU.max)
                        nc.vector.tensor_reduce(mx[:, G:2 * G], sc[:, :, S:NK], AX_X, ALU.max).then_inc(maxed, 1)
                        wait(dve, maxed, s - 1)
                        nc.vector.tensor_tensor(shifted[:, :, 0:S], sc[:, :, 0:S], over(mx[:, 0:G], S), ALU.subtract)
                        nc.vector.tensor_tensor(shifted[:, :, S:NK], sc[:, :, S:NK], over(mx[:, G:2 * G], NC + 1),
                                                ALU.subtract).then_inc(s_shifted, 1)
                    if has(s0, g, 0):
                        if isinstance(t, int) and t == 0 and g < 2:
                            dve.wait_ge(bias_loaded[g], 32 if g == 0 else 32 * (ST - 1))
                        wait(dve, squared, s)
                        wait(dve, sin_part, s)
                        wait(dve, q_proj, s + 1)
                        nc.vector.tensor_tensor(qk_b[:, 0:GW], bank_q[:, :], mem["qk_bias"][:, 0, g * GW:(g + 1) * GW],
                                                ALU.add).then_inc(q_biased, 1)
                        wait(dve, k_proj, s + 1)
                        nc.vector.tensor_tensor(qk_b[:, GW:2 * GW], bank_k[:, :], mem["qk_bias"][:, 1, g * GW:(g + 1) * GW],
                                                ALU.add).then_inc(k_biased, 1)
                    if has(s0, g, 2):
                        gg = (g + 2) % ST
                        wait(dve, exped, s - 1)
                        nc.vector.tensor_reduce(sums[:, 0:G], e_sb[:, :, 0:S], AX_X, ALU.add)
                        nc.vector.tensor_reduce(sums[:, G:2 * G], e_sb[:, :, S:NK], AX_X, ALU.add).then_inc(e_summed, 1)
                        wait(dve, e_summed, s - 1)
                        nc.vector.reciprocal(rsums, sums).then_inc(e_recip, 1)
                        wait(dve, e_recip, s - 1)
                        wait(dve, p_turned, s - 2)
                        nc.vector.tensor_tensor(heads(p_loc, G), e_sb[:, :, 0:S], over(rsums[:, 0:G], S), ALU.mult)
                        if gg == 0:
                            wait(dve, pc_turned, t)
                        nc.vector.tensor_tensor(p_comp[:, gg * G * NC:(gg + 1) * G * NC].rearrange("p (h c) -> p h c", h=G),
                                                e_sb[:, :, S:S + NC], over(rsums[:, G:2 * G], NC), ALU.mult)
                        nc.vector.tensor_tensor(p_comp[:, PC + gg * G:PC + (gg + 1) * G].unsqueeze(2), e_sb[:, :, NK - 1:NK],
                                                rsums[:, G:2 * G].unsqueeze(2), ALU.mult).then_inc(probs, 1)
                    if g == ST - 1 and has(s0, 0, ST):
                        wait(dve, rstd_ready, t)
                        dst = x1[:, t - 1, :] if isinstance(t, int) else x1[:, bass.ds(t - 1, 1), :].squeeze(1)
                        nc.vector.tensor_scalar(dst, h_sb, mv[:, 0:1], rstd, ALU.subtract, ALU.mult).then_inc(x1_ready, 1)

            tiles(dve, tile)
            wait(dve, x1_ready, TILES)

        @block.gpsimd
        def _(pool):
            pool.dma_start(ctx_sink := p_comp[:, 0:NH], a["sink_kT"]).then_inc(sinks_placed, 16)
            pool.wait_ge(sinks_placed, 16)
            for k in range(ST):
                for b in range(2):
                    nc.gpsimd.tensor_copy(kT[k][:, :, b, NK - 1:NK], ctx_sink[:, k * G:(k + 1) * G].unsqueeze(2)).then_inc(zeroed, 1)

            def tile(t, s0):
                for g in range(ST):
                    s = s0 + g
                    if has(s0, g, 1):
                        wait(pool, scored, s - ST)
                        wait(pool, q_biased, s)
                        wait(pool, k_biased, s)
                        wait(pool, rotated, s - 1)
                        src = qk_b.rearrange("p (i h d) -> p i h d", i=2, h=G)
                        part = rot_part.rearrange("p (i h d) -> p i h d", i=2, h=G)
                        for i in range(2):
                            last = nc.gpsimd.tensor_tensor(
                                halves(part[:, i]), halves(src[:, i, :, 0:ROT])[:, :, ::-1, :],
                                mem["rot_s"][:, i, :].rearrange("p (a b) -> p a b", a=2).unsqueeze(1)
                                .to_broadcast([P, G, 2, HALF]), ALU.mult)
                        last.then_inc(sin_part, 1)
                        wait(pool, inv_ready, s - 1)
                        wait(pool, summed_sq, s)
                        nc.gpsimd.tensor_tensor(ms, ss, rms_eps, ALU.add).then_inc(ms_ready, 1)
                        wait(pool, ms_ready, s)
                        wait(pool, normed, s - 1)
                        nc.gpsimd.tensor_tensor(inv, ms, neg_half, ALU.pow).then_inc(inv_ready, 1)
                        wait(pool, inv_ready, s)
                        wait(pool, rotated, s)
                        r = heads(rot[(g + 1) % 2], 2 * G)
                        nc.gpsimd.tensor_tensor(r, r, over(inv, HD), ALU.mult).then_inc(normed, 1)
                    if g == ST - 1 and has(s0, 0, ST):
                        rsqrt_var(t - 1)
                    if has(s0, g, 1):
                        gg = (g + ST - 1) % ST
                        tt = t if g else t - 1
                        src = (ckT_at(tt)).rearrange("p (b c) -> p b c", b=2)
                        for j in range(G):
                            last = nc.gpsimd.tensor_copy(kT[gg][:, j, :, S:S + NC], src)
                        last.then_inc(ck_placed, 1)

            def ckT_at(t):
                return mem["ckT"][:, t * 2 * NC:(t + 1) * 2 * NC] if isinstance(t, int) else mem["ckT"][:, bass.ds(t * (2 * NC), 2 * NC)]

            def rsqrt_var(t):
                wait(pool, h_mv, t + 1)
                nc.gpsimd.tensor_tensor(var_eps, mv[:, 1:2], ln_eps, ALU.add).then_inc(var_ready, 1)
                wait(pool, var_ready, t + 1)
                nc.gpsimd.tensor_tensor(rstd, var_eps, neg_half[:, 0:1], ALU.pow).then_inc(rstd_ready, 1)

            tiles(pool, tile)


def mixing(nc, a, mem, psum):
    arena, x1, ident = mem["arena"], mem["x1"], mem["ident"]
    v_all = arena[:, 0:TILES * D].rearrange("p (t d) -> p t d", t=TILES)
    x1T = arena[:, TILES * D:2 * TILES * D].rearrange("p (t d) -> p t d", t=TILES)
    low = arena[:, 2 * TILES * D:ARENA]
    mixT = low[:, 0:RH * P].rearrange("p (h q) -> p h q", h=RH)
    cursor = [RH * P]

    def carve(n):
        cursor[0] += n
        assert cursor[0] <= ARENA - 2 * TILES * D
        return low[:, cursor[0] - n:cursor[0]]

    gT = [carve(D) for _ in range(2)]
    cT = [carve(RING * D).rearrange("p (h n) -> p h n", h=RH) for _ in range(2)]
    gram, wh = mem["gram"], mem["wh"]
    decay = carve(RH * S)
    mix = carve(RH * S)
    zero = carve(P).bitcast(BF16)
    assert cursor[0] <= FFN_KEPT0
    raw = raw_weights(mem)
    wd_raw = mem["wo"][:, :, :]
    gu, wd = ffn_weights(mem)
    select = mem["select"]
    sel_raw = x1T[0:PARTS * NE, 10:TILES, :].rearrange("p t d -> p (t d)")[:, 0:ET * P]
    wo_w, gamma, beta, wr, before = ffn_small(mem)
    b_xg = [psum[:, i * 512:(i + 1) * 512] for i in range(2)]
    b_v = [psum[:, (2 + i) * 512:(2 + i) * 512 + D] for i in range(2)]
    b_s = psum[:, 6 * 512:7 * 512]

    with ExitStack() as ctx:
        def sem(name):
            return ctx.enter_context(nc.semaphore(name))

        cT_loaded = [sem(f"cT_loaded{i}") for i in range(2)]
        xg_ready, v_ready, xg_copied, v_stored = sem("xg_ready"), sem("v_ready"), sem("xg_copied"), sem("v_stored")
        s_added = sem("s_added")
        decay_loaded, zeroed, sel_loaded, sel_ready = sem("decay_loaded"), sem("mix_zeroed"), sem("sel_loaded"), sem("sel_ready")
        s_closed, decayed, mix_ready = sem("s_closed"), sem("decayed"), sem("mix_ready")
        raw_loaded, ffn_hi, ffn_lo, wd_loaded = mem["raw_loaded"], sem("ffn_hi"), sem("ffn_lo"), sem("wd_loaded")
        wd_hi_ready, wd_rest, small_loaded = sem("wd_hi_ready"), sem("wd_rest"), sem("small_loaded")
        block = ctx.enter_context(nc.Block())

        quarter = {t0 + q: (kind, q) for kind, t0 in (("gate", 0), ("down", 5), ("up", 10)) for q in range(4)}

        def buffer(t):
            return first_ctx(mem) if t == 0 else cT[t // RING % 2][:, :, t % RING * P:(t % RING + 1) * P]

        def quarter_of(kind, part, q):
            if kind == "down":
                v = wd_raw if part is None else wd[:, part]
                return v[:, q * WD_PIECE:(q + 1) * WD_PIECE, :]
            v = raw if part is None else gu[:, int(kind == "up"), part]
            return v[:, q // 2, q % 2 * FALL // 2:(q % 2 + 1) * FALL // 2]

        @block.sync
        def _(sp):
            cTv = a["ctxT"].rearrange("(h p) n -> p h n", p=P)

            def load(t0, n):
                sp.dma_start(cT[t0 // RING % 2][:, :, t0 % RING * P:(t0 % RING + n) * P],
                             cTv[:, :, t0 * P:(t0 + n) * P]).then_inc(cT_loaded[t0 // RING % 2], 16)

            def down(f0, f1):
                sp.dma_start(wd_raw[:, f0:f1, :], a["down"][f0 * P:f1 * P, :].rearrange("(f p) n -> p f n", p=P)).then_inc(wd_loaded, 16)

            load(1, RING - 1)
            sp.dma_start(sel_raw, a["select"]).then_inc(sel_loaded, 16)
            load(RING, RING)
            down(0, 6)
            down(6, FT - 1)
            sp.dma_start(wd_raw[0:rows(FT - 1), FT - 1, :], a["down"][(FT - 1) * P:FALL, :]).then_inc(wd_loaded, 16)
            sp.wait_ge(v_ready, RING)
            load(2 * RING, RING)
            for k in range(KD):
                sp.wait_ge(ffn_lo, 2 * (k + 1))
                load_raw(sp, a, mem, "upT", k)
            sp.wait_ge(v_ready, 2 * RING)
            load(3 * RING, RING)
            sp.dma_start(decay[0:S, :], a["decay"]).then_inc(decay_loaded, 16)
            for dst, src in ((wo_w, a["wo_w"].rearrange("(k p) n -> p k n", p=P)), (gamma, a["gn_gamma"].partition_broadcast(P)),
                             (beta, a["gn_beta"].partition_broadcast(P)), (wr, a["WrT"].rearrange("(k p) e -> p k e", p=P)),
                             (before, a["before"].partition_broadcast(P))):
                sp.dma_start(dst, src).then_inc(small_loaded, 16)
            sp.wait_ge(small_loaded, 16 * 5)

        @block.tensor
        def _(pe):
            pe.wait_ge(mem["wg_loaded"], 32)
            pe.wait_ge(zeroed, 2)
            nc.tensor.matmul(b_s[0:S, 0:RH * S], zero[:, 0:S], zero[:, 0:RH * S], start=True, stop=False)

            for t in range(TILES + 1):
                i = t % 2
                if t < TILES:
                    wait(pe, xg_copied, t - 1)
                    for k in range(KD):
                        nc.tensor.transpose(b_xg[i][:, k * P:(k + 1) * P], x1[:, t, k * P:(k + 1) * P], ident[:, :])
                    if t == 0:
                        pe.wait_ge(mem["ctx_loaded"], 16)
                    else:
                        pe.wait_ge(cT_loaded[t // RING % 2], 16 * (t // (2 * RING) + 1))
                    for h in range(RH):
                        last = nc.tensor.matmul(b_xg[i][:, D + h * P:D + (h + 1) * P], gram[:, h, :], buffer(t)[:, h, :],
                                                start=True, stop=True)
                    last.then_inc(xg_ready, 1)
                    wait(pe, v_stored, t - 1)
                    for h in range(RH):
                        last = nc.tensor.matmul(b_v[i][:, h * HD:(h + 1) * HD], buffer(t)[:, h, :], wh[:, h, :],
                                                start=True, stop=True)
                    last.then_inc(v_ready, 1)
                if t > 0:
                    wait(pe, xg_copied, t)
                    for b in range(2):
                        for h in range(RH):
                            c = h * P + b * S
                            last = nc.tensor.matmul(b_s[0:S, h * S:(h + 1) * S], gT[1 - i][:, c:c + S], x1T[:, t - 1, c:c + S],
                                                    start=False, stop=False)
                    last.then_inc(s_added, 1)
            nc.tensor.matmul(b_s[0:S, 0:RH * S], zero[:, 0:S], zero[:, 0:RH * S], start=False, stop=True).then_inc(s_closed, 1)

        @block.scalar
        def _(act):
            for t in range(TILES):
                kind, q = quarter.get(t, (None, 0))
                if kind in ("gate", "up"):
                    act.wait_ge(raw_loaded, 16 * KD * (1 if kind == "gate" else 2))
                    nc.scalar.activation(quarter_of(kind, 0, q), quarter_of(kind, None, q), ACT.Copy).then_inc(ffn_hi, 1)
                wait(act, xg_ready, t + 1)
                if t == 10:
                    act.wait_ge(sel_ready, 1)
                nc.scalar.activation(x1T[:, t, :], b_xg[t % 2][:, 0:D], ACT.Copy)
                wait(act, s_added, t - 1)
                nc.scalar.activation(gT[t % 2], b_xg[t % 2][:, D:2 * D], ACT.Copy).then_inc(xg_copied, 1)
            act.wait_ge(mix_ready, 1)
            for h in range(RH):
                for b in range(2):
                    nc.scalar.activation(mixT[b * S:(b + 1) * S, h, b * S:(b + 1) * S], mix[0:S, h * S:(h + 1) * S], ACT.Copy)

        @block.vector
        def _(dve):
            nc.vector.memset(mixT, 0.0).then_inc(zeroed, 1)
            nc.vector.memset(zero, 0.0).then_inc(zeroed, 1)

            for t in range(TILES):
                wait(dve, v_ready, t + 1)
                nc.vector.tensor_copy(v_all[:, t, :], b_v[t % 2]).then_inc(v_stored, 1)
                kind, q = quarter.get(t, (None, 0))
                if kind == "down":
                    dve.wait_ge(wd_loaded, 48)
                    nc.vector.tensor_copy(quarter_of(kind, 0, q), quarter_of(kind, None, q)).then_inc(wd_hi_ready, 1)
                elif kind is not None:
                    dve.wait_ge(ffn_hi, q + 1 + 4 * (kind == "up"))
                    nc.vector.tensor_tensor(quarter_of(kind, 1, q), quarter_of(kind, None, q),
                                            quarter_of(kind, 0, q).bitcast(F32), ALU.subtract).then_inc(ffn_lo, 1)
            dve.wait_ge(s_closed, 1)
            dve.wait_ge(decay_loaded, 16)
            nc.vector.tensor_tensor(mix[0:S, :], b_s[0:S, 0:RH * S], decay[0:S, :], ALU.mult).then_inc(decayed, 1)
            dve.wait_ge(decayed, 1)
            nc.vector.scalar_tensor_tensor(out=mix[0:S, :], in0=mix[0:S, :], scalar=-1.0, in1=mix[0:S, :], op0=ALU.mult,
                                           op1=ALU.max).then_inc(decayed, 1)
            dve.wait_ge(decayed, 2)
            nc.vector.tensor_scalar(mix[0:S, :], mix[0:S, :], 1.0, None, ALU.max).then_inc(mix_ready, 1)
            dve.wait_ge(v_stored, TILES)

        @block.gpsimd
        def _(pool):
            pool.wait_ge(sel_loaded, 16)
            nc.gpsimd.tensor_copy(select[0:PARTS * NE, :], sel_raw).then_inc(sel_ready, 1)
            pool.wait_ge(wd_loaded, 48)
            rest = (slice(0, P), slice(4 * WD_PIECE, FT - 1)), (slice(0, rows(FT - 1)), slice(FT - 1, FT))
            for n, (p, f) in enumerate(rest):
                nc.gpsimd.tensor_copy(wd[p, 0, f], wd_raw[p, f]).then_inc(wd_rest, 1)
                pool.wait_ge(wd_rest, n + 1)
                nc.gpsimd.tensor_tensor(wd[p, 1, f], wd_raw[p, f], wd[p, 0, f].bitcast(F32), ALU.subtract)
            for q in range(4):
                pool.wait_ge(wd_hi_ready, q + 1)
                nc.gpsimd.tensor_tensor(quarter_of("down", 1, q), quarter_of("down", None, q),
                                        quarter_of("down", 0, q).bitcast(F32), ALU.subtract)


def raw_weights(mem):
    flat = mem["qk_bias"][:, :, :].rearrange("p i n -> p (i n)")
    return flat[:, 0:KD * FALL].rearrange("p (k n) -> p k n", k=KD)


def load_raw(eng, a, mem, name, k):
    eng.dma_start(raw_weights(mem)[:, k, :], a[name][k * P:(k + 1) * P, :]).then_inc(mem["raw_loaded"], 16)


RING = 4
WD_PIECE = 3
FFN_KEPT0 = 3328


def ffn_weights(mem):
    flat = mem["w_split"][:, :, :, :, :].rearrange("p i j k n -> p (i j k n)")
    return (flat[:, 0:4 * KD * FALL].rearrange("p (i j k n) -> p i j k n", i=2, j=2, k=KD),
            flat[:, 4 * KD * FALL:4 * KD * FALL + 2 * FT * D].rearrange("p (j f n) -> p j f n", j=2, f=FT))


def ffn_small(mem):
    flat = mem["arena"][:, 2 * TILES * D + FFN_KEPT0:ARENA]
    return (flat[:, 0:KD * D].rearrange("p (k n) -> p k n", k=KD), flat[:, 2 * D:3 * D], flat[:, 3 * D:4 * D],
            mem["ckT"][:, 0:KD * NE].rearrange("p (k e) -> p k e", k=KD),
            mem["rot_c"][:, 0, 0:NE * NE].rearrange("p (e j) -> p e j", e=NE))


def feed_forward(nc, a, mem, psum, out):
    arena, x1, ident, stats = mem["arena"], mem["x1"], mem["ident"], mem["stats"]
    v_all = arena[:, 0:TILES * D].rearrange("p (t d) -> p t d", t=TILES)
    w_all = arena[:, TILES * D:2 * TILES * D].rearrange("p (t d) -> p t d", t=TILES)
    low = arena[:, 2 * TILES * D:ARENA]
    mixT = low[:, 0:RH * P].rearrange("p (h q) -> p h q", h=RH)
    cursor = [RH * P]

    def carve(n):
        cursor[0] += n
        assert cursor[0] <= ARENA - 2 * TILES * D
        return low[:, cursor[0] - n:cursor[0]]

    x2n = carve(CH * D)
    sil = carve(CT)
    hid = [carve(CT) for _ in range(2)]
    rank = [carve(CH * NE * NE) for _ in range(2)]
    assert cursor[0] <= FFN_KEPT0
    wo_w, gamma, beta, wr, before = ffn_small(mem)
    flat = mem["qk_bias"][:, :, :].rearrange("p i n -> p (i n)")
    y = flat[:, 0:CH * D]
    turned = flat[:, CH * D:2 * CH * D]
    h3 = flat[:, 2 * CH * D:3 * CH * D]
    x2c = flat[:, 3 * CH * D:4 * CH * D]
    gu, wd = ffn_weights(mem)
    rflat = mem["w_split"][:, :, :, :, :].rearrange("p i j k n -> p (i j k n)")[:, 4 * KD * FALL + 2 * FT * D:]
    x2_hi = rflat[:, 0:KD * CT].rearrange("p (k n) -> p k n", k=KD)
    x2_lo = rflat[:, KD * CT:2 * KD * CT].rearrange("p (k n) -> p k n", k=KD)
    hid_hi = [rflat[:, (2 * KD + i) * CT:(2 * KD + i + 1) * CT] for i in range(2)]
    hid_lo = mem["x_parts"][:, :, :, :].rearrange("p j k n -> p (j k n)")
    select, wg = mem["select"], mem["wg"]
    zero = mem["rot_c"][:, 1, 0:64].bitcast(BF16)
    zeros = mem["sink_rows"][:, :].bitcast(BF16)
    score = mem["rot_s"][:, 0, 0:CH * NE].rearrange("p (t e) -> p t e", t=CH)
    ranks = mem["rot_s"][:, 0, 32:32 + CH * NE].rearrange("p (t e) -> p t e", t=CH)
    rest = mem["rot_s"][:, 1, 0:CH * NE].rearrange("p (t e) -> p t e", t=CH)
    parts = mem["maskb"][:, 0:CH * PARTS * NE].rearrange("p (t c e) -> p t c e", t=CH, c=PARTS)
    wT_b = mem["w_parts"][0:PARTS * NE, :]
    smax, ssum, srec = stats[:, 8:12], stats[:, 12:16], stats[:, 16:20]
    bn = [stats[:, 20 + 6 * j:26 + 6 * j] for j in range(CH)]
    mv = stats[:, 44:52].rearrange("p (t c) -> p t c", t=CH)
    ve, rstd = stats[:, 52:56], stats[:, 56:60]
    bn3 = [stats[:, 60 + 6 * j:66 + 6 * j] for j in range(CH)]
    mv3 = stats[:, 84:92].rearrange("p (t c) -> p t c", t=CH)
    ve3, rstd3 = stats[:, 92:96], stats[:, 96:100]
    neg_half = stats[:, 0:CH]
    ln_eps, gn_eps = stats[:, 112:113], stats[:, 113:114]
    b_u, b_w = [psum[:, i * 512:(i + 1) * 512] for i in (1, 2)]
    b_g = [psum[:, i * 512:(i + 1) * 512] for i in (0, 7)]
    b_acc = psum[:, 3 * 512:5 * 512]
    b_f = psum[:, 5 * 512:7 * 512]
    b_r = psum[:, 5 * 512:6 * 512]
    b_gate = [psum[:, i * 512:(i + 1) * 512] for i in range(4)]

    def tok(ap):
        return ap.rearrange("p (t d) -> p t d", t=CH)

    with ExitStack() as ctx:
        def sem(name):
            return ctx.enter_context(nc.semaphore(name))

        g_ready, u_ready, w_ready = sem("g_ready"), sem("u_ready"), sem("wsel_ready")
        silued, gated, hid_ready, down_done = sem("silued"), sem("gated"), sem("hid_ready"), sem("down_done")
        o_ready, o_stats, o_mv, o_var, o_rstd, o_normed = [sem("f_" + n) for n in ("o_ready", "o_stats", "o_mv", "o_var", "o_rstd", "o_normed")]
        scaled, biased, wy_ready, wy_turned, wyT_copied, mixed = [sem("f_" + n) for n in ("scaled", "biased", "wy_ready", "wy_turned", "wyT_copied", "mixed")]
        h_ready, h_stats, h_mv, h_var, h_rstd, x2_ready = [sem("f_" + n) for n in ("h_ready", "h_stats", "h_mv", "h_var", "h_rstd", "x2_ready")]
        x2_turned, x2T_copied, logits, maxed, less, exped = [sem("f_" + n) for n in ("x2_turned", "x2T_copied", "logits", "maxed", "less", "exped")]
        parts_ready, parts_turned, wT_ready, own = [sem("f_" + n) for n in ("parts_ready", "parts_turned", "wT_ready", "own")]
        high, split, cur_copied = sem("f_high"), sem("f_split"), sem("f_cur_copied")
        acc_ready, h3_ready, h3_stats, h3_mv, h3_var, h3_rstd, y3_ready, stored = [
            sem("t_" + n) for n in ("acc_ready", "h3_ready", "h3_stats", "h3_mv", "h3_var", "h3_rstd", "y3_ready", "stored")]
        zeroed, hid_high, hid_made = sem("f_zeroed"), sem("hid_high"), sem("hid_made")
        gate_ready, gate_stored = sem("gate_ready"), sem("gate_stored")
        block = ctx.enter_context(nc.Block())

        def nothing(i, c):
            pass

        def gates(f, i, do):
            if isinstance(f, int) and f == 0:
                for pair in {0: range(6), 5: range(6, TILES // 2)}.get(i, ()):
                    do(pair)

        def chunks(eng, front=nothing, slot=nothing, turn=lambda f: None, back=nothing,
                   last=lambda: None):
            for i in range(FT):
                front(i, 0)
                if i == 7:
                    turn(0)

            def both(c):
                for i in range(FT):
                    slot(c, i)
                    if not isinstance(c, int):
                        back(i, c - 1)
                    front(i, c + 1)
            both(0)
            with eng.Fori(1, CHUNKS - 1) as c:
                both(c)
            for i in range(FT):
                slot(CHUNKS - 1, i)
                back(i, CHUNKS - 2)
            slot(CHUNKS, 0)
            last()

        def c_past(c, i, lag):
            return not isinstance(c, int) or c > 0 or i >= lag

        def part(view, f):
            return view[:, f * CH:(f + 1) * CH, :] if isinstance(f, int) else view[:, bass.ds(f * CH, CH), :]

        @block.sync
        def _(sp):
            o = out.rearrange("(c t p) d -> c p t d", t=CH, p=P)

            def store(c):
                wait(sp, y3_ready, c + 1)
                dst = o[c] if isinstance(c, int) else o[bass.ds(c, 1)][0]
                sp.dma_start(dst, tok(h3)).then_inc(stored, 16)
            with sp.Fori(0, CHUNKS - 1) as c:
                store(c)
            for half in range(2):
                tiles = slice(half * CH // 2, (half + 1) * CH // 2)
                sp.wait_ge(y3_ready, CHUNKS + half)
                sp.dma_start(o[CHUNKS - 1][:, tiles, :], tok(h3)[:, tiles, :]).then_inc(stored, 16)
            sp.wait_ge(stored, 16 * (CHUNKS + 1))

        @block.tensor
        def _(pe):
            pe.wait_ge(zeroed, 1)

            def gate(pair):
                wait(pe, gate_stored, pair - 3)
                for t in range(2):
                    for k in range(KD):
                        last = nc.tensor.matmul(b_gate[pair % 4][:, t * D:(t + 1) * D], w_all[:, 2 * pair + t, k * P:(k + 1) * P],
                                                wg[:, k, :], start=k == 0, stop=k == KD - 1)
                last.then_inc(gate_ready, 1)

            def front(i, f):
                if i == 0:
                    wait(pe, x2T_copied, f)
                    wait(pe, wT_ready, f)
                    for h in range(RH):
                        last = nc.tensor.matmul(b_f[:, h * 512:(h + 1) * 512].rearrange("p (t e) -> p t e", t=CH), mixT[:, h, :],
                                                part(v_all, f)[:, :, h * HD:(h + 1) * HD], start=True, stop=True)
                    last.then_inc(o_ready, 1)
                if i == 4:
                    wait(pe, wy_ready, f + 1)
                    wait(pe, o_normed, f + 1)
                    for k in range(KD):
                        for t in range(CH):
                            last = nc.tensor.transpose(b_f[:, k * CT + t * P:k * CT + (t + 1) * P],
                                                       y[:, t * D + k * P:t * D + (k + 1) * P], ident[:, :])
                    last.then_inc(wy_turned, 1)
                if i == 5:
                    wait(pe, wyT_copied, f + 1)
                    for t in range(CH):
                        for k in range(KD):
                            last = nc.tensor.matmul(b_f[:, t * D:(t + 1) * D], turned[:, k * CT + t * P:k * CT + (t + 1) * P],
                                                    wo_w[:, k, :], start=k == 0, stop=k == KD - 1)
                    last.then_inc(mixed, 1)
                gates(f, i, gate)
                if i == 7:
                    wait(pe, x2_ready, f + 1)
                    wait(pe, h_ready, f + 1)
                    for k in range(KD):
                        for t in range(CH):
                            last = nc.tensor.transpose(b_f[:, k * CT + t * P:k * CT + (t + 1) * P],
                                                       x2n[:, t * D + k * P:t * D + (k + 1) * P], ident[:, :])
                    last.then_inc(x2_turned, 1)
                if i == 8:
                    wait(pe, x2T_copied, f + 1)
                    for t in range(CH):
                        for k in range(KD):
                            last = nc.tensor.matmul(b_r[:, t * NE:(t + 1) * NE], turned[:, k * CT + t * P:k * CT + (t + 1) * P],
                                                    wr[:, k, :], start=k == 0, stop=k == KD - 1)
                    last.then_inc(logits, 1)
                if i == 12 and not (isinstance(f, int) and f == 0):
                    turn_parts(f)

            def turn_parts(f):
                wait(pe, parts_ready, f + 1)
                for t in range(CH):
                    last = nc.tensor.transpose(b_rb[0:PARTS * NE, t * P:(t + 1) * P],
                                               parts[:, t].rearrange("p c e -> p (c e)"), mem["identb"][:, :])
                last.then_inc(parts_turned, 1)

            b_rb = b_r[:, 0:CT // 2].bitcast(BF16)

            def down(c, i):
                n = rows(i)
                wait(pe, hid_ready, c * FT + (i + 1))
                for t in range(CH):
                    for hs, p in ((hid_hi[i % 2], 0), (hid_lo, 0), (hid_hi[i % 2], 1)):
                        last = nc.tensor.matmul(b_acc[:, t * D:(t + 1) * D], hs[0:n, t * P:(t + 1) * P], wd[0:n, p, i, :],
                                                start=False, stop=False)
                last.then_inc(down_done, 1)

            def close(c):
                down(c, FT - 1)
                for k in range(2):
                    last = nc.tensor.matmul(b_acc[:, k * 512:(k + 1) * 512], zero[:, 0:P], zeros[:, :], start=False, stop=True)
                last.then_inc(acc_ready, 1)

            def slot(c, i):
                if isinstance(c, int) and c == CHUNKS:
                    close(c - 1)
                    return
                n = rows(i)
                cols = slice(i * P, i * P + n)
                if i == 0:
                    if isinstance(c, int) and c == 0:
                        pe.wait_ge(gate_stored, TILES // 2)
                for which, bk, free, ago, done in ((0, b_g[i % 2], silued, 1, g_ready), (1, b_u, gated, 0, u_ready)):
                    if c_past(c, i, ago + 1):
                        wait(pe, free, c * FT + (i - ago))
                    m = 0
                    for k in range(KD):
                        if i == 0 and which == 0:
                            wait(pe, split, c * KD + (k + 1))
                        for xs, p in ((x2_hi, 0), (x2_lo, 0), (x2_hi, 1)):
                            last = nc.tensor.matmul(bk[0:n, :], gu[:, which, p, k, cols], xs[:, k, :], start=m == 0, stop=m == 5)
                            m += 1
                    last.then_inc(done, 1)
                if i < ET:
                    if i == 0:
                        if isinstance(c, int) and c == 0:
                            turn_parts(0)
                        wait(pe, wT_ready, c + 1)
                    wait(pe, hid_made, c * FT + i)
                    nc.tensor.matmul(b_w[:, :], select[0:PARTS * NE, i * P:(i + 1) * P], wT_b, start=True,
                                     stop=True).then_inc(w_ready, 1)
                if i == 0:
                    if not isinstance(c, int) or c > 0:
                        close(c - 1)
                else:
                    if i == 1:
                        wait(pe, h3_ready, c)
                        for k in range(2):
                            nc.tensor.matmul(b_acc[:, k * 512:(k + 1) * 512], zero[:, 0:P], zeros[:, :], start=True, stop=False)
                    down(c, i - 1)

            chunks(pe, front, slot)

        @block.scalar
        def _(act):
            def gate(pair):
                act.wait_ge(gate_ready, pair + 1)
                nc.scalar.activation(w_all[:, 2 * pair:2 * pair + 2, :].rearrange("p t d -> p (t d)"), b_gate[pair % 4],
                                     ACT.Relu).then_inc(gate_stored, 1)

            def front(i, f):
                if i == 4:
                    wait(act, wy_turned, f + 1)
                    wait(act, split, f * KD)
                    nc.scalar.activation(turned, b_f, ACT.Copy).then_inc(wyT_copied, 1)
                gates(f, i, gate)
                if i == 7:
                    wait(act, x2_turned, f + 1)
                    wait(act, mixed, f + 1)
                    nc.scalar.activation(turned, b_f, ACT.Copy).then_inc(x2T_copied, 1)
                if i == 9:
                    wait(act, less, f + 1)
                    nc.scalar.activation(score, score, ACT.Exp).then_inc(exped, 1)

            def slot(c, i):
                if isinstance(c, int) and c == CHUNKS:
                    return
                n = rows(i)
                wait(act, g_ready, c * FT + (i + 1))
                wait(act, gated, c * FT + i)
                nc.scalar.activation(sil[0:n, :], b_g[i % 2][0:n, :], ACT.Silu).then_inc(silued, 1)
                if i == FT - 1 and not (isinstance(c, int) and c == CHUNKS - 1):
                    turn(c + 1)
                wait(act, hid_made, c * FT + (i + 1))
                if c_past(c, i, 2):
                    wait(act, down_done, c * FT + (i - 1))
                nc.scalar.activation(hid_hi[i % 2][0:n, :], hid[i % 2][0:n, :], ACT.Copy).then_inc(hid_high, 1)
                if i == 0:
                    wait(act, h3_ready, c)
                    wait(act, x2_ready, c + 1)
                    nc.scalar.activation(x2c, x2n, ACT.Copy).then_inc(cur_copied, 1)

            def turn(f):
                wait(act, u_ready, f * FT)
                wait(act, x2T_copied, f + 1)
                for k in range(KD):
                    nc.scalar.activation(x2_hi[:, k, :], turned[:, k * CT:(k + 1) * CT], ACT.Copy).then_inc(high, 1)

            chunks(act, front, slot, turn)

        @block.vector
        def _(dve):
            nc.vector.memset(zeros, 0.0)
            nc.vector.memset(zero, 0.0).then_inc(zeroed, 1)
            OWN = 13
            count = [0]

            def front(i, f):
                if i == 0:
                    wait(dve, o_ready, f + 1)
                    o = b_f.rearrange("p (h t e) -> p h t e", h=RH, t=CH)
                    for t in range(CH):
                        last = nc.vector.bn_stats(bn[t], o[:, :, t, :])
                    last.then_inc(o_stats, 1)
                    wait(dve, o_stats, f + 1)
                    carry(nc, stats)
                    for t in range(CH):
                        last = nc.vector.bn_aggr(mv[:, t, :], bn[t])
                    last.then_inc(o_mv, 1)
                first = isinstance(f, int) and f == 0
                if i == 1:
                    wait(dve, o_rstd, f + 1)
                    o = b_f.rearrange("p (h t e) -> p h t e", h=RH, t=CH)
                    for t in range(CH):
                        last = nc.vector.tensor_scalar(y[:, t * D:(t + 1) * D].rearrange("p (h e) -> p h e", h=RH), o[:, :, t, :],
                                                       mv[:, t, 0:1], rstd[:, t:t + 1], ALU.subtract, ALU.mult)
                    last.then_inc(o_normed, 1)
                    if first:
                        dve.wait_ge(o_normed, 1)
                        nc.vector.tensor_tensor(tok(y), tok(y), gamma.unsqueeze(1).to_broadcast([P, CH, D]), ALU.mult).then_inc(scaled, 1)
                        dve.wait_ge(scaled, 1)
                        nc.vector.tensor_tensor(tok(y), tok(y), beta.unsqueeze(1).to_broadcast([P, CH, D]), ALU.add).then_inc(biased, 1)
                if i == 3:
                    wait(dve, biased, f + 1)
                    dve.wait_ge(gate_stored, CH // 2 if first else TILES // 2)
                    nc.vector.tensor_tensor(tok(y), tok(y), part(w_all, f), ALU.mult).then_inc(wy_ready, 1)
                if i == 5:
                    wait(dve, mixed, f + 1)
                    wait(dve, wy_turned, f + 1)
                    nc.vector.tensor_tensor(tok(y), tok(b_f), part(x1, f), ALU.add).then_inc(h_ready, 1)
                    wait(dve, h_ready, f + 1)
                    for t in range(CH):
                        last = nc.vector.bn_stats(bn[t], y[:, t * D:(t + 1) * D])
                    last.then_inc(h_stats, 1)
                    wait(dve, h_stats, f + 1)
                    carry(nc, stats)
                    for t in range(CH):
                        last = nc.vector.bn_aggr(mv[:, t, :], bn[t])
                    last.then_inc(h_mv, 1)
                if i == 6:
                    wait(dve, h_rstd, f + 1)
                    wait(dve, cur_copied, f)
                    for t in range(CH):
                        last = nc.vector.tensor_scalar(x2n[:, t * D:(t + 1) * D], y[:, t * D:(t + 1) * D], mv[:, t, 0:1],
                                                       rstd[:, t:t + 1], ALU.subtract, ALU.mult)
                    last.then_inc(x2_ready, 1)
                if i == 8:
                    lg = b_r[:, 0:CH * NE].rearrange("p (t e) -> p t e", t=CH)
                    wait(dve, logits, f + 1)
                    nc.vector.tensor_reduce(smax, lg, AX_X, ALU.max).then_inc(maxed, 1)
                    wait(dve, maxed, f + 1)
                    nc.vector.tensor_tensor(score, lg, over(smax, NE), ALU.subtract).then_inc(less, 1)
                def link(ins):
                    count[0] += 1
                    ins.then_inc(own, 1)
                    wait(dve, own, f * OWN + count[0])

                if i == 10:
                    count[0] = 0
                    wait(dve, exped, f + 1)
                    link(nc.vector.tensor_reduce(ssum, score, AX_X, ALU.add))
                    link(nc.vector.reciprocal(srec, ssum))
                    link(nc.vector.tensor_tensor(score, score, over(srec, NE), ALU.mult))
                    above, equal = [r.rearrange("p (t e j) -> p t e j", t=CH, e=NE) for r in rank]
                    of_j = score.unsqueeze(2).to_broadcast([P, CH, NE, NE])
                    of_e = score.unsqueeze(3).to_broadcast([P, CH, NE, NE])
                    nc.vector.tensor_tensor(above, of_j, of_e, ALU.is_gt)
                    link(nc.vector.tensor_tensor(equal, of_j, of_e, ALU.is_equal))
                    r1 = rank[1].rearrange("p (t e j) -> p t (e j)", t=CH, e=NE)
                    link(nc.vector.tensor_tensor(r1, r1, before.rearrange("p e j -> p (e j)").unsqueeze(1)
                                                 .to_broadcast([P, CH, NE * NE]), ALU.mult))
                    link(nc.vector.tensor_tensor(rank[0], rank[0], rank[1], ALU.add))
                if i == 11:
                    link(nc.vector.tensor_reduce(ranks, rank[0].rearrange("p (t e j) -> p t e j", t=CH, e=NE), AX_X,
                                                 ALU.add))
                    link(nc.vector.tensor_scalar(ranks, ranks, 1.5, None, ALU.is_lt))
                    link(nc.vector.tensor_tensor(rest, score, ranks, ALU.mult))
                    for c in range(PARTS):
                        ins = nc.vector.tensor_copy(parts[:, :, c, :], rest)
                        if c < PARTS - 1:
                            link(ins)
                            link(nc.vector.tensor_tensor(rest, rest, parts[:, :, c, :], ALU.subtract))
                    ins.then_inc(parts_ready, 1)
                    assert count[0] == OWN
                if i == 12:
                    wait(dve, parts_turned, f + 1)
                    wait(dve, w_ready, f * ET)
                    nc.vector.tensor_copy(wT_b, b_r[:, 0:CT // 2].bitcast(BF16)[0:PARTS * NE, :]).then_inc(wT_ready, 1)

            def slot(c, i):
                if isinstance(c, int) and c == CHUNKS:
                    return
                n = rows(i)
                last_slot = i == FT - 1 and not (isinstance(c, int) and c == CHUNKS - 1)
                wait(dve, u_ready, c * FT + (i + 1))
                wait(dve, silued, c * FT + (i + 1))
                if c_past(c, i, 2):
                    wait(dve, hid_ready, c * FT + (i - 1))
                h = hid[i % 2][0:n, :]
                if i < ET:
                    nc.vector.tensor_tensor(h, sil[0:n, :], b_u[0:n, :], ALU.mult).then_inc(gated, 1)
                    wait(dve, w_ready, c * ET + (i + 1))
                    wait(dve, gated, c * FT + (i + 1))
                    nc.vector.tensor_tensor(h, h, b_w[0:n, :], ALU.mult).then_inc(hid_made, 1)
                else:
                    nc.vector.tensor_tensor(h, sil[0:n, :], b_u[0:n, :], ALU.mult).then_inc(gated, 1)
                    if last_slot:
                        turn(c + 1)
                    wait(dve, gated, c * FT + (i + 1))
                    nc.vector.tensor_copy(stats[:, 100:101], stats[:, 0:1]).then_inc(hid_made, 1)
                wait(dve, hid_high, c * FT + (i + 1))
                if c_past(c, i, 1):
                    wait(dve, down_done, c * FT + i)
                nc.vector.tensor_tensor(hid_lo[0:n, :], h, hid_hi[i % 2][0:n, :].bitcast(F32), ALU.subtract).then_inc(hid_ready, 1)

            def back(i, c):
                if i == 0:
                    wait(dve, acc_ready, c + 1)
                    wait(dve, cur_copied, c + 1)
                    wait(dve, stored, c * 16)
                    nc.vector.tensor_tensor(h3, b_acc, x2c, ALU.add).then_inc(h3_ready, 1)
                if i == 4:
                    wait(dve, h3_ready, c + 1)
                    for t in range(CH):
                        last = nc.vector.bn_stats(bn3[t], h3[:, t * D:(t + 1) * D])
                    last.then_inc(h3_stats, 1)
                    wait(dve, h3_stats, c + 1)
                    carry(nc, stats)
                    for t in range(CH):
                        last = nc.vector.bn_aggr(mv3[:, t, :], bn3[t])
                    last.then_inc(h3_mv, 1)
                if i == 7:
                    wait(dve, h3_rstd, c + 1)
                    for t in range(CH):
                        last = nc.vector.tensor_scalar(h3[:, t * D:(t + 1) * D], h3[:, t * D:(t + 1) * D], mv3[:, t, 0:1],
                                                       rstd3[:, t:t + 1], ALU.subtract, ALU.mult)
                    last.then_inc(y3_ready, 1)

            def last_back():
                c = CHUNKS - 1
                dve.wait_ge(acc_ready, c + 1)
                dve.wait_ge(cur_copied, c + 1)
                dve.wait_ge(stored, c * 16)
                for half in range(2):
                    cols, mine = slice(half * CT, (half + 1) * CT), range(half * CH // 2, (half + 1) * CH // 2)
                    n = c + half + 1
                    nc.vector.tensor_tensor(h3[:, cols], b_acc[:, cols], x2c[:, cols], ALU.add).then_inc(h3_ready, 1)
                    dve.wait_ge(h3_ready, n)
                    for t in mine:
                        last = nc.vector.bn_stats(bn3[t], h3[:, t * D:(t + 1) * D])
                    last.then_inc(h3_stats, 1)
                    dve.wait_ge(h3_stats, n)
                    for t in mine:
                        last = nc.vector.bn_aggr(mv3[:, t, :], bn3[t])
                    last.then_inc(h3_mv, 1)
                for half in range(2):
                    dve.wait_ge(h3_rstd, c + half + 1)
                    for t in range(half * CH // 2, (half + 1) * CH // 2):
                        last = nc.vector.tensor_scalar(h3[:, t * D:(t + 1) * D], h3[:, t * D:(t + 1) * D], mv3[:, t, 0:1],
                                                       rstd3[:, t:t + 1], ALU.subtract, ALU.mult)
                    last.then_inc(y3_ready, 1)

            def turn(f):
                wait(dve, u_ready, f * FT)
                for k in range(KD):
                    wait(dve, high, f * KD + (k + 1))
                    nc.vector.tensor_tensor(x2_lo[:, k, :], turned[:, k * CT:(k + 1) * CT], x2_hi[:, k, :].bitcast(F32),
                                            ALU.subtract).then_inc(split, 1)

            chunks(dve, front, slot, turn, back, last_back)

        @block.gpsimd
        def _(pool):
            def rsqrt(var, eps, tmp, dst, ready, between, done, n):
                wait(pool, ready, n)
                k = tmp.shape[1]
                nc.gpsimd.tensor_tensor(tmp.unsqueeze(2), var[:, :, 1:2], eps.to_broadcast([P, k]).unsqueeze(2),
                                        ALU.add).then_inc(between, 1)
                wait(pool, between, n)
                nc.gpsimd.tensor_tensor(dst, tmp, neg_half[:, 0:k], ALU.pow).then_inc(done, 1)

            def front(i, f):
                if i == 0:
                    rsqrt(mv, gn_eps, ve, rstd, o_mv, o_var, o_rstd, f + 1)
                if i == 1 and not (isinstance(f, int) and f == 0):
                    wait(pool, o_normed, f + 1)
                    nc.gpsimd.tensor_tensor(tok(y), tok(y), gamma.unsqueeze(1).to_broadcast([P, CH, D]), ALU.mult).then_inc(scaled, 1)
                    wait(pool, scaled, f + 1)
                    nc.gpsimd.tensor_tensor(tok(y), tok(y), beta.unsqueeze(1).to_broadcast([P, CH, D]), ALU.add).then_inc(biased, 1)
                if i == 5:
                    rsqrt(mv, ln_eps, ve, rstd, h_mv, h_var, h_rstd, f + 1)

            def back(i, c):
                if i == 4:
                    rsqrt(mv3, ln_eps, ve3, rstd3, h3_mv, h3_var, h3_rstd, c + 1)

            def last_back():
                for half in range(2):
                    tiles = slice(half * CH // 2, (half + 1) * CH // 2)
                    rsqrt(mv3[:, tiles, :], ln_eps, ve3[:, tiles], rstd3[:, tiles], h3_mv, h3_var, h3_rstd, CHUNKS + half)

            chunks(pool, front=front, back=back, last=last_back)


def constants():
    inv_freq = (1.0 / np.float32(10000.0) ** (np.arange(HALF, dtype=np.float32) * np.float32(2.0 / ROT))).astype(np.float32)

    def rotation(pos):
        ang = (pos.astype(np.float32)[:, None] * inv_freq[None, :]).astype(np.float32)
        c, s = np.cos(ang).astype(np.float32), np.sin(ang).astype(np.float32)
        ones = np.ones((len(pos), HD - ROT), np.float32)
        return np.concatenate([c, c, ones], 1), np.concatenate([-s, s], 1)

    pos = np.arange(P) % S
    ends = (np.arange(P) % NC) * BLK + BLK - 1
    cos_t, sin_t = rotation(pos)
    cos_e, sin_e = rotation(ends)
    open_ = np.concatenate([np.arange(S)[None] <= pos[:, None], (np.arange(NC) * BLK + BLK - 1)[None] <= pos[:, None],
                            np.ones((P, 1), bool)], 1)
    gam = (1.0 - 2.0 ** (-5.0 - np.arange(RH, dtype=np.float32))).astype(np.float32)
    expo = np.arange(S, dtype=np.float32)[None, :] - np.arange(S, dtype=np.float32)[:, None]
    dm = np.where(expo[None] <= 0, gam[:, None, None] ** expo[None], 0.0).astype(np.float32)
    dm = dm / np.sqrt(dm.sum(axis=-1))[:, None, :] / np.sqrt(np.float32(HD))
    decay = dm.transpose(2, 0, 1).reshape(S, RH * S).astype(np.float32)
    expert = np.arange(ET * P) // EF
    select = np.tile((expert[None] == np.arange(NE)[:, None]).astype(np.float32), (PARTS, 1))
    before = (np.arange(NE)[None] < np.arange(NE)[:, None]).astype(np.float32).reshape(1, -1)
    mask = np.where(open_, 0.0, -1e30).astype(np.float32)
    return {"ident": np.eye(P, dtype=np.float32), "cos_token": cos_t, "sin_token": sin_t, "cos_entry": cos_e,
            "sin_entry": sin_e, "mask": np.tile(mask, (1, G)), "decay": decay, "select": select, "before": before}


def kernel(**inputs):
    import concourse.bacc as _bacc
    from concourse import mybir as _mybir
    from concourse.bass_utils import run_bass_kernel_spmd as _run

    i = {k: np.asarray(v) for k, v in inputs.items()}
    at = {k[len("L0_attn_"):]: v for k, v in i.items() if k.startswith("L0_attn_")}
    x = i["x"].reshape(TOK, D)
    arrays = {
        "x": x, "xT": x.T, "Wq": at["Wq"], "Wlk": at["Wlk"], "Wlv": at["Wlv"], "Wo": at["Wo"],
        "Wk": at["Wk"], "Wv": at["Wv"], "Wc": at["Wc"].reshape(1, D), "bc": at["bc"].reshape(1, 1),
        "bq": at["bq"].reshape(1, -1), "blk": at["blk"].reshape(1, -1), "bk": at["bk"].reshape(1, -1),
        "bvT": at["bv"].reshape(HD, 1), "blvT": at["blv"].reshape(NH, HD).T, "qn_w": at["qn_w"].reshape(1, -1),
        "kn_w": at["kn_w"].reshape(1, -1), "sink_kT": at["sink_k"].T, "sink_vT": at["sink_v"].T,
        "bo": at["bo"].reshape(1, D),
    }
    xa = {k[len("L0_xattn_"):]: v for k, v in i.items() if k.startswith("L0_xattn_")}
    ff = {k[len("L0_ffn_"):]: v for k, v in i.items() if k.startswith("L0_ffn_")}
    arrays |= {
        "ctxT": i["ctx_2048"].reshape(TOK, D).T, "Wh": xa["Wh"], "WhT": xa["Wh"].transpose(0, 2, 1), "wg_w": xa["wg_w"],
        "wo_w": xa["wo_w"], "gn_gamma": xa["gn_gamma"].reshape(1, D), "gn_beta": xa["gn_beta"].reshape(1, D),
        "WrT": ff["Wr"].T,
        "gateT": np.concatenate([ff["Wg"].reshape(NE * EF, D), ff["Wsg"]]).T,
        "upT": np.concatenate([ff["Wu"].reshape(NE * EF, D), ff["Wsu"]]).T,
        "down": np.concatenate([ff["Wd"].transpose(0, 2, 1).reshape(NE * EF, D), ff["Wsd"].T]),
    }
    arrays |= constants()
    arrays = {k: np.ascontiguousarray(v) for k, v in arrays.items()}
    nc = _bacc.Bacc("TRN2", target_bir_lowering=False, num_devices=1)
    a = {k: nc.dram_tensor(f"in_{k}", v.shape, _mybir.dt.from_np(v.dtype), kind="ExternalInput").ap()
         for k, v in arrays.items()}
    out = nc.dram_tensor("out", (TOK, D), F32, kind="ExternalOutput").ap()
    scratch = nc.dram_tensor("cw_scratch", (NE_ * NH, D), F32, kind="Internal").ap()
    program(nc, a, out, scratch)
    r = _run(nc, [{f"in_{k}": v for k, v in arrays.items()}], core_ids=[0])
    return r.results[0]["out"].reshape(B, S, D)
```
